# Optimizing a Trainium2 kernel written in Bass

```python
import numpy as np
import jax
import jax.numpy as jnp

def _softmax(x, axis=-1):
    return jax.nn.softmax(x, axis=axis)

def _gelu(x):
    return jax.nn.gelu(x, approximate=True)

def _silu(x):
    return jax.nn.silu(x)

def _sigmoid(x):
    return jax.nn.sigmoid(x)

def _layernorm(x, axis=-1, eps=1e-05):
    m = jnp.mean(x, axis=axis, keepdims=True)
    v = jnp.var(x, axis=axis, keepdims=True)
    return (x - m) / jnp.sqrt(v + eps)

def _scatter_add(tgt, idx, src, axis=0):
    return tgt.at[idx].add(src)

def _segment_sum(src, seg, n):
    return jax.ops.segment_sum(src, seg, n)
kernel_name = 'mk_gps_d1_gnn_r8_fb7c90'

def setup_inputs(seed: int=0):
    np.random.seed(seed)
    _w = jnp.asarray

    def _rec_inputs():
        import jax
        import jax.numpy as jnp
        _gk = jax.random.key(seed)
        x = -0.0003713 + 1 * jax.random.normal(jax.random.fold_in(_gk, 1), (12500, 256), jnp.float32)
        src = jax.random.randint(jax.random.fold_in(_gk, 2), (200000,), 0, 12500, jnp.int32)
        dst = jnp.minimum((12500 * jax.random.uniform(jax.random.fold_in(_gk, 3), (200000,)) ** 2.0).astype(jnp.int32), 99999)
        _o = jnp.argsort(dst, stable=True)
        src = src[_o]
        dst = dst[_o]
        edge_type_16 = jax.random.randint(jax.random.fold_in(_gk, 12), (200000,), 0, 16, jnp.int32)
        return (x, src, dst, edge_type_16)
    x, src, dst, edge_type_16 = _rec_inputs()

    def _L0_gnn_setup():
        import jax, jax.numpy as jnp
        import numpy as np
        N_NODES = 6250
        N_EDGES = 100000
        HDIM = 256
        NUMRELS = 16

        def _gru_cell(x, h, w_ih, w_hh, b_ih, b_hh):
            gi = x @ w_ih.T + b_ih
            gh = h @ w_hh.T + b_hh
            i_r, i_z, i_n = jnp.split(gi, 3, axis=-1)
            h_r, h_z, h_n = jnp.split(gh, 3, axis=-1)
            r = jax.nn.sigmoid(i_r + h_r)
            z = jax.nn.sigmoid(i_z + h_z)
            n = jnp.tanh(i_n + r * h_n)
            return (1.0 - z) * n + z * h
        key = jax.random.key(seed)
        ks = jax.random.split(key, 9)
        h = jax.random.normal(ks[0], (N_NODES, HDIM), dtype=jnp.float32)
        relvectors = jax.random.normal(ks[1], (NUMRELS, HDIM), dtype=jnp.float32)
        s = 1.0 / np.sqrt(HDIM)
        w_ih = jax.random.uniform(ks[2], (3 * HDIM, HDIM), minval=-s, maxval=s, dtype=jnp.float32)
        w_hh = jax.random.uniform(ks[3], (3 * HDIM, HDIM), minval=-s, maxval=s, dtype=jnp.float32)
        b_ih = jax.random.uniform(ks[4], (3 * HDIM,), minval=-s, maxval=s, dtype=jnp.float32)
        b_hh = jax.random.uniform(ks[5], (3 * HDIM,), minval=-s, maxval=s, dtype=jnp.float32)
        edge_src = jax.random.randint(ks[6], (N_EDGES,), 0, N_NODES, dtype=jnp.int32)
        edge_dst = jax.random.randint(ks[7], (N_EDGES,), 0, N_NODES, dtype=jnp.int32)
        edge_rel = jax.random.randint(ks[8], (N_EDGES,), 0, NUMRELS, dtype=jnp.int32)
        return {'h': h, 'relvectors': relvectors, 'w_ih': w_ih, 'w_hh': w_hh, 'b_ih': b_ih, 'b_hh': b_hh, 'edge_src': edge_src, 'edge_dst': edge_dst, 'edge_rel': edge_rel}
    _L0_gnn_all = _L0_gnn_setup()
    _L0_gnn_in = {k: v for k, v in _L0_gnn_all.items() if k in ('relvectors', 'w_ih', 'w_hh', 'b_ih', 'b_hh')}
    del _L0_gnn_all

    def _L0_mix_setup():
        import jax, jax.numpy as jnp
        import numpy as np
        D_MODEL = 256
        NHEAD = 8
        D_HEAD = D_MODEL // NHEAD
        DIM_FF = 1024
        B, L = (4, 2048)
        LN_EPS = 1e-05

        def _layernorm(x, g, b):
            mu = jnp.mean(x, axis=-1, keepdims=True)
            var = jnp.mean((x - mu) ** 2, axis=-1, keepdims=True)
            return (x - mu) * jax.lax.rsqrt(var + LN_EPS) * g + b

        def _phi(x):
            return jnp.where(x > 0, x + 1.0, jnp.exp(x))
        key = jax.random.key(seed)
        ks = jax.random.split(key, 16)
        s_in = 1.0 / np.sqrt(D_MODEL)
        s_ff = 1.0 / np.sqrt(DIM_FF)
        inp = {'x': jax.random.normal(ks[0], (B, L, D_MODEL), dtype=jnp.float32), 'Wq': jax.random.normal(ks[1], (D_MODEL, D_MODEL), dtype=jnp.float32) * s_in, 'bq': jnp.zeros((D_MODEL,), jnp.float32), 'Wk': jax.random.normal(ks[2], (D_MODEL, D_MODEL), dtype=jnp.float32) * s_in, 'bk': jnp.zeros((D_MODEL,), jnp.float32), 'Wv': jax.random.normal(ks[3], (D_MODEL, D_MODEL), dtype=jnp.float32) * s_in, 'bv': jnp.zeros((D_MODEL,), jnp.float32), 'Wo': jax.random.normal(ks[4], (D_MODEL, D_MODEL), dtype=jnp.float32) * s_in, 'bo': jnp.zeros((D_MODEL,), jnp.float32), 'W1': jax.random.normal(ks[5], (D_MODEL, DIM_FF), dtype=jnp.float32) * s_in, 'b1': jnp.zeros((DIM_FF,), jnp.float32), 'W2': jax.random.normal(ks[6], (DIM_FF, D_MODEL), dtype=jnp.float32) * s_ff, 'b2': jnp.zeros((D_MODEL,), jnp.float32), 'ln1_g': jnp.ones((D_MODEL,), jnp.float32), 'ln1_b': jnp.zeros((D_MODEL,), jnp.float32), 'ln2_g': jnp.ones((D_MODEL,), jnp.float32), 'ln2_b': jnp.zeros((D_MODEL,), jnp.float32)}
        return inp
    _L0_mix_all = _L0_mix_setup()
    _L0_mix_in = {k: v for k, v in _L0_mix_all.items() if k in ('Wq', 'bq', 'Wk', 'bk', 'Wv', 'bv', 'Wo', 'bo', 'W1', 'b1', 'W2', 'b2', 'ln1_g', 'ln1_b', 'ln2_g', 'ln2_b')}
    del _L0_mix_all

    def _L0_ffn_setup():
        import jax, jax.numpy as jnp
        import numpy as np
        BN_EPS = 0.001

        def _bn(h, g, b, m, v):
            return g * (h - m) * jax.lax.rsqrt(v + BN_EPS) + b
        key = jax.random.key(seed)
        ks = jax.random.split(key, 8)
        B, F, Df = (256, 64, 256)
        E, H, D = (8, 256, 256)
        s1 = 1.0 / np.sqrt(Df)
        s2 = 1.0 / np.sqrt(H)
        return {'x': jax.random.normal(ks[0], (B, F, Df), jnp.float32), 'Wr': jax.random.normal(ks[1], (Df, E), jnp.float32) * s1, 'br': jnp.zeros((E,), jnp.float32), 'W1': jax.random.normal(ks[2], (E, Df, H), jnp.float32) * s1, 'b1': jnp.zeros((E, H), jnp.float32), 'g1': jnp.ones((E, H), jnp.float32), 'be1': jnp.zeros((E, H), jnp.float32), 'm1': jnp.zeros((E, H), jnp.float32), 'v1': jnp.ones((E, H), jnp.float32), 'W2': jax.random.normal(ks[3], (E, H, H), jnp.float32) * s2, 'b2': jnp.zeros((E, H), jnp.float32), 'g2': jnp.ones((E, H), jnp.float32), 'be2': jnp.zeros((E, H), jnp.float32), 'm2': jnp.zeros((E, H), jnp.float32), 'v2': jnp.ones((E, H), jnp.float32), 'Wo': jax.random.normal(ks[4], (E, H, D), jnp.float32) * s2, 'bo': jnp.zeros((E, D), jnp.float32)}
    _L0_ffn_all = _L0_ffn_setup()
    _L0_ffn_in = {k: v for k, v in _L0_ffn_all.items() if k in ('Wr', 'br', 'W1', 'b1', 'g1', 'be1', 'm1', 'v1', 'W2', 'b2', 'g2', 'be2', 'm2', 'v2', 'Wo', 'bo')}
    del _L0_ffn_all
    return {'x': x, 'src': src, 'dst': dst, 'edge_type_16': edge_type_16, 'L0_gnn_relvectors': _L0_gnn_in['relvectors'], 'L0_gnn_w_ih': _L0_gnn_in['w_ih'], 'L0_gnn_w_hh': _L0_gnn_in['w_hh'], 'L0_gnn_b_ih': _L0_gnn_in['b_ih'], 'L0_gnn_b_hh': _L0_gnn_in['b_hh'], 'L0_mix_Wq': _L0_mix_in['Wq'], 'L0_mix_bq': _L0_mix_in['bq'], 'L0_mix_Wk': _L0_mix_in['Wk'], 'L0_mix_bk': _L0_mix_in['bk'], 'L0_mix_Wv': _L0_mix_in['Wv'], 'L0_mix_bv': _L0_mix_in['bv'], 'L0_mix_Wo': _L0_mix_in['Wo'], 'L0_mix_bo': _L0_mix_in['bo'], 'L0_mix_W1': _L0_mix_in['W1'], 'L0_mix_b1': _L0_mix_in['b1'], 'L0_mix_W2': _L0_mix_in['W2'], 'L0_mix_b2': _L0_mix_in['b2'], 'L0_mix_ln1_g': _L0_mix_in['ln1_g'], 'L0_mix_ln1_b': _L0_mix_in['ln1_b'], 'L0_mix_ln2_g': _L0_mix_in['ln2_g'], 'L0_mix_ln2_b': _L0_mix_in['ln2_b'], 'L0_ffn_Wr': _L0_ffn_in['Wr'], 'L0_ffn_br': _L0_ffn_in['br'], 'L0_ffn_W1': _L0_ffn_in['W1'], 'L0_ffn_b1': _L0_ffn_in['b1'], 'L0_ffn_g1': _L0_ffn_in['g1'], 'L0_ffn_be1': _L0_ffn_in['be1'], 'L0_ffn_m1': _L0_ffn_in['m1'], 'L0_ffn_v1': _L0_ffn_in['v1'], 'L0_ffn_W2': _L0_ffn_in['W2'], 'L0_ffn_b2': _L0_ffn_in['b2'], 'L0_ffn_g2': _L0_ffn_in['g2'], 'L0_ffn_be2': _L0_ffn_in['be2'], 'L0_ffn_m2': _L0_ffn_in['m2'], 'L0_ffn_v2': _L0_ffn_in['v2'], 'L0_ffn_Wo': _L0_ffn_in['Wo'], 'L0_ffn_bo': _L0_ffn_in['bo']}

def reference(x, src, dst, edge_type_16, L0_gnn_relvectors, L0_gnn_w_ih, L0_gnn_w_hh, L0_gnn_b_ih, L0_gnn_b_hh, L0_mix_Wq, L0_mix_bq, L0_mix_Wk, L0_mix_bk, L0_mix_Wv, L0_mix_bv, L0_mix_Wo, L0_mix_bo, L0_mix_W1, L0_mix_b1, L0_mix_W2, L0_mix_b2, L0_mix_ln1_g, L0_mix_ln1_b, L0_mix_ln2_g, L0_mix_ln2_b, L0_ffn_Wr, L0_ffn_br, L0_ffn_W1, L0_ffn_b1, L0_ffn_g1, L0_ffn_be1, L0_ffn_m1, L0_ffn_v1, L0_ffn_W2, L0_ffn_b2, L0_ffn_g2, L0_ffn_be2, L0_ffn_m2, L0_ffn_v2, L0_ffn_Wo, L0_ffn_bo):
    import jax
    import jax.numpy as jnp

    def _L0_gnn_ref(h, relvectors, w_ih, w_hh, b_ih, b_hh, edge_src, edge_dst, edge_rel):
        import jax, jax.numpy as jnp
        import numpy as np
        N_NODES = 6250
        N_EDGES = 100000
        HDIM = 256
        NUMRELS = 16

        def _gru_cell(x, h, w_ih, w_hh, b_ih, b_hh):
            gi = x @ w_ih.T + b_ih
            gh = h @ w_hh.T + b_hh
            i_r, i_z, i_n = jnp.split(gi, 3, axis=-1)
            h_r, h_z, h_n = jnp.split(gh, 3, axis=-1)
            r = jax.nn.sigmoid(i_r + h_r)
            z = jax.nn.sigmoid(i_z + h_z)
            n = jnp.tanh(i_n + r * h_n)
            return (1.0 - z) * n + z * h
        msg = h[edge_src] + relvectors[edge_rel]
        red = jax.ops.segment_sum(msg, edge_dst, num_segments=h.shape[0])
        return _gru_cell(red, h, w_ih, w_hh, b_ih, b_hh)

    def _L0_mix_ref(x, Wq, bq, Wk, bk, Wv, bv, Wo, bo, W1, b1, W2, b2, ln1_g, ln1_b, ln2_g, ln2_b):
        import jax, jax.numpy as jnp
        import numpy as np
        D_MODEL = 256
        NHEAD = 8
        D_HEAD = D_MODEL // NHEAD
        DIM_FF = 1024
        B, L = (4, 2048)
        LN_EPS = 1e-05

        def _layernorm(x, g, b):
            mu = jnp.mean(x, axis=-1, keepdims=True)
            var = jnp.mean((x - mu) ** 2, axis=-1, keepdims=True)
            return (x - mu) * jax.lax.rsqrt(var + LN_EPS) * g + b

        def _phi(x):
            return jnp.where(x > 0, x + 1.0, jnp.exp(x))
        Bq, Lq, _ = x.shape
        q = (x @ Wq + bq).reshape(Bq, Lq, NHEAD, D_HEAD)
        k = (x @ Wk + bk).reshape(Bq, Lq, NHEAD, D_HEAD)
        v = (x @ Wv + bv).reshape(Bq, Lq, NHEAD, D_HEAD)
        q_phi = _phi(q)
        k_phi = _phi(k)
        kv = jnp.einsum('blhd,blhe->bhde', k_phi, v)
        k_sum = k_phi.sum(axis=1)
        z = 1.0 / (jnp.einsum('blhd,bhd->blh', q_phi, k_sum) + 1e-06)
        out = jnp.einsum('blhd,bhde,blh->blhe', q_phi, kv, z)
        out = out.reshape(Bq, Lq, D_MODEL) @ Wo + bo
        x = _layernorm(x + out, ln1_g, ln1_b)
        ff = jax.nn.relu(x @ W1 + b1) @ W2 + b2
        x = _layernorm(x + ff, ln2_g, ln2_b)
        return x

    def _L0_ffn_ref(x, Wr, br, W1, b1, g1, be1, m1, v1, W2, b2, g2, be2, m2, v2, Wo, bo):
        import jax, jax.numpy as jnp
        import numpy as np
        BN_EPS = 0.001

        def _bn(h, g, b, m, v):
            return g * (h - m) * jax.lax.rsqrt(v + BN_EPS) + b
        feat = jnp.mean(x, axis=0)
        w = jax.nn.softmax(feat @ Wr + br, axis=-1)
        h = jnp.einsum('bfd,edh->bfeh', x, W1) + b1
        h = jax.nn.relu(_bn(h, g1, be1, m1, v1))
        h = jnp.einsum('bfeh,ehk->bfek', h, W2) + b2
        h = jax.nn.relu(_bn(h, g2, be2, m2, v2))
        y = jnp.einsum('bfeh,ehd->bfed', h, Wo) + bo
        return jnp.einsum('bfed,fe->bfd', y, w)
    xn = _layernorm(x, axis=-1)
    x = x + _L0_gnn_ref(xn, L0_gnn_relvectors, L0_gnn_w_ih, L0_gnn_w_hh, L0_gnn_b_ih, L0_gnn_b_hh, src, dst, edge_type_16) + _L0_mix_ref(xn[None], L0_mix_Wq, L0_mix_bq, L0_mix_Wk, L0_mix_bk, L0_mix_Wv, L0_mix_bv, L0_mix_Wo, L0_mix_bo, L0_mix_W1, L0_mix_b1, L0_mix_W2, L0_mix_b2, L0_mix_ln1_g, L0_mix_ln1_b, L0_mix_ln2_g, L0_mix_ln2_b)[0]
    x = x + _L0_ffn_ref(_layernorm(x, axis=-1)[None], L0_ffn_Wr, L0_ffn_br, L0_ffn_W1, L0_ffn_b1, L0_ffn_g1, L0_ffn_be1, L0_ffn_m1, L0_ffn_v1, L0_ffn_W2, L0_ffn_b2, L0_ffn_g2, L0_ffn_be2, L0_ffn_m2, L0_ffn_v2, L0_ffn_Wo, L0_ffn_bo)[0]
    return x

_drawn_inputs = setup_inputs


def setup_inputs(seed=0):
    import zlib

    import numpy as np

    out = dict(_drawn_inputs(seed))
    spreads = {'L0_mix_bq': (0.0, 0.8),
     'L0_mix_bk': (0.0, 0.8),
     'L0_mix_bv': (0.0, 0.1),
     'L0_mix_bo': (0.0, 0.1),
     'L0_mix_b1': (0.0, 0.336),
     'L0_mix_b2': (0.0, 0.1),
     'L0_mix_ln1_g': (1.0, 0.2),
     'L0_mix_ln1_b': (0.0, 0.1),
     'L0_mix_ln2_g': (1.0, 0.2),
     'L0_mix_ln2_b': (0.0, 0.1),
     'L0_ffn_br': (0.0, 0.551),
     'L0_ffn_b1': (0.0, 0.772),
     'L0_ffn_g1': (1.0, 0.6),
     'L0_ffn_be1': (0.0, 0.8),
     'L0_ffn_m1': (0.0, 0.78),
     'L0_ffn_v1': (1.0, 0.6),
     'L0_ffn_b2': (0.0, 0.553),
     'L0_ffn_g2': (1.0, 0.6),
     'L0_ffn_be2': (0.0, 0.582),
     'L0_ffn_m2': (0.0, 0.571),
     'L0_ffn_v2': (1.0, 0.6),
     'L0_ffn_bo': (0.0, 0.414)}
    factors = {'L0_gnn_b_ih': 8.0,
     'L0_gnn_b_hh': 8.0,
     'L0_mix_Wq': 8.0,
     'L0_mix_Wk': 8.0,
     'L0_mix_Wv': 8.0}
    for name, (base, spread) in spreads.items():
        noise = np.random.default_rng([zlib.crc32(name.encode()), seed]).standard_normal(out[name].shape)
        drawn = base * np.exp(spread * noise) if base else spread * noise
        out[name] = jnp.asarray(drawn.astype(out[name].dtype))
    for name, factor in factors.items():
        out[name] = (out[name] * factor).astype(out[name].dtype)
    return out
```

```python
from contextlib import ExitStack

import concourse.bass as bass
from concourse import mybir

ALU = mybir.AluOpType
ACT = mybir.ActivationFunctionType
AX = mybir.AxisListType
F32 = mybir.dt.float32
F32R = mybir.dt.float32r
F16 = mybir.dt.float16
I32 = mybir.dt.int32

P = 128
N, D = 12500, 256
KT = D // P
TPG = 4
G = TPG * P
GROUPS = -(-N // G)
PAIRS = GROUPS // 2
NP = GROUPS * G
TILES = NP // P
E = 200000
SC = 8
SA, SB = 2, 6
SUPER = GROUPS * (SA + SB)
EP = SUPER * SC * P
RELS = 16
FF = 1024
FT = FF // P
HD = 32
NE = 8
LN_EPS = 1e-5
BN_EPS = 1e-3
DEN_EPS = 1e-6
LO = 2048.0
VALID = N - (GROUPS - 1) * G
NEWTON = 3
RSQRT_OPS = 1 + 3 * NEWTON
NORM_OPS = 4 + RSQRT_OPS + 1

assert GROUPS % 2 == 1 and EP >= E and TILES <= P and 2 * SA % 4 == 0 and 2 * SB % 4 == 0


def wait(eng, sem, value):
    if not isinstance(value, int) or value > 0:
        eng.wait_ge(sem, value)


def each_group(eng, group):
    group(0, 0, 0, True)
    group(1, 1, 0, True)
    with eng.Fori(1, PAIRS) as i:
        group(i * 2, 0, i, True)
        group(i * 2 + 1, 1, i, True)
    group(GROUPS - 1, 0, PAIRS, False)


def rsqrt(dve, y, v, t, done, base):
    dve.wait_ge(done, base)
    dve.tensor_scalar(y.bitcast(I32), v.bitcast(I32), -0.5, 1597463007.0,
                      ALU.mult, ALU.add).then_inc(done, 1)
    k = base + 1
    for _ in range(NEWTON):
        dve.wait_ge(done, k)
        dve.scalar_tensor_tensor(t, y, -0.5, y, ALU.mult, ALU.mult).then_inc(done, 1)
        dve.wait_ge(done, k + 1)
        dve.tensor_tensor(t, t, v, ALU.mult).then_inc(done, 1)
        dve.wait_ge(done, k + 2)
        dve.scalar_tensor_tensor(y, t, 1.5, y, ALU.add, ALU.mult).then_inc(done, 1)
        k = k + 3


def norm_rows(dve, out, x, w, done, base):
    for j in range(TPG):
        ins = dve.bn_stats(w["st"][:, j, :], x[:, j, :])
    ins.then_inc(done, 1)
    dve.wait_ge(done, base + 1)
    dve.sem_inc(done, 1)
    for j in range(TPG):
        ins = dve.bn_aggr(w["mv"][:, j, :], w["st"][:, j, :])
    ins.then_inc(done, 1)
    dve.wait_ge(done, base + 3)
    dve.tensor_scalar(w["ve"][:, :], w["mv"][:, :, 1], LN_EPS, None, ALU.add).then_inc(done, 1)
    rsqrt(dve, w["rs"][:, :], w["ve"][:, :], w["tt"][:, :], done, base + 4)
    dve.wait_ge(done, base + 4 + RSQRT_OPS)
    for j in range(TPG):
        ins = dve.tensor_scalar(out[:, j, :], x[:, j, :], w["mv"][:, j, 0:1], w["rs"][:, j:j + 1],
                                ALU.subtract, ALU.mult)
    ins.then_inc(done, 1)


def norm_work(sb):
    return {"st": sb("stats", [P, TPG, 6], F32), "mv": sb("mean_var", [P, TPG, 2], F32),
            "ve": sb("var_eps", [P, TPG], F32), "rs": sb("rstd", [P, TPG], F32),
            "tt": sb("newton", [P, TPG], F32)}


def rows(ap, g):
    return ap.rearrange("(g j p) d -> g p j d", j=TPG, p=P)[g]


def rows_d(ap, g):
    return rows(ap, g)


def across(ap, n):
    return ap.unsqueeze(1).broadcast_to([ap.shape[0], n, ap.shape[1]])


class Names:

    def __init__(self, nc, ctx, phase):
        self.nc, self.ctx, self.phase = nc, ctx, phase

    def sb(self, name, shape, dt):
        return self.ctx.enter_context(self.nc.sbuf_tensor(f"{self.phase}_{name}", shape, dt))

    def ps(self, name, shape):
        return self.ctx.enter_context(self.nc.psum_tensor(f"{self.phase}_ps_{name}", shape, F32))

    def sem(self, name):
        return self.ctx.enter_context(self.nc.semaphore(f"{self.phase}_{name}"))


def norm_phase(nc, a, d, keep):
    with ExitStack() as ctx:
        m = Names(nc, ctx, "norm")
        x = [m.sb(f"x{u}", [P, TPG, D], F32) for u in range(2)]
        xn = [m.sb(f"xn{u}", [P, TPG, D], F32) for u in range(2)]
        pair = [m.sb(f"pair{u}", [P, TPG, 2, D], F16) for u in range(2)]
        rest = m.sb("rest", [P, TPG, D], F32)
        xT = [m.sb(f"xT{u}", [P, KT, G], F32) for u in range(2)]
        w = norm_work(m.sb)
        dst = m.sb("dst", [P, SUPER, SC], I32)
        ends = m.sb("ends", [P, 2, SUPER], F32)
        ends_all = m.sb("ends_all", [P, 2, SUPER], F32)
        low = m.sb("low", [P, SUPER], F32)
        psT = [m.ps(f"T{u}", [P, KT, G]) for u in range(2)]

        x_in = [m.sem(f"x_in{u}") for u in range(2)]
        const_in = m.sem("const_in")
        ends_done = m.sem("ends_done")
        reduced = m.sem("reduced")
        normed = m.sem("normed")
        high_done = m.sem("high_done")
        rest_done = m.sem("rest_done")
        low_done = m.sem("low_done")
        turned = m.sem("turned")
        xT_done = m.sem("xT_done")
        rows_out = [m.sem(f"rows_out{u}") for u in range(2)]
        pair_out = [m.sem(f"pair_out{u}") for u in range(2)]
        xT_out = [m.sem(f"xT_out{u}") for u in range(2)]

        with nc.Block() as block:
            @block.sync
            def _(sp):
                sp.dma_start(x[0][:, :, :], rows(a["x"], 0)).then_inc(x_in[0], 16)
                sp.dma_start(keep["ident"][:, :], a["identity"]).then_inc(const_in, 16)
                sp.dma_start(dst[:, :, :], a["dst_by_super"]).then_inc(const_in, 16)

                def group(g, u, i, more):
                    if more:
                        wait(sp, normed, g * NORM_OPS)
                        sp.dma_start(x[1 - u][:, :, :], rows(a["x"], g + 1)).then_inc(x_in[1 - u], 16)
                    sp.wait_ge(normed, (g + 1) * NORM_OPS)
                    sp.dma_start(rows(d["xn"], g), xn[u][:, :, :]).then_inc(rows_out[u], 16)
                    sp.wait_ge(xT_done, g + 1)
                    sp.dma_start(d["xnT"][g], xT[u][:, :, :]).then_inc(xT_out[u], 16)
                    sp.wait_ge(low_done, g + 1)
                    sp.dma_start(rows(d["pairs"], g), pair[u][:, :, :, :].rearrange("p j h d -> p j (h d)")
                                 ).then_inc(pair_out[u], 16)

                each_group(sp, group)
                for u in range(2):
                    for out in (rows_out[u], pair_out[u], xT_out[u]):
                        sp.wait_ge(out, 16 * (PAIRS + 1 - u))

            @block.vector
            def _(dve):
                dve.wait_ge(const_in, 32)
                dve.tensor_reduce(ends[:, 0, :], dst[:, :, :], AX.X, ALU.max)
                dve.tensor_reduce(ends[:, 1, :], dst[:, :, :], AX.X, ALU.min, negate=True
                                  ).then_inc(ends_done, 1)

                def group(g, u, i, more):
                    dve.wait_ge(x_in[u], 16 * (i + 1))
                    wait(dve, rows_out[u], 16 * i)
                    wait(dve, turned, g - 1)
                    wait(dve, high_done, g - 1)
                    norm_rows(dve, xn[u], x[u], w, normed, g * NORM_OPS)
                    dve.wait_ge(normed, (g + 1) * NORM_OPS)
                    dve.wait_ge(high_done, g + 1)
                    wait(dve, low_done, g)
                    dve.tensor_tensor(rest[:, :, :], xn[u][:, :, :], pair[u][:, :, 0, :],
                                      ALU.subtract).then_inc(rest_done, 1)

                each_group(dve, group)
                dve.wait_ge(reduced, 1)
                dve.tensor_copy(keep["count"][:, :], ends_all[:, 0, :])
                dve.tensor_scalar(keep["first"][:, :], ends_all[:, 1, :], -1.0, None, ALU.mult
                                  ).then_inc(ends_done, 1)
                dve.wait_ge(ends_done, 2)
                dve.tensor_scalar(keep["count"][:, :], keep["count"][:, :], 7, None,
                                  ALU.logical_shift_right)
                dve.tensor_scalar(keep["first"][:, :], keep["first"][:, :], 7, None,
                                  ALU.logical_shift_right).then_inc(ends_done, 1)
                dve.wait_ge(ends_done, 3)
                dve.scalar_tensor_tensor(keep["count"][:, :], keep["count"][:, :], 1.0,
                                         keep["first"][:, :], ALU.add, ALU.subtract
                                         ).then_inc(ends_done, 1)
                dve.wait_ge(ends_done, 4)

            @block.gpsimd
            def _(pool):
                pool.memset(keep["red"][:, :, :], 0.0)
                pool.memset(keep["rel_count"][:, :, :], 0.0)
                pool.wait_ge(ends_done, 1)
                pool.partition_all_reduce(ends_all[:, :, :].rearrange("p a s -> p (a s)"),
                                          ends[:, :, :].rearrange("p a s -> p (a s)"), P,
                                          bass.bass_isa.ReduceOp.max).then_inc(reduced, 1)

            @block.tensor
            def _(pe):
                pe.wait_ge(const_in, 32)

                def group(g, u, i, more):
                    pe.wait_ge(normed, (g + 1) * NORM_OPS)
                    wait(pe, xT_done, g - 1)
                    for k in range(KT):
                        for j in range(TPG):
                            ins = pe.transpose(psT[u][:, k, j * P:(j + 1) * P],
                                               xn[u][:, j, k * P:(k + 1) * P], keep["ident"][:, :])
                    ins.then_inc(turned, 1)

                each_group(pe, group)

            @block.scalar
            def _(act):
                def group(g, u, i, more):
                    act.wait_ge(normed, (g + 1) * NORM_OPS)
                    wait(act, pair_out[u], 16 * i)
                    act.activation(pair[u][:, :, 0, :], xn[u][:, :, :], ACT.Copy).then_inc(high_done, 1)
                    act.wait_ge(turned, g + 1)
                    wait(act, xT_out[u], 16 * i)
                    for k in range(KT):
                        ins = act.activation(xT[u][:, k, :], psT[u][:, k, :], ACT.Copy)
                    ins.then_inc(xT_done, 1)
                    act.wait_ge(rest_done, g + 1)
                    act.activation(pair[u][:, :, 1, :], rest[:, :, :], ACT.Copy, scale=LO
                                   ).then_inc(low_done, 1)

                each_group(act, group)


class Super:

    def __init__(self, per_pair, i, k):
        self.s = i * per_pair + k
        self.ring4, self.turn4 = k % 4, i * (per_pair // 4) + k // 4
        self.ring2, self.turn2 = k % 2, i * (per_pair // 2) + k // 2


def super_a(i, u, q):
    return Super(2 * SA, i, SA * u + q)


def super_b(i, u, q):
    return Super(2 * SB, i, GROUPS * SA + SB * u + q)


VEC_R1 = 2
VEC_N1 = VEC_R1 + NORM_OPS
VEC_U = VEC_N1 + 2
VEC_R2 = VEC_U + 1
VEC_N2 = VEC_R2 + NORM_OPS
VEC = VEC_N2 + 3


def mix_phase(nc, a, d, keep):
    with ExitStack() as ctx:
        m = Names(nc, ctx, "mix")
        wkv = m.sb("wkv", [P, KT, 2 * D], F32)
        wq = m.sb("wq", [P, KT, D], F32)
        wo = m.sb("wo", [P, KT, D], F32)
        w1 = m.sb("w1", [P, KT, FF], F32)
        w2 = m.sb("w2", [P, FT, D], F32)
        bkv = m.sb("bkv", [P, 2 * D], F32)
        row5 = m.sb("row5", [P, 5, D], F32)
        g1row = m.sb("g1row", [P, D], F32)
        col = m.sb("col", [P, 3 * KT + FT], F32)
        bq, g1, n1b, b1 = (col[:, 0:KT], col[:, KT:2 * KT], col[:, 2 * KT:3 * KT], col[:, 3 * KT:])
        row_bo, row_n1b, row_b2, row_g2, row_n2b = (row5[:, c, :] for c in range(5))
        kvb = m.sb("kvb", [P, KT, P], F32)
        ksb = m.sb("ksb", [P, KT, P], F32)
        ones = m.sb("ones", [P, HD], F32)
        zero = m.sb("zero", [P, P], F32)
        edge = [m.sb(f"edge{r}", [P, 3, SC], I32) for r in range(4)]
        msg = [m.sb(f"msg{r}", [P, SC, 2 * D], F16) for r in range(2)]
        typ = [m.sb(f"typ{r}", [P, SC, RELS], F16) for r in range(2)]
        hot = m.sb("hot", [P, SC, P], F16)
        xT = [m.sb(f"xT{u}", [P, KT, G], F32) for u in range(2)]
        xn = m.sb("xn", [P, TPG, D], F32)
        x = m.sb("x", [P, TPG, D], F32)
        ex, re = x[:, 0:2, :].rearrange("p a d -> p (a d)"), x[:, 2:4, :].rearrange("p a d -> p (a d)")
        qphi = m.sb("qphi", [P, KT, G], F32)
        x1T = qphi
        h = m.sb("h", [P, FT, G], F32)
        out = m.sb("out", [P, TPG, D], F32)
        w = norm_work(m.sb)
        kb = [h[:, r, 0:D] for r in (0, 1)]
        va = [h[:, 2 + r, 0:KT * (P + 2)].rearrange("p (b c) -> p b c", b=KT) for r in (0, 1)]
        kex = [h[:, 4 + r, 0:D] for r in (0, 1)]
        kre = [h[:, 4 + r, D:2 * D] for r in (0, 1)]
        kphi = [h[:, 6 + r, 0:D] for r in (0, 1)]

        pa = [m.ps(f"pa{r}", [P, G]) for r in range(2)]
        pb = m.ps("pb", [P, TPG, D])
        pc = m.ps("pc", [P, TPG, D])
        pbf = pb[:, :, :].rearrange("p (b j) d -> p b (j d)", b=2)
        pcf = pc[:, :, :].rearrange("p (b j) d -> p b (j d)", b=2)
        ring = [pa[0][:, :], pa[1][:, :], pbf[:, 0, :], pbf[:, 1, :]]
        seg = m.ps("seg", [P, 2 * D])
        cnt = m.ps("cnt", [P, RELS])
        acc = pcf[:, 0, 0:KT * (P + 2)].rearrange("p (b c) -> p b c", b=KT)

        w_in = m.sem("w_in")
        edge_in = [m.sem(f"edge_in{r}") for r in range(4)]
        gathered = [m.sem(f"gathered{r}") for r in range(2)]
        gather_go = m.sem("gather_go")
        hot_ready = m.sem("hot_ready")
        summed = m.sem("summed")
        low_added = m.sem("low_added")
        added = m.sem("added")
        super_done = m.sem("super_done")
        xT_in = [m.sem(f"xT_in{u}") for u in range(2)]
        xn_in, x_in = m.sem("xn_in"), m.sem("x_in")
        set_up = m.sem("set_up")
        kv_mm, kv_bias, kv_act, kphi_done, acc_mm = (
            m.sem(n) for n in ("kv_mm", "kv_bias", "kv_act", "kphi_done", "acc_mm"))
        heads_done = m.sem("heads_done")
        q_mm, q_act, qphi_done, nd_mm, den_done, rec_done, attn_done, wo_mm = (
            m.sem(n) for n in ("q_mm", "q_act", "qphi_done", "nd_mm", "den_done", "rec_done",
                               "attn_done", "wo_mm"))
        x1_mm, x1T_done, ff1_mm, h_done, ff2_mm, vec, stored = (
            m.sem(n) for n in ("x1_mm", "x1T_done", "ff1_mm", "h_done", "ff2_mm", "vec", "stored"))
        N_W = 16 * 11

        with nc.Block() as block:
            @block.sync
            def _(sp):
                def edges(s, r):
                    sp.dma_start(edge[r][:, :, :], a["edges"][s]).then_inc(edge_in[r], 16)

                def next_edges(c):
                    if isinstance(c.s, int) and c.s + 4 >= SUPER:
                        return
                    sp.wait_ge(super_done, c.s + 1)
                    edges(c.s + 4, c.ring4)

                for r in range(4):
                    edges(r, r)
                sp.dma_start(xT[0][:, :, :], d["xnT"][0]).then_inc(xT_in[0], 16)

                def group_a(g, u, i, more):
                    if more:
                        wait(sp, kv_mm, TPG * g)
                        sp.dma_start(xT[1 - u][:, :, :], d["xnT"][g + 1]).then_inc(xT_in[1 - u], 16)
                    for q in range(SA):
                        next_edges(super_a(i, u, q))

                each_group(sp, group_a)
                sp.dma_start(xn[:, :, :], rows(d["xn"], 0)).then_inc(xn_in, 16)
                sp.wait_ge(kv_mm, TPG * GROUPS)
                sp.dma_start(xT[1][:, :, :], d["xnT"][0]).then_inc(xT_in[1], 16)

                def group_b(g, u, i, more):
                    if more:
                        wait(sp, q_mm, KT * g)
                        sp.dma_start(xT[u][:, :, :], d["xnT"][g + 1]).then_inc(xT_in[u], 16)
                    for q in range(SB):
                        if q == 1:
                            sp.wait_ge(qphi_done, KT * (g + 1))
                            sp.dma_start(x[:, :, :], rows(a["x"], g)).then_inc(x_in, 16)
                        if q == SB // 2 and more:
                            sp.wait_ge(vec, VEC * g + VEC_N1 + 1)
                            sp.wait_ge(x1_mm, g + 1)
                            sp.dma_start(xn[:, :, :], rows(d["xn"], g + 1)).then_inc(xn_in, 16)
                        next_edges(super_b(i, u, q))
                    sp.wait_ge(vec, VEC * (g + 1))
                    sp.dma_start(rows(d["mid"], g), out[:, :, :]).then_inc(stored, 16)

                each_group(sp, group_b)
                sp.wait_ge(stored, 16 * GROUPS)

            @block.gpsimd
            def _(pool):
                def gather(c):
                    pool.wait_ge(edge_in[c.ring4], 16 * (c.turn4 + 1))
                    wait(pool, super_done, c.s - 1)
                    pool.sem_inc(gather_go, 1)
                    for k in range(SC):
                        pool.indirect_dma_start(
                            msg[c.ring2][:, k, :], None, d["pairs"],
                            bass.IndirectOffsetOnAxis(edge[c.ring4][:, 0, k:k + 1], 0)
                        ).then_inc(gathered[c.ring2], 16)

                for k in range(4):
                    gather(Super(4, 0, k))
                with pool.Fori(1, SUPER // 4) as i:
                    for k in range(4):
                        gather(Super(4, i, k))

            @block.tensor
            def _(pe):
                visit = pe.alloc_register("pe_visit")
                pe.reg_mov(visit, 0)

                def segment(c):
                    count = pe.value_load(keep["count"][0:1, bass.ds(c.s, 1)], min_val=1, max_val=TILES)
                    with pe.Fori(0, count):
                        v = pe.snap(visit)
                        pe.wait_ge(gathered[c.ring2], 16 * SC * (c.turn2 + 1))
                        pe.wait_ge(hot_ready, v + 1)
                        pe.wait_ge(added, v + 1)
                        for k in range(SC):
                            pe.matmul(seg[:, :], hot[:, k, :], msg[c.ring2][:, k, :],
                                      start=(k == 0), stop=(k == SC - 1))
                            ins = pe.matmul(cnt[:, :], hot[:, k, :], typ[c.ring2][:, k, :],
                                            start=(k == 0), stop=(k == SC - 1))
                        ins.then_inc(summed, 1)
                        pe.reg_add(visit, visit, 1)

                pe.wait_ge(w_in, N_W)
                pe.wait_ge(set_up, 1)
                pe.matmul(pcf[:, 0, 0:KT * (P + 2)], zero[:, :], wkv[:, 0, 0:KT * (P + 2)],
                          start=True, stop=False, skip_group_check=True)

                def group_a(g, u, i, more):
                    pe.wait_ge(xT_in[u], 16 * (i + 1))

                    def project(j):
                        wait(pe, kv_bias, TPG * g + j - 1)
                        for k in range(KT):
                            ins = pe.matmul(pa[j % 2][:, :], xT[u][:, k, j * P:(j + 1) * P],
                                            wkv[:, k, :], start=(k == 0), stop=(k == KT - 1))
                        ins.then_inc(kv_mm, 1)

                    def accumulate(j):
                        n = P if more else max(0, min(P, VALID - j * P))
                        if n == 0:
                            return
                        pe.wait_ge(kphi_done, TPG * g + j + 1)
                        last = not more and j == (VALID - 1) // P
                        for b in range(KT):
                            ins = pe.matmul(acc[:, b, 0:P + 1], kphi[j % 2][0:n, b * P:(b + 1) * P],
                                            va[j % 2][0:n, b, 0:P + 1], start=False, stop=last,
                                            skip_group_check=True)
                        ins.then_inc(acc_mm, 1)

                    project(0)
                    project(1)
                    segment(super_a(i, u, 0))
                    accumulate(0)
                    project(2)
                    accumulate(1)
                    project(3)
                    segment(super_a(i, u, 1))
                    accumulate(2)
                    accumulate(3)

                each_group(pe, group_a)
                pe.wait_ge(heads_done, 1)

                def group_b(g, u, i, more):
                    pe.wait_ge(xT_in[1 - u], 16 * ((PAIRS + 1 if u == 0 else PAIRS + 2) + i))
                    wait(pe, h_done, FT * g)
                    for b in range(KT):
                        for k in range(KT):
                            ins = pe.matmul(pa[b][:, :], wq[:, k, b * P:(b + 1) * P], xT[1 - u][:, k, :],
                                            start=(k == 0), stop=(k == KT - 1))
                        ins.then_inc(q_mm, 1)
                    segment(super_b(i, u, 0))
                    pe.wait_ge(qphi_done, KT * (g + 1))
                    wait(pe, vec, VEC * (g - 1) + VEC_R2)
                    for b, (num, den) in enumerate(((pa[0][:, :], pa[1][:, :]), (pcf[:, 0, :], pcf[:, 1, :]))):
                        pe.matmul(num, kvb[:, b, :], qphi[:, b, :], start=True, stop=True)
                        pe.matmul(den, ksb[:, b, :], qphi[:, b, :], start=True, stop=True
                                  ).then_inc(nd_mm, 1)
                    segment(super_b(i, u, 1))
                    pe.wait_ge(attn_done, KT * (g + 1))
                    for j in range(TPG):
                        for k in range(KT):
                            ins = pe.matmul(pb[:, j, :], qphi[:, k, j * P:(j + 1) * P], wo[:, k, :],
                                            start=(k == 0), stop=(k == KT - 1))
                    ins.then_inc(wo_mm, 1)
                    segment(super_b(i, u, 2))
                    pe.wait_ge(vec, VEC * g + VEC_N1)
                    for k in range(KT):
                        for j in range(TPG):
                            ins = pe.transpose(pa[k][:, j * P:(j + 1) * P], xn[:, j, k * P:(k + 1) * P],
                                               keep["ident"][:, :])
                    ins.then_inc(x1_mm, 1)
                    segment(super_b(i, u, 3))
                    pe.wait_ge(x1T_done, KT * (g + 1))
                    for f in range(FT):
                        if f >= 4:
                            pe.wait_ge(h_done, FT * g + f - 3)
                        for k in range(KT):
                            ins = pe.matmul(ring[f % 4], w1[:, k, f * P:(f + 1) * P], x1T[:, k, :],
                                            start=(k == 0), stop=(k == KT - 1))
                        ins.then_inc(ff1_mm, 1)
                    segment(super_b(i, u, 4))
                    pe.wait_ge(h_done, FT * (g + 1))
                    for j in range(TPG):
                        for k in range(FT):
                            ins = pe.matmul(pc[:, j, :], h[:, k, j * P:(j + 1) * P], w2[:, k, :],
                                            start=(k == 0), stop=(k == FT - 1))
                    ins.then_inc(ff2_mm, 1)
                    segment(super_b(i, u, 5))

                each_group(pe, group_b)

            @block.scalar
            def _(act):
                feats = "(k p) n -> p k n"
                for t, src in ((wkv[:, :, :], a["w_kv"].rearrange(feats, p=P)),
                               (wq[:, :, :], a["w_q"].rearrange(feats, p=P)),
                               (wo[:, :, :], a["w_o"].rearrange(feats, p=P)),
                               (w1[:, :, :], a["w_ff1"].rearrange(feats, p=P)),
                               (w2[:, :, :], a["w_ff2"].rearrange(feats, p=P)),
                               (bkv[:, :], a["b_kv"].partition_broadcast(P)),
                               (row5[:, :, :], a["rows5"].partition_broadcast(P)),
                               (g1row[:, :], a["ln1_g"].partition_broadcast(P)),
                               (col[:, :], a["mix_cols"]),
                               (keep["iota"][:, :], a["iota"].partition_broadcast(P)),
                               (keep["base"][:, :], a["tile_base"].partition_broadcast(P))):
                    act.dma_start(t, src).then_inc(w_in, 16)
                act.wait_ge(w_in, N_W)

                def group_a(g, u, i, more):
                    for j in range(TPG):
                        act.wait_ge(kv_bias, TPG * g + j + 1)
                        wait(act, kphi_done, TPG * g + j - 1)
                        act.activation(kex[j % 2], kb[j % 2], ACT.Exp)
                        act.activation(kre[j % 2], kb[j % 2], ACT.Relu).then_inc(kv_act, 1)

                each_group(act, group_a)

                def group_b(g, u, i, more):
                    for b in range(KT):
                        act.wait_ge(q_mm, KT * g + b + 1)
                        wait(act, qphi_done, KT * g + b)
                        wait(act, vec, VEC * g)
                        act.activation(ex, pa[b][:, :], ACT.Exp, bias=bq[:, b:b + 1])
                        act.activation(re, pa[b][:, :], ACT.Relu, bias=bq[:, b:b + 1]
                                       ).then_inc(q_act, 1)
                    act.wait_ge(x1_mm, g + 1)
                    act.wait_ge(wo_mm, g + 1)
                    for k in range(KT):
                        act.activation(x1T[:, k, :], pa[k][:, :], ACT.Identity, scale=g1[:, k:k + 1],
                                       bias=n1b[:, k:k + 1]).then_inc(x1T_done, 1)
                    wait(act, ff2_mm, g)
                    for f in range(FT):
                        act.wait_ge(ff1_mm, FT * g + f + 1)
                        act.activation(h[:, f, :], ring[f % 4], ACT.Relu, bias=b1[:, f:f + 1]
                                       ).then_inc(h_done, 1)

                each_group(act, group_b)

            @block.vector
            def _(dve):
                visit = dve.alloc_register("dve_visit")
                dve.reg_mov(visit, 0)
                tile = dve.alloc_register("dve_tile")
                dve.sem_inc(added, 1)
                dve.memset(zero[:, :], 0.0)
                dve.memset(ones[:, :], 1.0)
                dve.memset(kvb[:, :, :], 0.0)
                dve.memset(ksb[:, :, :], 0.0)
                for r in range(2):
                    ins = dve.memset(va[r][:, :, P:P + 2], 1.0)
                ins.then_inc(set_up, 1)
                dve.wait_ge(w_in, N_W)

                def segment(c):
                    first = dve.value_load(keep["first"][0:1, bass.ds(c.s, 1)], min_val=0,
                                           max_val=TILES - 1)
                    count = dve.value_load(keep["count"][0:1, bass.ds(c.s, 1)], min_val=1,
                                           max_val=TILES)
                    dve.wait_ge(edge_in[c.ring4], 16 * (c.turn4 + 1))
                    e = edge[c.ring4]
                    dve.tensor_tensor(typ[c.ring2][:, :, :],
                                      e[:, 2, :].unsqueeze(2).broadcast_to([P, SC, RELS]),
                                      across(keep["iota"][:, 0:RELS], SC), ALU.is_equal)
                    dve.reg_mov(tile, first)
                    with dve.Fori(0, count):
                        v = dve.snap(visit)
                        t = dve.snap(tile, min_val=0, max_val=TILES - 1)
                        dve.scalar_tensor_tensor(hot[:, :, :],
                                                 e[:, 1, :].unsqueeze(2).broadcast_to([P, SC, P]),
                                                 keep["base"][:, bass.ds(t, 1)],
                                                 across(keep["iota"][:, :], SC),
                                                 ALU.subtract, ALU.is_equal).then_inc(hot_ready, 1)
                        dve.wait_ge(summed, v + 1)
                        dve.wait_ge(added, v + 1)
                        red = keep["red"][:, bass.ds(t, 1), :].rearrange("p a d -> p (a d)")
                        rel = keep["rel_count"][:, bass.ds(t, 1), :].rearrange("p a d -> p (a d)")
                        dve.scalar_tensor_tensor(red, seg[:, D:2 * D], 1.0 / LO, red,
                                                 ALU.mult, ALU.add).then_inc(low_added, 1)
                        dve.wait_ge(low_added, v + 1)
                        dve.tensor_tensor(red, seg[:, 0:D], red, ALU.add)
                        dve.tensor_tensor(rel, cnt[:, :], rel, ALU.add).then_inc(added, 1)
                        dve.reg_add(visit, visit, 1)
                        dve.reg_add(tile, tile, 1)
                    dve.sem_inc(super_done, 1)

                def group_a(g, u, i, more):
                    def bias(j):
                        dve.wait_ge(kv_mm, TPG * g + j + 1)
                        wait(dve, kv_act, TPG * g + j - 1)
                        wait(dve, acc_mm, TPG * g + j - 1)
                        dve.tensor_tensor(kb[j % 2], pa[j % 2][:, 0:D], bkv[:, 0:D], ALU.add)
                        dve.tensor_tensor(va[j % 2][:, :, 0:P],
                                          pa[j % 2][:, D:2 * D].rearrange("p (b c) -> p b c", b=KT),
                                          bkv[:, D:2 * D].rearrange("p (b c) -> p b c", b=KT),
                                          ALU.add).then_inc(kv_bias, 1)

                    def phi(j):
                        dve.wait_ge(kv_act, TPG * g + j + 1)
                        dve.scalar_tensor_tensor(kphi[j % 2], kex[j % 2], 1.0, kre[j % 2],
                                                 ALU.min, ALU.add).then_inc(kphi_done, 1)

                    bias(0)
                    bias(1)
                    phi(0)
                    phi(1)
                    segment(super_a(i, u, 0))
                    bias(2)
                    bias(3)
                    phi(2)
                    phi(3)
                    segment(super_a(i, u, 1))

                each_group(dve, group_a)
                dve.wait_ge(acc_mm, TPG * (GROUPS - 1) + -(-VALID // P))
                for b in range(KT):
                    for r in range(0, P, HD):
                        dve.tensor_copy(kvb[r:r + HD, b, r:r + HD], acc[r:r + HD, b, r:r + HD])
                        ins = dve.tensor_scalar(ksb[r:r + HD, b, r:r + HD], ones[r:r + HD, :],
                                                acc[r:r + HD, b, P:P + 1], None, ALU.mult)
                ins.then_inc(heads_done, 1)

                def group_b(g, u, i, more):
                    base = VEC * g
                    wait(dve, ff1_mm, FT * g)
                    for b in range(KT):
                        dve.wait_ge(q_act, KT * g + b + 1)
                        dve.scalar_tensor_tensor(qphi[:, b, :], ex, 1.0, re,
                                                 ALU.min, ALU.add).then_inc(qphi_done, 1)
                    segment(super_b(i, u, 0))
                    for b, (num, den) in enumerate(((pa[0][:, :], pa[1][:, :]), (pcf[:, 0, :], pcf[:, 1, :]))):
                        k = KT * g + b
                        dve.wait_ge(nd_mm, KT * (g + 1))
                        wait(dve, attn_done, k)
                        z = out[:, 0:2, :].rearrange("p a d -> p (a d)")
                        if b == 0:
                            wait(dve, stored, 16 * g)
                        dve.tensor_scalar(z, den, DEN_EPS, None, ALU.add).then_inc(den_done, 1)
                        dve.wait_ge(den_done, k + 1)
                        dve.reciprocal(z, z).then_inc(rec_done, 1)
                        dve.wait_ge(rec_done, k + 1)
                        dve.tensor_tensor(qphi[:, b, :], num, z, ALU.mult).then_inc(attn_done, 1)
                    segment(super_b(i, u, 1))
                    dve.wait_ge(wo_mm, g + 1)
                    dve.wait_ge(xn_in, 16 * (g + 1))
                    dve.tensor_tensor(xn[:, :, :], pb[:, :, :], xn[:, :, :], ALU.add).then_inc(vec, 1)
                    dve.wait_ge(vec, base + 1)
                    dve.tensor_tensor(xn[:, :, :], xn[:, :, :], across(row_bo, TPG), ALU.add
                                      ).then_inc(vec, 1)
                    dve.wait_ge(vec, base + VEC_R1)
                    segment(super_b(i, u, 2))
                    norm_rows(dve, xn, xn, w, vec, base + VEC_R1)
                    dve.wait_ge(vec, base + VEC_N1)
                    dve.wait_ge(attn_done, KT * (g + 1))
                    dve.tensor_tensor(out[:, :, :], xn[:, :, :], across(g1row[:, :], TPG), ALU.mult
                                      ).then_inc(vec, 1)
                    dve.wait_ge(vec, base + VEC_N1 + 1)
                    segment(super_b(i, u, 3))
                    dve.tensor_tensor(out[:, :, :], out[:, :, :], across(row_n1b, TPG),
                                      ALU.add).then_inc(vec, 1)
                    segment(super_b(i, u, 4))
                    dve.wait_ge(ff2_mm, g + 1)
                    dve.wait_ge(vec, base + VEC_U)
                    dve.tensor_tensor(out[:, :, :], pc[:, :, :], out[:, :, :], ALU.add
                                      ).then_inc(vec, 1)
                    dve.wait_ge(vec, base + VEC_R2)
                    norm_rows(dve, out, out, w, vec, base + VEC_R2)
                    dve.wait_ge(vec, base + VEC_N2)
                    dve.tensor_tensor(out[:, :, :], out[:, :, :], across(row_g2, TPG), ALU.mult
                                      ).then_inc(vec, 1)
                    dve.wait_ge(vec, base + VEC_N2 + 1)
                    dve.tensor_tensor(out[:, :, :], out[:, :, :], across(row_n2b, TPG), ALU.add
                                      ).then_inc(vec, 1)
                    dve.wait_ge(vec, base + VEC_N2 + 2)
                    dve.wait_ge(x_in, 16 * (g + 1))
                    dve.tensor_tensor(out[:, :, :], out[:, :, :], x[:, :, :], ALU.add
                                      ).then_inc(vec, 1)
                    segment(super_b(i, u, 5))

                n1b_b2 = m.sem("n1b_b2")
                dve.tensor_tensor(row_n1b, row_n1b, row_b2, ALU.add).then_inc(n1b_b2, 1)
                dve.wait_ge(n1b_b2, 1)
                each_group(dve, group_b)


def gru_phase(nc, a, d, keep):
    with ExitStack() as ctx:
        m = Names(nc, ctx, "gru")
        raw = m.sb("raw", [P, KT, 3 * D], F32)
        w_hi = [m.sb(f"w_hi{s}", [P, KT, 3 * D], F32R) for s in range(2)]
        w_lo = [m.sb(f"w_lo{s}", [P, KT, 3 * D], F32R) for s in range(2)]
        rel = m.sb("rel", [RELS, D], F32)
        col = m.sb("col", [P, 4 * KT], F32)
        gate_b = m.sb("gate_b", [P, 2 * KT], F32)
        xT = [m.sb(f"xT{u}", [P, KT, G], F32) for u in range(2)]
        x_hi, x_lo = m.sb("x_hi", [P, KT, G], F32R), m.sb("x_lo", [P, KT, G], F32R)
        r_hi, r_lo = m.sb("r_hi", [P, KT, G], F32R), m.sb("r_lo", [P, KT, G], F32R)
        red = m.sb("red", [P, TPG, D], F32)
        relc = m.sb("relc", [P, TPG, RELS], F32)
        relT = m.sb("relT", [RELS, G], F32)
        gr, gz, gn = m.sb("gr", [P, G], F32), m.sb("gz", [P, G], F32), m.sb("gn", [P, G], F32)
        gT = m.sb("gT", [P, KT, G], F32)
        mid = [m.sb(f"mid{u}", [P, TPG, D], F32) for u in range(2)]

        p_red = m.ps("red", [P, KT, G])
        p_gate = [m.ps(f"gate{q}", [P, G]) for q in range(4)]
        p_out = m.ps("out", [P, TPG, D])
        p_relT = p_out[0:RELS, 0:2, :].rearrange("p a d -> p (a d)")

        w_in = [m.sem(f"w_in{s}") for s in range(2)]
        c_in = m.sem("c_in")
        w_split = m.sem("w_split")
        w_high = m.sem("w_high")
        bias_sum = m.sem("bias_sum")
        xT_in = [m.sem(f"xT_in{u}") for u in range(2)]
        mid_in = [m.sem(f"mid_in{u}") for u in range(2)]
        stored = [m.sem(f"stored{u}") for u in range(2)]
        (copied, relT_mm, relT_done, red_mm, high, x_low, r_high, r_low, gates, reset, hn, pre, tan,
         diff, prod, g_done, out_mm, sum_done) = (m.sem(n) for n in (
             "copied", "relT_mm", "relT_done", "red_mm", "high", "x_low", "r_high", "r_low", "gates",
             "reset", "hn", "pre", "tan", "diff", "prod", "g_done", "out_mm", "sum_done"))
        feats = "(k p) n -> p k n"

        with nc.Block() as block:
            @block.sync
            def _(sp):
                sp.dma_start(raw[:, :, :], a["w_ihT"].rearrange(feats, p=P)).then_inc(w_in[0], 16)
                sp.dma_start(rel[:, :], a["rel"]).then_inc(c_in, 16)
                sp.dma_start(col[:, :], a["gru_cols"]).then_inc(c_in, 16)
                sp.dma_start(gate_b[:, :], a["gru_gate_cols"]).then_inc(c_in, 16)
                sp.dma_start(xT[0][:, :, :], d["xnT"][0]).then_inc(xT_in[0], 16)
                sp.dma_start(mid[0][:, :, :], rows(d["mid"], 0)).then_inc(mid_in[0], 16)
                sp.wait_ge(w_split, 1)
                sp.dma_start(raw[:, :, :], a["w_hhT"].rearrange(feats, p=P)).then_inc(w_in[1], 16)

                def group(g, u, i, more):
                    if more:
                        wait(sp, g_done, KT * g)
                        sp.dma_start(xT[1 - u][:, :, :], d["xnT"][g + 1]).then_inc(xT_in[1 - u], 16)
                        wait(sp, stored[1 - u], 16 * i if u == 0 else 16 * (i + 1))
                        sp.dma_start(mid[1 - u][:, :, :], rows(d["mid"], g + 1)
                                     ).then_inc(mid_in[1 - u], 16)
                    sp.wait_ge(sum_done, g + 1)
                    sp.dma_start(rows(d["all"], g), mid[u][:, :, :]).then_inc(stored[u], 16)

                each_group(sp, group)
                for u in range(2):
                    sp.wait_ge(stored[u], 16 * (PAIRS + 1 - u))

            @block.tensor
            def _(pe):
                pe.wait_ge(c_in, 48)
                pe.wait_ge(w_split, 2)

                def messages(g):
                    pe.wait_ge(copied, g + 1)
                    wait(pe, sum_done, g - 1)
                    for j in range(TPG):
                        ins = pe.transpose(p_relT[:, j * P:(j + 1) * P], relc[:, j, :],
                                           keep["ident"][:, :])
                    ins.then_inc(relT_mm, 1)
                    pe.wait_ge(relT_done, g + 1)
                    wait(pe, r_low, KT * g)
                    for b in range(KT):
                        pe.matmul(p_red[:, b, :], rel[:, b * P:(b + 1) * P], relT[:, :],
                                  start=True, stop=False)
                        for j in range(TPG):
                            ins = pe.matmul(p_red[:, b, j * P:(j + 1) * P],
                                            red[:, j, b * P:(b + 1) * P], keep["ident"][:, :],
                                            start=False, stop=(j == TPG - 1))
                    ins.then_inc(red_mm, 1)

                def group(g, u, i, more):
                    if isinstance(g, int) and g == 0:
                        messages(0)
                    pe.wait_ge(x_low, KT * (g + 1))
                    pe.wait_ge(r_low, KT * (g + 1))
                    for b in range(KT):
                        def products(gate, sides, col0):
                            n = 0
                            last = len(sides) * KT * 3
                            for s in sides:
                                hi, lo = ((r_hi, r_lo), (x_hi, x_lo))[s]
                                for k in range(KT):
                                    for wt, act_ in ((w_hi[s], hi), (w_hi[s], lo), (w_lo[s], hi)):
                                        ins = pe.matmul(p_gate[gate][:, :],
                                                        wt[:, k, col0 + b * P:col0 + (b + 1) * P],
                                                        act_[:, k, :], start=(n == 0), stop=(n == last - 1))
                                        n += 1
                            ins.then_inc(gates, 1)
                        item = KT * g + b
                        wait(pe, reset, 2 * item)
                        wait(pe, pre, item)
                        products(0, (1, 0), 0)
                        products(3, (1,), 2 * D)
                        products(2, (0,), 2 * D)
                        products(1, (1, 0), D)
                    if more:
                        messages(g + 1)
                    pe.wait_ge(g_done, KT * (g + 1))
                    for j in range(TPG):
                        for b in range(KT):
                            ins = pe.transpose(p_out[:, j, b * P:(b + 1) * P],
                                               gT[:, b, j * P:(j + 1) * P], keep["ident"][:, :])
                    ins.then_inc(out_mm, 1)

                each_group(pe, group)

            @block.scalar
            def _(act):
                for s in range(2):
                    act.wait_ge(w_in[s], 16)
                    act.activation(w_hi[s][:, :, :], raw[:, :, :], ACT.Copy).then_inc(w_high, 1)

                act.wait_ge(bias_sum, 1)

                def take(g, u, i):
                    wait(act, red_mm, g)
                    act.activation(red[:, :, :], keep["red"][:, bass.ds(g * TPG, TPG), :], ACT.Copy)
                    act.activation(relc[:, :, :], keep["rel_count"][:, bass.ds(g * TPG, TPG), :],
                                   ACT.Copy).then_inc(copied, 1)
                    act.wait_ge(relT_mm, g + 1)
                    act.activation(relT[:, :], p_relT, ACT.Copy).then_inc(relT_done, 1)

                def halves(g, u, i):
                    act.wait_ge(xT_in[u], 16 * (i + 1))
                    wait(act, gates, 4 * KT * g)
                    act.activation(x_hi[:, :, :], xT[u][:, :, :], ACT.Copy).then_inc(high, 1)
                    act.wait_ge(red_mm, g + 1)
                    for b in range(KT):
                        act.activation(r_hi[:, b, :], p_red[:, b, :], ACT.Copy).then_inc(r_high, 1)

                def group(g, u, i, more):
                    if isinstance(g, int) and g == 0:
                        take(0, 0, 0)
                    halves(g, u, i)
                    for b in range(KT):
                        item = KT * g + b
                        act.wait_ge(gates, 4 * item + 1)
                        wait(act, hn, item)
                        act.activation(gr[:, :], p_gate[0][:, :], ACT.Sigmoid, bias=gate_b[:, b:b + 1]
                                       ).then_inc(reset, 1)
                        act.wait_ge(gates, 4 * item + 4)
                        wait(act, g_done, item)
                        act.activation(gz[:, :], p_gate[1][:, :], ACT.Sigmoid,
                                       bias=gate_b[:, KT + b:KT + b + 1]).then_inc(reset, 1)
                        act.wait_ge(pre, item + 1)
                        act.activation(gn[:, :], gn[:, :], ACT.Tanh, bias=col[:, 2 * KT + b:2 * KT + b + 1]
                                       ).then_inc(tan, 1)
                    if more:
                        take(g + 1, 1 - u, i)

                each_group(act, group)

            @block.vector
            def _(dve):
                dve.wait_ge(c_in, 48)
                dve.tensor_tensor(gate_b[:, :], gate_b[:, :], col[:, 0:2 * KT], ALU.add
                                  ).then_inc(bias_sum, 1)
                for s in range(2):
                    dve.wait_ge(w_high, s + 1)
                    dve.tensor_tensor(w_lo[s][:, :, :], raw[:, :, :], w_hi[s][:, :, :].bitcast(F32),
                                      ALU.subtract).then_inc(w_split, 1)

                def group(g, u, i, more):
                    dve.wait_ge(high, g + 1)
                    wait(dve, gates, 4 * KT * g)
                    for b in range(KT):
                        dve.tensor_tensor(x_lo[:, b, :], xT[u][:, b, :], x_hi[:, b, :].bitcast(F32),
                                          ALU.subtract).then_inc(x_low, 1)
                    for b in range(KT):
                        dve.wait_ge(r_high, KT * g + b + 1)
                        dve.tensor_tensor(r_lo[:, b, :], p_red[:, b, :], r_hi[:, b, :].bitcast(F32),
                                          ALU.subtract).then_inc(r_low, 1)
                    for b in range(KT):
                        item = KT * g + b
                        dve.wait_ge(gates, 4 * item + 3)
                        dve.wait_ge(reset, 2 * item + 1)
                        wait(dve, g_done, item)
                        dve.scalar_tensor_tensor(gn[:, :], p_gate[3][:, :], col[:, 3 * KT + b:3 * KT + b + 1],
                                                 gr[:, :], ALU.add, ALU.mult).then_inc(hn, 1)
                        dve.wait_ge(hn, item + 1)
                        dve.tensor_tensor(gn[:, :], p_gate[2][:, :], gn[:, :], ALU.add).then_inc(pre, 1)
                        dve.wait_ge(tan, item + 1)
                        wait(dve, out_mm, g)
                        dve.tensor_tensor(gT[:, b, :], xT[u][:, b, :], gn[:, :], ALU.subtract
                                          ).then_inc(diff, 1)
                        dve.wait_ge(diff, item + 1)
                        dve.wait_ge(reset, 2 * item + 2)
                        dve.tensor_tensor(gT[:, b, :], gT[:, b, :], gz[:, :], ALU.mult).then_inc(prod, 1)
                        dve.wait_ge(prod, item + 1)
                        dve.tensor_tensor(gT[:, b, :], gT[:, b, :], gn[:, :], ALU.add).then_inc(g_done, 1)
                    dve.wait_ge(out_mm, g + 1)
                    dve.wait_ge(mid_in[u], 16 * (i + 1))
                    dve.tensor_tensor(mid[u][:, :, :], p_out[:, :, :], mid[u][:, :, :], ALU.add
                                      ).then_inc(sum_done, 1)

                each_group(dve, group)


def experts_phase(nc, a, d, keep):
    with ExitStack() as ctx:
        m = Names(nc, ctx, "moe")
        LAYERS = 3
        hi = [[m.sb(f"w_hi{l}_{e}", [P, KT, D], F32R) for e in range(NE)] for l in range(LAYERS)]
        lo = [[m.sb(f"w_lo{l}_{e}", [P, KT, D], F32R) for e in range(NE)] for l in range(LAYERS)]
        raw = [m.sb(f"raw{r}", [P, KT, D], F32) for r in range(4)]
        wr = m.sb("wr", [P, KT, NE], F32)
        wr_hi, wr_lo = m.sb("wr_hi", [P, KT, NE], F32R), m.sb("wr_lo", [P, KT, NE], F32R)
        br = m.sb("br", [P, NE], F32)
        bo = m.sb("bo", [NE, D], F32)
        bn = m.sb("bn", [P, 5, 2, NE * KT], F32)
        scale, shift = m.sb("scale", [P, 2, NE * KT], F32), m.sb("shift", [P, 2, NE * KT], F32)
        bt = m.sb("bt", [P, 2, NE * KT], F32)
        x3 = [m.sb(f"x3_{u}", [P, TPG, D], F32) for u in range(2)]
        f = m.sb("f", [P, TPG, D], F32)
        f_hi = [m.sb(f"f_hi{u}", [P, KT, G], F32R) for u in range(2)]
        f_lo = [m.sb(f"f_lo{u}", [P, KT, G], F32R) for u in range(2)]
        act_f = [m.sb(f"act{l}", [P, KT, G], F32) for l in range(2)]
        act_hi = [[m.sb(f"act_hi{l}_{r}", [P, KT, G], F32R) for r in range(2)] for l in range(2)]
        act_lo = [[m.sb(f"act_lo{l}_{r}", [P, KT, G], F32R) for r in range(2)] for l in range(2)]
        logit = m.sb("logit", [P, TPG, NE], F32)
        top, tot = m.sb("top", [P, TPG], F32), m.sb("tot", [P, TPG], F32)
        gate = [m.sb(f"gate{u}", [P, TPG, NE], F32) for u in range(2)]
        gateT = m.sb("gateT", [NE, G], F32)
        w = norm_work(m.sb)

        p_h = [[m.ps(f"h{l}_{k}", [P, G]) for k in range(KT)] for l in range(2)]
        p_y = m.ps("y", [P, TPG, D])
        p_f = m.ps("f", [P, KT, G])
        p_logit = p_f[:, 0, 0:TPG * NE].rearrange("p (j e) -> p j e", j=TPG)
        p_gateT = p_f[0:NE, 1, :]

        raw_in = [m.sem(f"raw_in{r}") for r in range(4)]
        c_in = m.sem("c_in")
        w_high, w_low, prep = m.sem("w_high"), m.sem("w_low"), m.sem("prep")
        x_in = [m.sem(f"x_in{u}") for u in range(2)]
        stored = [m.sem(f"stored{u}") for u in range(2)]
        (normed, f_mm, f_high, f_low, logit_mm, softmax, expd, gateT_mm, gateT_done, bias_mm,
         acc_done, y_mm) = (m.sem(n) for n in (
             "normed", "f_mm", "f_high", "f_low", "logit_mm", "softmax", "expd", "gateT_mm",
             "gateT_done", "bias_mm", "acc_done", "y_mm"))
        h_mm = [m.sem(f"h_mm{l}") for l in range(2)]
        h_act = [m.sem(f"h_act{l}") for l in range(2)]
        h_low = [m.sem(f"h_low{l}") for l in range(2)]
        softmax_in, normed_w = m.sem("softmax_in"), m.sem("normed_w")
        SOFTMAX = 5
        ACC = 1 + NE
        n_w = LAYERS * NE

        with nc.Block() as block:
            @block.sync
            def _(sp):
                for t, src in ((wr[:, :, :], a["w_router"].rearrange("(k p) n -> p k n", p=P)),
                               (br[:, :], a["b_router"].partition_broadcast(P)),
                               (bo[:, :], a["b_out"]),
                               (bn[:, :, :, :], a["bn_cols"])):
                    sp.dma_start(t, src).then_inc(c_in, 16)
                for n in range(n_w):
                    wait(sp, w_low, n - 3)
                    sp.dma_start(raw[n % 4][:, :, :], a["w_experts"][n % LAYERS, n // LAYERS]
                                 ).then_inc(raw_in[n % 4], 16)
                    if n == 3:
                        sp.dma_start(x3[0][:, :, :], rows(d["all"], 0)).then_inc(x_in[0], 16)

                def group(g, u, i, more):
                    if more:
                        wait(sp, stored[1 - u], 16 * i if u == 0 else 16 * (i + 1))
                        sp.dma_start(x3[1 - u][:, :, :], rows(d["all"], g + 1)
                                     ).then_inc(x_in[1 - u], 16)
                    sp.wait_ge(acc_done, ACC * (g + 1))
                    sp.dma_start(rows(a["out"], g), x3[u][:, :, :]).then_inc(stored[u], 16)

                each_group(sp, group)
                for u in range(2):
                    sp.wait_ge(stored[u], 16 * (PAIRS + 1 - u))

            @block.tensor
            def _(pe):
                def passes(out, wt, act, first, last):
                    for n, (p, q) in enumerate(((wt[0], act[0]), (wt[0], act[1]), (wt[1], act[0]))):
                        ins = pe.matmul(out, p, q, start=(first and n == 0), stop=(last and n == 2))
                    return ins

                def turn(g, u):
                    pe.wait_ge(normed, NORM_OPS * (g + 1))
                    wait(pe, gateT_done, g)
                    for k in range(KT):
                        for j in range(TPG):
                            ins = pe.transpose(p_f[:, k, j * P:(j + 1) * P], f[:, j, k * P:(k + 1) * P],
                                               keep["ident"][:, :])
                    ins.then_inc(f_mm, 1)

                def route(g, u):
                    pe.wait_ge(f_low, KT * (g + 1))
                    for j in range(TPG):
                        for k in range(KT):
                            t = slice(j * P, (j + 1) * P)
                            ins = passes(p_logit[:, j, :], (f_hi[u][:, k, t], f_lo[u][:, k, t]),
                                         (wr_hi[:, k, :], wr_lo[:, k, :]), k == 0, k == KT - 1)
                    ins.then_inc(logit_mm, 1)

                def turn_gates(g, u):
                    pe.wait_ge(softmax, SOFTMAX * (g + 1))
                    for j in range(TPG):
                        ins = pe.transpose(p_gateT[:, j * P:(j + 1) * P], gate[u][:, j, :],
                                           keep["ident"][:, :])
                    ins.then_inc(gateT_mm, 1)

                def biases(g):
                    pe.wait_ge(gateT_done, g + 1)
                    wait(pe, acc_done, ACC * g)
                    for j in range(TPG):
                        ins = pe.matmul(p_y[:, j, :], gateT[:, j * P:(j + 1) * P], bo[:, :],
                                        start=True, stop=True)
                    ins.then_inc(bias_mm, 1)

                def layer1(g, u, e):
                    n = NE * g + e
                    wait(pe, h_act[0], KT * n)
                    for b in range(KT):
                        c = slice(b * P, (b + 1) * P)
                        for k in range(KT):
                            ins = passes(p_h[0][b][:, :], (hi[0][e][:, k, c], lo[0][e][:, k, c]),
                                         (f_hi[u][:, k, :], f_lo[u][:, k, :]), k == 0, k == KT - 1)
                        ins.then_inc(h_mm[0], 1)

                def layer2(g, e):
                    n = NE * g + e
                    pe.wait_ge(h_low[0], KT * (n + 1))
                    wait(pe, h_act[1], KT * n)
                    for b in range(KT):
                        c = slice(b * P, (b + 1) * P)
                        for k in range(KT):
                            ins = passes(p_h[1][b][:, :], (hi[1][e][:, k, c], lo[1][e][:, k, c]),
                                         (act_hi[0][e % 2][:, k, :], act_lo[0][e % 2][:, k, :]),
                                         k == 0, k == KT - 1)
                        ins.then_inc(h_mm[1], 1)

                def layer3(g, e):
                    n = NE * g + e
                    pe.wait_ge(h_low[1], KT * (n + 1))
                    pe.wait_ge(acc_done, ACC * g + 1 + e)
                    for j in range(TPG):
                        t = slice(j * P, (j + 1) * P)
                        for k in range(KT):
                            ins = passes(p_y[:, j, :], (act_hi[1][e % 2][:, k, t], act_lo[1][e % 2][:, k, t]),
                                         (hi[2][e][:, k, :], lo[2][e][:, k, :]), k == 0, k == KT - 1)
                    ins.then_inc(y_mm, 1)

                pe.wait_ge(w_low, n_w)
                pe.wait_ge(prep, 2)
                turn(0, 0)
                pe.wait_ge(f_low, KT)
                layer1(0, 0, 0)
                route(0, 0)
                layer1(0, 0, 1)
                turn_gates(0, 0)
                layer2(0, 0)

                def group(g, u, i, more):
                    for e in range(NE):
                        if e < NE - 2:
                            layer1(g, u, e + 2)
                        elif more:
                            layer1(g + 1, 1 - u, e + 2 - NE)
                        if e < NE - 1:
                            layer2(g, e + 1)
                        elif more:
                            layer2(g + 1, 0)
                        if e == 0:
                            biases(g)
                        layer3(g, e)
                        if more and e == 2:
                            turn(g + 1, 1 - u)
                        if more and e == 3:
                            route(g + 1, 1 - u)
                        if more and e == 5:
                            turn_gates(g + 1, 1 - u)

                each_group(pe, group)

            @block.scalar
            def _(act):
                for n in range(n_w):
                    act.wait_ge(raw_in[n % 4], 16 * (n // 4 + 1))
                    act.activation(hi[n % LAYERS][n // LAYERS][:, :, :], raw[n % 4][:, :, :], ACT.Copy
                                   ).then_inc(w_high, 1)
                act.wait_ge(c_in, 64)
                act.activation(wr_hi[:, :, :], wr[:, :, :], ACT.Copy).then_inc(w_high, 1)

                def take_f(g, u):
                    act.wait_ge(f_mm, g + 1)
                    if isinstance(g, int) is False or g >= 1:
                        wait(act, h_mm[0], KT * NE * (g - 1))
                    for k in range(KT):
                        act.activation(f_hi[u][:, k, :], p_f[:, k, :], ACT.Copy).then_inc(f_high, 1)

                def exponent(g, u):
                    act.wait_ge(softmax, SOFTMAX * g + 2)
                    act.activation(logit[:, :, :], logit[:, :, :], ACT.Exp).then_inc(expd, 1)

                def take_gates(g):
                    act.wait_ge(gateT_mm, g + 1)
                    wait(act, bias_mm, g)
                    act.activation(gateT[:, :], p_gateT, ACT.Copy).then_inc(gateT_done, 1)

                def layer(l, g, e):
                    n = NE * g + e
                    reader = (h_mm[1], y_mm)[l]
                    wait(act, reader, KT * (n - 1) if l == 0 else n - 1)
                    for b in range(KT):
                        act.wait_ge(h_mm[l], KT * n + b + 1)
                        wait(act, h_low[l], KT * (n - 1) + b + 1)
                        c = e * KT + b
                        for t in (act_f[l], act_hi[l][e % 2]):
                            ins = act.activation(t[:, b, :], p_h[l][b][:, :], ACT.Relu,
                                                 scale=scale[:, l, c:c + 1], bias=shift[:, l, c:c + 1])
                        ins.then_inc(h_act[l], 1)

                act.wait_ge(prep, 2)
                take_f(0, 0)
                layer(0, 0, 0)
                exponent(0, 0)
                layer(0, 0, 1)
                take_gates(0)
                layer(1, 0, 0)

                def group(g, u, i, more):
                    for e in range(NE):
                        if e < NE - 2:
                            layer(0, g, e + 2)
                        elif more:
                            layer(0, g + 1, e + 2 - NE)
                        if e < NE - 1:
                            layer(1, g, e + 1)
                        elif more:
                            layer(1, g + 1, 0)
                        if more and e == 2:
                            take_f(g + 1, 1 - u)
                        if more and e == 3:
                            exponent(g + 1, 1 - u)
                        if more and e == 5:
                            take_gates(g + 1)

                each_group(act, group)

            @block.vector
            def _(dve):
                dve.wait_ge(c_in, 64)
                b_, g_, be, mean, var = (bn[:, c, :, :] for c in range(5))
                dve.tensor_scalar(var, var, BN_EPS, None, ALU.add).then_inc(normed_w, 1)
                rsqrt(dve, scale[:, :, :], var, bt[:, :, :], normed_w, 1)
                k = 1 + RSQRT_OPS
                dve.wait_ge(normed_w, k)
                dve.tensor_tensor(scale[:, :, :], scale[:, :, :], g_, ALU.mult).then_inc(normed_w, 1)
                dve.tensor_tensor(shift[:, :, :], b_, mean, ALU.subtract).then_inc(normed_w, 1)
                dve.wait_ge(normed_w, k + 2)
                dve.tensor_tensor(shift[:, :, :], shift[:, :, :], scale[:, :, :], ALU.mult
                                  ).then_inc(normed_w, 1)
                dve.wait_ge(normed_w, k + 3)
                dve.tensor_tensor(shift[:, :, :], shift[:, :, :], be, ALU.add).then_inc(prep, 1)
                for n in range(n_w):
                    dve.wait_ge(w_high, n + 1)
                    dve.tensor_tensor(lo[n % LAYERS][n // LAYERS][:, :, :], raw[n % 4][:, :, :],
                                      hi[n % LAYERS][n // LAYERS][:, :, :].bitcast(F32), ALU.subtract
                                      ).then_inc(w_low, 1)
                dve.wait_ge(w_high, n_w + 1)
                dve.tensor_tensor(wr_lo[:, :, :], wr[:, :, :], wr_hi[:, :, :].bitcast(F32), ALU.subtract
                                  ).then_inc(prep, 1)

                def norm(g, u, i):
                    dve.wait_ge(x_in[u], 16 * (i + 1))
                    wait(dve, f_mm, g)
                    norm_rows(dve, f, x3[u], w, normed, NORM_OPS * g)

                def low_f(g, u):
                    for k in range(KT):
                        dve.wait_ge(f_high, KT * g + k + 1)
                        dve.tensor_tensor(f_lo[u][:, k, :], p_f[:, k, :], f_hi[u][:, k, :].bitcast(F32),
                                          ALU.subtract).then_inc(f_low, 1)

                def softmax_a(g):
                    base = SOFTMAX * g
                    dve.wait_ge(logit_mm, g + 1)
                    wait(dve, softmax, base)
                    dve.tensor_tensor(logit[:, :, :], p_logit, across(br[:, :], TPG), ALU.add
                                      ).then_inc(softmax_in, 1)
                    dve.wait_ge(softmax_in, g + 1)
                    dve.tensor_reduce(top[:, :], logit[:, :, :], AX.X, ALU.max).then_inc(softmax, 1)
                    dve.wait_ge(softmax, base + 1)
                    dve.tensor_tensor(logit[:, :, :], logit[:, :, :],
                                      top[:, :].unsqueeze(2).broadcast_to([P, TPG, NE]), ALU.subtract
                                      ).then_inc(softmax, 1)

                def softmax_b(g, u):
                    base = SOFTMAX * g
                    dve.wait_ge(expd, g + 1)
                    dve.tensor_reduce(tot[:, :], logit[:, :, :], AX.X, ALU.add).then_inc(softmax, 1)
                    dve.wait_ge(softmax, base + 3)
                    dve.reciprocal(tot[:, :], tot[:, :]).then_inc(softmax, 1)
                    dve.wait_ge(softmax, base + 4)
                    dve.tensor_tensor(gate[u][:, :, :], logit[:, :, :],
                                      tot[:, :].unsqueeze(2).broadcast_to([P, TPG, NE]), ALU.mult
                                      ).then_inc(softmax, 1)

                def low(l, g, e):
                    n = NE * g + e
                    for b in range(KT):
                        dve.wait_ge(h_act[l], KT * n + b + 1)
                        dve.tensor_tensor(act_lo[l][e % 2][:, b, :], act_f[l][:, b, :],
                                          act_hi[l][e % 2][:, b, :].bitcast(F32), ALU.subtract
                                          ).then_inc(h_low[l], 1)

                def sum_biases(g, u):
                    dve.wait_ge(bias_mm, g + 1)
                    dve.tensor_tensor(x3[u][:, :, :], p_y[:, :, :], x3[u][:, :, :], ALU.add
                                      ).then_inc(acc_done, 1)

                def sum_expert(g, u, e):
                    dve.wait_ge(y_mm, NE * g + e + 1)
                    dve.wait_ge(acc_done, ACC * g + 1 + e)
                    for j in range(TPG):
                        ins = dve.scalar_tensor_tensor(x3[u][:, j, :], p_y[:, j, :],
                                                       gate[u][:, j, e:e + 1], x3[u][:, j, :],
                                                       ALU.mult, ALU.add)
                    ins.then_inc(acc_done, 1)

                norm(0, 0, 0)
                low_f(0, 0)
                low(0, 0, 0)
                softmax_a(0)
                softmax_b(0, 0)
                low(0, 0, 1)
                low(1, 0, 0)

                def group(g, u, i, more):
                    for e in range(NE):
                        if e < NE - 2:
                            low(0, g, e + 2)
                        elif more:
                            low(0, g + 1, e + 2 - NE)
                        if e < NE - 1:
                            low(1, g, e + 1)
                        elif more:
                            low(1, g + 1, 0)
                        if e == 0:
                            sum_biases(g, u)
                        sum_expert(g, u, e)
                        if more and e == 1:
                            norm(g + 1, 1 - u, i if u == 0 else i + 1)
                        if more and e == 2:
                            low_f(g + 1, 1 - u)
                        if more and e == 3:
                            softmax_a(g + 1)
                            softmax_b(g + 1, 1 - u)

                each_group(dve, group)


def build(nc, a):
    d = {"xn": nc.dram_tensor("xn_rows", (NP, D), F32).ap(),
         "xnT": nc.dram_tensor("xn_turned", (GROUPS, P, KT, G), F32).ap(),
         "pairs": nc.dram_tensor("xn_pairs", (NP, 2 * D), F16).ap(),
         "mid": nc.dram_tensor("mid_rows", (NP, D), F32).ap(),
         "all": nc.dram_tensor("all_rows", (NP, D), F32).ap()}
    with ExitStack() as ctx:
        keep = {}
        m = Names(nc, ctx, "keep")
        keep["ident"] = m.sb("ident", [P, P], F32)
        with ExitStack() as sums:
            s = Names(nc, sums, "keep")
            keep["iota"] = s.sb("iota", [P, P], F32)
            keep["base"] = s.sb("base", [P, TILES], F32)
            keep["first"] = s.sb("first", [P, SUPER], I32)
            keep["count"] = s.sb("count", [P, SUPER], I32)
            keep["red"] = s.sb("red", [P, TILES, D], F32)
            keep["rel_count"] = s.sb("rel_count", [P, TILES, RELS], F32)
            norm_phase(nc, a, d, keep)
            mix_phase(nc, a, d, keep)
            gru_phase(nc, a, d, keep)
        experts_phase(nc, a, d, keep)


def kernel(x, src, dst, edge_type_16, **w):
    import numpy as np

    import concourse.bacc as bacc
    from concourse.bass_utils import run_bass_kernel_spmd

    def get(name):
        return np.asarray(w[name])

    def columns(v):
        v = np.asarray(v)
        return v.reshape(-1, P).T

    xp = np.zeros((NP, D), np.float32)
    xp[:N] = np.asarray(x)
    edges = np.zeros((3, EP), np.int32)
    edges[1, :] = N
    for k, v in enumerate((src, dst, edge_type_16)):
        edges[k, :E] = np.asarray(v)
    by_super = np.ascontiguousarray(edges.reshape(3, SUPER, SC, P).transpose(1, 3, 0, 2))
    M, F, R = "L0_mix_", "L0_ffn_", "L0_gnn_"
    b_ih, b_hh = get(R + "b_ih"), get(R + "b_hh")
    arrays = {
        "x": xp,
        "edges": by_super,
        "dst_by_super": np.ascontiguousarray(by_super[:, :, 1, :].transpose(1, 0, 2)),
        "identity": np.eye(P, dtype=np.float32),
        "iota": np.arange(P, dtype=np.float32),
        "tile_base": np.arange(TILES, dtype=np.float32) * P,
        "w_kv": np.concatenate([get(M + "Wk"), get(M + "Wv")], axis=1),
        "b_kv": np.concatenate([get(M + "bk"), get(M + "bv")]),
        "w_q": get(M + "Wq"), "w_o": get(M + "Wo"), "w_ff1": get(M + "W1"), "w_ff2": get(M + "W2"),
        "rows5": np.stack([get(M + n) for n in ("bo", "ln1_b", "b2", "ln2_g", "ln2_b")]),
        "ln1_g": get(M + "ln1_g"),
        "mix_cols": np.concatenate([columns(get(M + n)) for n in ("bq", "ln1_g", "ln1_b", "b1")], axis=1),
        "w_ihT": np.ascontiguousarray(get(R + "w_ih").T),
        "w_hhT": np.ascontiguousarray(get(R + "w_hh").T),
        "rel": get(R + "relvectors"),
        "gru_cols": np.concatenate([columns(b_ih), columns(b_hh[2 * D:])], axis=1),
        "gru_gate_cols": columns(b_hh[:2 * D]),
        "w_router": get(F + "Wr"), "b_router": get(F + "br"), "b_out": get(F + "bo"),
        "w_experts": np.stack([get(F + n).reshape(NE, KT, P, D).transpose(0, 2, 1, 3)
                               for n in ("W1", "W2", "Wo")]),
        "bn_cols": np.stack([np.stack([columns(get(F + n + l)) for l in "12"], axis=1)
                             for n in ("b", "g", "be", "m", "v")], axis=1),
    }
    arrays = {k: np.ascontiguousarray(v) for k, v in arrays.items()}
    nc = bacc.Bacc("TRN2", target_bir_lowering=False, num_devices=1)
    aps = {k: nc.dram_tensor(f"in_{k}", v.shape, mybir.dt.from_np(v.dtype), kind="ExternalInput").ap()
           for k, v in arrays.items()}
    aps["out"] = nc.dram_tensor("out", (NP, D), F32, kind="ExternalOutput").ap()
    build(nc, aps)
    res = run_bass_kernel_spmd(nc, [{f"in_{k}": v for k, v in arrays.items()}], core_ids=[0])
    return res.results[0]["out"][:N]
```

```python
from contextlib import ExitStack

import concourse.bass as bass
from concourse import mybir

ALU = mybir.AluOpType
ACT = mybir.ActivationFunctionType
AX = mybir.AxisListType
F32 = mybir.dt.float32
F32R = mybir.dt.float32r
F16 = mybir.dt.float16
I32 = mybir.dt.int32

P = 128
N, D = 12500, 256
KT = D // P
TPG = 4
G = TPG * P
GROUPS = -(-N // G)
PAIRS = GROUPS // 2
NP = GROUPS * G
TILES = NP // P
E = 200000
SC = 8
SA, SB = 2, 6
SUPER = GROUPS * (SA + SB)
EP = SUPER * SC * P
RELS = 16
FF = 1024
FT = FF // P
HD = 32
NE = 8
LN_EPS = 1e-5
BN_EPS = 1e-3
DEN_EPS = 1e-6
PAIR = 2048.0
RT = N // P + 1
RW = D + RELS
MW = 2 * D + RELS
VALID = N - (GROUPS - 1) * G
NEWTON = 3
RSQRT_OPS = 1 + 3 * NEWTON
NORM_OPS = 4 + RSQRT_OPS + 1

assert GROUPS % 2 == 1 and EP >= E and TILES <= P and 2 * SA % 4 == 0 and 2 * SB % 4 == 0


def wait(eng, sem, value):
    if not isinstance(value, int) or value > 0:
        eng.wait_ge(sem, value)


def each_group(eng, group):
    group(0, 0, 0, True)
    group(1, 1, 0, True)
    with eng.Fori(1, PAIRS) as i:
        group(i * 2, 0, i, True)
        group(i * 2 + 1, 1, i, True)
    group(GROUPS - 1, 0, PAIRS, False)


def rsqrt(dve, y, v, t, done, base):
    dve.wait_ge(done, base)
    dve.tensor_scalar(y.bitcast(I32), v.bitcast(I32), -0.5, 1597463007.0,
                      ALU.mult, ALU.add).then_inc(done, 1)
    k = base + 1
    for _ in range(NEWTON):
        dve.wait_ge(done, k)
        dve.scalar_tensor_tensor(t, y, -0.5, y, ALU.mult, ALU.mult).then_inc(done, 1)
        dve.wait_ge(done, k + 1)
        dve.tensor_tensor(t, t, v, ALU.mult).then_inc(done, 1)
        dve.wait_ge(done, k + 2)
        dve.scalar_tensor_tensor(y, t, 1.5, y, ALU.add, ALU.mult).then_inc(done, 1)
        k = k + 3


def norm_rows(dve, out, x, w, done, base):
    for j in range(TPG):
        ins = dve.bn_stats(w["st"][:, j, :], x[:, j, :])
    ins.then_inc(done, 1)
    dve.wait_ge(done, base + 1)
    dve.sem_inc(done, 1)
    for j in range(TPG):
        ins = dve.bn_aggr(w["mv"][:, j, :], w["st"][:, j, :])
    ins.then_inc(done, 1)
    dve.wait_ge(done, base + 3)
    dve.tensor_scalar(w["ve"][:, :], w["mv"][:, :, 1], LN_EPS, None, ALU.add).then_inc(done, 1)
    rsqrt(dve, w["rs"][:, :], w["ve"][:, :], w["tt"][:, :], done, base + 4)
    dve.wait_ge(done, base + 4 + RSQRT_OPS)
    for j in range(TPG):
        ins = dve.tensor_scalar(out[:, j, :], x[:, j, :], w["mv"][:, j, 0:1], w["rs"][:, j:j + 1],
                                ALU.subtract, ALU.mult)
    ins.then_inc(done, 1)


def norm_work(sb):
    return {"st": sb("stats", [P, TPG, 6], F32), "mv": sb("mean_var", [P, TPG, 2], F32),
            "ve": sb("var_eps", [P, TPG], F32), "rs": sb("rstd", [P, TPG], F32),
            "tt": sb("newton", [P, TPG], F32)}


def rows(ap, g):
    return ap.rearrange("(g j p) d -> g p j d", j=TPG, p=P)[g]


def across(ap, n):
    return ap.unsqueeze(1).broadcast_to([ap.shape[0], n, ap.shape[1]])


class Names:

    def __init__(self, nc, ctx, phase):
        self.nc, self.ctx, self.phase = nc, ctx, phase

    def sb(self, name, shape, dt):
        return self.ctx.enter_context(self.nc.sbuf_tensor(f"{self.phase}_{name}", shape, dt))

    def ps(self, name, shape):
        return self.ctx.enter_context(self.nc.psum_tensor(f"{self.phase}_ps_{name}", shape, F32))

    def sem(self, name):
        return self.ctx.enter_context(self.nc.semaphore(f"{self.phase}_{name}"))


def norm_phase(nc, a, d, keep):
    with ExitStack() as ctx:
        m = Names(nc, ctx, "norm")
        x = [m.sb(f"x{u}", [P, TPG, D], F32) for u in range(2)]
        xn = [m.sb(f"xn{u}", [P, TPG, D], F32) for u in range(2)]
        pair = [m.sb(f"pair{u}", [P, TPG, 2, D], F16) for u in range(2)]
        xT = [m.sb(f"xT{u}", [P, KT, G], F32) for u in range(2)]
        w = norm_work(m.sb)
        dst = m.sb("dst", [P, SUPER, SC], I32)
        ends = m.sb("ends", [P, 2, SUPER], F32)
        ends_all = m.sb("ends_all", [P, 2, SUPER], F32)
        psT = [m.ps(f"T{u}", [P, KT, G]) for u in range(2)]

        x_in = [m.sem(f"x_in{u}") for u in range(2)]
        const_in = m.sem("const_in")
        ends_done = m.sem("ends_done")
        reduced = m.sem("reduced")
        normed = m.sem("normed")
        high_done = m.sem("high_done")
        low_done = m.sem("low_done")
        turned = m.sem("turned")
        xT_done = m.sem("xT_done")
        rows_out = [m.sem(f"rows_out{u}") for u in range(2)]
        pair_out = [m.sem(f"pair_out{u}") for u in range(2)]
        xT_out = [m.sem(f"xT_out{u}") for u in range(2)]

        with nc.Block() as block:
            @block.sync
            def _(sp):
                sp.dma_start(x[0][:, :, :], rows(a["x"], 0)).then_inc(x_in[0], 16)
                sp.dma_start(keep["ident"][:, :], a["identity"]).then_inc(const_in, 16)
                sp.dma_start(dst[:, :, :], a["dst_by_super"]).then_inc(const_in, 16)

                def group(g, u, i, more):
                    if more:
                        wait(sp, normed, g * NORM_OPS)
                        sp.dma_start(x[1 - u][:, :, :], rows(a["x"], g + 1)).then_inc(x_in[1 - u], 16)
                    sp.wait_ge(normed, (g + 1) * NORM_OPS)
                    sp.dma_start(rows(d["xn"], g), xn[u][:, :, :]).then_inc(rows_out[u], 16)
                    sp.wait_ge(xT_done, g + 1)
                    sp.dma_start(d["xnT"][g], xT[u][:, :, :]).then_inc(xT_out[u], 16)
                    if not (isinstance(g, int) and g == 0):
                        pairs(g - 1, 1 - u)
                    if not more:
                        pairs(g, u)

                def pairs(g, u):
                    sp.wait_ge(low_done, g + 1)
                    sp.dma_start(rows(d["pairs"], g), pair[u][:, :, :, :].rearrange("p j h d -> p j (h d)")
                                 ).then_inc(pair_out[u], 16)

                each_group(sp, group)
                for u in range(2):
                    for out in (rows_out[u], pair_out[u], xT_out[u]):
                        sp.wait_ge(out, 16 * (PAIRS + 1 - u))
                sp.dma_start(d["xnT"][GROUPS], xT[0][:, :, :]).then_inc(xT_out[0], 16)
                sp.wait_ge(xT_out[0], 16 * (PAIRS + 2))

            @block.vector
            def _(dve):
                dve.wait_ge(const_in, 32)
                dve.tensor_reduce(ends[:, 0, :], dst[:, :, :], AX.X, ALU.max)
                dve.tensor_reduce(ends[:, 1, :], dst[:, :, :], AX.X, ALU.min, negate=True
                                  ).then_inc(ends_done, 1)

                def group(g, u, i, more):
                    dve.wait_ge(x_in[u], 16 * (i + 1))
                    wait(dve, low_done, g - 1)
                    wait(dve, rows_out[u], 16 * i)
                    wait(dve, turned, g - 1)
                    norm_rows(dve, xn[u], x[u], w, normed, g * NORM_OPS)
                    if isinstance(g, int) and g == 0:
                        return
                    low_half(g - 1, 1 - u)
                    if not more:
                        low_half(g, u)

                def low_half(g, u):
                    dve.wait_ge(high_done, g + 1)
                    dve.scalar_tensor_tensor(pair[u][:, :, 0, :], xn[u][:, :, :], PAIR,
                                             pair[u][:, :, 1, :], ALU.mult, ALU.subtract
                                             ).then_inc(low_done, 1)

                each_group(dve, group)
                dve.wait_ge(reduced, 1)
                dve.tensor_copy(keep["count"][:, :], ends_all[:, 0, :])
                dve.tensor_scalar(keep["first"][:, :], ends_all[:, 1, :], -1.0, None, ALU.mult
                                  ).then_inc(ends_done, 1)
                dve.wait_ge(ends_done, 2)
                dve.tensor_scalar(keep["count"][:, :], keep["count"][:, :], 7, None,
                                  ALU.logical_shift_right)
                dve.tensor_scalar(keep["first"][:, :], keep["first"][:, :], 7, None,
                                  ALU.logical_shift_right).then_inc(ends_done, 1)
                dve.wait_ge(ends_done, 3)
                dve.scalar_tensor_tensor(keep["count"][:, :], keep["count"][:, :], 1.0,
                                         keep["first"][:, :], ALU.add, ALU.subtract
                                         ).then_inc(ends_done, 1)
                dve.wait_ge(ends_done, 4)

            @block.gpsimd
            def _(pool):
                pool.memset(keep["red"][:, :, :], 0.0)
                pool.wait_ge(ends_done, 1)
                pool.partition_all_reduce(ends_all[:, :, :].rearrange("p a s -> p (a s)"),
                                          ends[:, :, :].rearrange("p a s -> p (a s)"), P,
                                          bass.bass_isa.ReduceOp.max).then_inc(reduced, 1)

            @block.tensor
            def _(pe):
                pe.wait_ge(const_in, 32)

                def group(g, u, i, more):
                    pe.wait_ge(normed, (g + 1) * NORM_OPS)
                    wait(pe, xT_done, g - 1)
                    for k in range(KT):
                        for j in range(TPG):
                            ins = pe.transpose(psT[u][:, k, j * P:(j + 1) * P],
                                               xn[u][:, j, k * P:(k + 1) * P], keep["ident"][:, :])
                    ins.then_inc(turned, 1)

                each_group(pe, group)

            @block.scalar
            def _(act):
                def group(g, u, i, more):
                    act.wait_ge(normed, (g + 1) * NORM_OPS)
                    wait(act, pair_out[u], 16 * i)
                    act.activation(pair[u][:, :, 1, :], xn[u][:, :, :], ACT.Copy, scale=PAIR
                                   ).then_inc(high_done, 1)
                    act.wait_ge(turned, g + 1)
                    wait(act, xT_out[u], 16 * i)
                    for k in range(KT):
                        ins = act.activation(xT[u][:, k, :], psT[u][:, k, :], ACT.Copy)
                    ins.then_inc(xT_done, 1)

                each_group(act, group)


class Super:

    def __init__(self, per_pair, i, k):
        self.s = i * per_pair + k
        self.ring4, self.turn4 = k % 4, i * (per_pair // 4) + k // 4
        self.ring2, self.turn2 = k % 2, i * (per_pair // 2) + k // 2


def super_a(i, u, q):
    return Super(2 * SA, i, SA * u + q)


def super_b(i, u, q):
    return Super(2 * SB, i, GROUPS * SA + SB * u + q)


ATT = 1 + NORM_OPS + 2
ATT_N = 1 + NORM_OPS
END = 1 + NORM_OPS + 3


def mix_phase(nc, a, d, keep):
    with ExitStack() as ctx:
        m = Names(nc, ctx, "mix")
        wkv = m.sb("wkv", [P, KT, 2 * D], F32)
        wq = m.sb("wq", [P, KT, D], F32)
        wo = m.sb("wo", [P, KT, D], F32)
        w1 = m.sb("w1", [P, KT, FF], F32)
        w2 = m.sb("w2", [P, FT, D], F32)
        bkv = m.sb("bkv", [P, 2 * D], F32)
        row6 = m.sb("row6", [P, 6, D], F32)
        row_bo, row_n1b, row_b2, row_g2, row_n2b, row_g1 = (row6[:, c, :] for c in range(6))
        row_res = row_n1b
        col = m.sb("col", [P, 3 * KT + FT], F32)
        bq, g1, n1b, b1 = (col[:, 0:KT], col[:, KT:2 * KT], col[:, 2 * KT:3 * KT], col[:, 3 * KT:])
        kvb = m.sb("kvb", [P, KT, P], F32)
        ksb = m.sb("ksb", [P, KT, P], F32)
        eps = m.sb("eps", [P, 1], F32)
        edge = [m.sb(f"edge{r}", [P, 3, SC], I32) for r in range(4)]
        msg = [m.sb(f"msg{r}", [P, SC, MW], F16) for r in range(2)]
        hot = m.sb("hot", [P, 2, SC, P], F16)
        xT = [m.sb(f"xT{u}", [P, KT, G], F32) for u in range(2)]
        xn = m.sb("xn", [P, TPG, D], F32)
        ex = m.sb("ex", [P, G], F32)
        qphi = m.sb("qphi", [P, KT, G], F32)
        x1T = m.sb("x1T", [P, KT, G], F32)
        h = m.sb("h", [P, FT, G], F32)
        out0 = m.sb("out", [P, TPG, D], F32)
        w = norm_work(m.sb)
        out = [out0[:, :, :], wkv[:, :, :].rearrange("p k (a d) -> p (k a) d", a=2)]
        z = bkv[:, :]
        x = xT[0][:, :, :].rearrange("p k (a d) -> p (k a) d", a=2)
        kb = [h[:, r, 0:D] for r in (0, 1)]
        va = [h[:, 2 + r, 0:KT * (P + 2)].rearrange("p (b c) -> p b c", b=KT) for r in (0, 1)]
        kex = [h[:, 4 + r, 0:D] for r in (0, 1)]
        kre = [h[:, 4 + r, D:2 * D] for r in (0, 1)]
        kphi = [h[:, 6 + r, 0:D] for r in (0, 1)]
        zero, ones = qphi[:, 0, 0:P], x1T[:, 0, 0:HD]

        pa = [m.ps(f"pa{r}", [P, G]) for r in range(2)]
        pb = m.ps("pb", [P, TPG, D])
        pc = m.ps("pc", [P, TPG, D])
        pbf = pb[:, :, :].rearrange("p (b j) d -> p b (j d)", b=2)
        pcf = pc[:, :, :].rearrange("p (b j) d -> p b (j d)", b=2)
        ring = [pa[0][:, :], pa[1][:, :], pbf[:, 0, :], pbf[:, 1, :]]
        seg = m.ps("seg", [P, 2, 2 * D])
        acc = pcf[:, 0, 0:KT * (P + 2)].rearrange("p (b c) -> p b c", b=KT)

        w_in = m.sem("w_in")
        edge_in = [m.sem(f"edge_in{r}") for r in range(4)]
        gathered = [m.sem(f"gathered{r}") for r in range(2)]
        gather_go = m.sem("gather_go")
        hot_ready = m.sem("hot_ready")
        summed = m.sem("summed")
        added = m.sem("added")
        super_done = m.sem("super_done")
        xT_in = [m.sem(f"xT_in{u}") for u in range(2)]
        xn_in, x_in = m.sem("xn_in"), m.sem("x_in")
        set_up = m.sem("set_up")
        kv_mm, kv_bias, kv_act, kphi_done, acc_mm = (
            m.sem(n) for n in ("kv_mm", "kv_bias", "kv_act", "kphi_done", "acc_mm"))
        heads_done = m.sem("heads_done")
        q_mm, q_act, qphi_done, nd_mm, den_done, rec_done, attn_done, wo_mm = (
            m.sem(n) for n in ("q_mm", "q_act", "qphi_done", "nd_mm", "den_done", "rec_done",
                               "attn_done", "wo_mm"))
        xn_bo, att, x1_mm, x1T_done, ff1_mm, h_done, ff2_mm, end, stored = (
            m.sem(n) for n in ("xn_bo", "att", "x1_mm", "x1T_done", "ff1_mm", "h_done", "ff2_mm",
                               "end", "stored"))
        N_W = 16 * 11

        with nc.Block() as block:
            @block.sync
            def _(sp):
                def edges(s, r):
                    sp.dma_start(edge[r][:, :, :], a["edges"][s]).then_inc(edge_in[r], 16)

                def next_edges(c):
                    if isinstance(c.s, int) and c.s + 4 >= SUPER:
                        return
                    sp.wait_ge(super_done, c.s + 1)
                    edges(c.s + 4, c.ring4)

                for r in range(4):
                    edges(r, r)
                sp.dma_start(xT[0][:, :, :], d["xnT"][0]).then_inc(xT_in[0], 16)

                def group_a(g, u, i, more):
                    if more:
                        wait(sp, kv_mm, TPG * g)
                        sp.dma_start(xT[1 - u][:, :, :], d["xnT"][g + 1]).then_inc(xT_in[1 - u], 16)
                    else:
                        sp.wait_ge(kv_mm, TPG * g)
                        sp.dma_start(xT[1][:, :, :], d["xnT"][0]).then_inc(xT_in[1], 16)
                        sp.dma_start(xn[:, :, :], rows(d["xn"], 0)).then_inc(xn_in, 16)
                    for q in range(SA):
                        next_edges(super_a(i, u, q))

                each_group(sp, group_a)
                sp.wait_ge(q_mm, KT)
                sp.dma_start(xT[1][:, :, :], d["xnT"][1]).then_inc(xT_in[1], 16)

                def group_b(g, u, i, more):
                    next_edges(super_b(i, u, 0))
                    if not (isinstance(g, int) and g >= GROUPS - 2):
                        sp.wait_ge(q_mm, KT * (g + 2))
                        sp.dma_start(xT[1][:, :, :], d["xnT"][g + 2]).then_inc(xT_in[1], 16)
                    next_edges(super_b(i, u, 1))
                    if more:
                        sp.wait_ge(att, ATT * (g + 1))
                        sp.wait_ge(x1_mm, g + 1)
                        sp.dma_start(xn[:, :, :], rows(d["xn"], g + 1)).then_inc(xn_in, 16)
                    next_edges(super_b(i, u, 2))
                    next_edges(super_b(i, u, 3))
                    if isinstance(g, int) and g == 0:
                        sp.dma_start(x, rows(a["x"], 0)).then_inc(x_in, 16)
                    else:
                        sp.wait_ge(end, END * g)
                        sp.dma_start(rows(d["mid"], g - 1), out[1 - u]).then_inc(stored, 16)
                        sp.dma_start(x, rows(a["x"], g)).then_inc(x_in, 16)
                    next_edges(super_b(i, u, 4))
                    next_edges(super_b(i, u, 5))

                each_group(sp, group_b)
                sp.wait_ge(xT_in[1], 16 * (PAIRS + GROUPS + 1))
                sp.wait_ge(end, END * GROUPS)
                sp.dma_start(rows(d["mid"], GROUPS - 1), out[0]).then_inc(stored, 16)
                sp.wait_ge(stored, 16 * GROUPS)

            @block.gpsimd
            def _(pool):
                def gather(c):
                    pool.wait_ge(edge_in[c.ring4], 16 * (c.turn4 + 1))
                    wait(pool, super_done, c.s - 1)
                    pool.sem_inc(gather_go, 1)
                    for k in range(SC):
                        pool.indirect_dma_start(
                            msg[c.ring2][:, k, 0:2 * D], None, d["pairs"],
                            bass.IndirectOffsetOnAxis(edge[c.ring4][:, 0, k:k + 1], 0)
                        ).then_inc(gathered[c.ring2], 16)

                for k in range(4):
                    gather(Super(4, 0, k))
                with pool.Fori(1, SUPER // 4) as i:
                    for k in range(4):
                        gather(Super(4, i, k))

            @block.tensor
            def _(pe):
                visit = pe.alloc_register("pe_visit")
                pe.reg_mov(visit, 0)
                pe.sem_inc(summed, 1)

                def segment(c):
                    count = pe.value_load(keep["count"][0:1, bass.ds(c.s, 1)], min_val=1, max_val=RT)
                    with pe.Fori(0, count):
                        v = pe.snap(visit)
                        pe.wait_ge(gathered[c.ring2], 16 * SC * (c.turn2 + 1))
                        pe.wait_ge(hot_ready, v + 1)
                        pe.wait_ge(added, v + 1)
                        to = seg[:, bass.ds(v % 2, 1), :].rearrange("p a d -> p (a d)")
                        on = hot[:, bass.ds(v % 2, 1), :, :].rearrange("p a c n -> p (a c) n")
                        for k in range(SC):
                            pe.matmul(to[:, 0:RW], on[:, k, :], msg[c.ring2][:, k, D:MW],
                                      start=(k == 0), stop=False)
                            ins = pe.matmul(to[:, 0:D], on[:, k, :], msg[c.ring2][:, k, 0:D],
                                            start=False, stop=(k == SC - 1))
                        ins.then_inc(summed, 1)
                        pe.reg_add(visit, visit, 1)
                    pe.drain().then_inc(super_done, 1)

                pe.wait_ge(w_in, N_W)
                pe.wait_ge(set_up, 1)
                pe.matmul(pcf[:, 0, 0:KT * (P + 2)], zero, wkv[:, 0, 0:KT * (P + 2)],
                          start=True, stop=False, skip_group_check=True)

                def group_a(g, u, i, more):
                    pe.wait_ge(xT_in[u], 16 * (i + 1))

                    def project(j):
                        wait(pe, kv_bias, TPG * g + j - 1)
                        for k in range(KT):
                            ins = pe.matmul(pa[j % 2][:, :], xT[u][:, k, j * P:(j + 1) * P],
                                            wkv[:, k, :], start=(k == 0), stop=(k == KT - 1))
                        ins.then_inc(kv_mm, 1)

                    def accumulate(j):
                        n = P if more else max(0, min(P, VALID - j * P))
                        if n == 0:
                            return
                        pe.wait_ge(kphi_done, TPG * g + j + 1)
                        last = not more and j == (VALID - 1) // P
                        for b in range(KT):
                            ins = pe.matmul(acc[:, b, 0:P + 1], kphi[j % 2][0:n, b * P:(b + 1) * P],
                                            va[j % 2][0:n, b, 0:P + 1], start=False, stop=last,
                                            skip_group_check=True)
                        ins.then_inc(acc_mm, 1)

                    project(0)
                    project(1)
                    segment(super_a(i, u, 0))
                    accumulate(0)
                    project(2)
                    accumulate(1)
                    project(3)
                    segment(super_a(i, u, 1))
                    accumulate(2)
                    accumulate(3)

                each_group(pe, group_a)

                def queries(g):
                    pe.wait_ge(xT_in[1], 16 * (PAIRS + 1 + g))
                    wait(pe, q_act, KT * g)
                    wait(pe, h_done, FT * (g - 1))
                    for b in range(KT):
                        for k in range(KT):
                            ins = pe.matmul(pa[b][:, :], wq[:, k, b * P:(b + 1) * P], xT[1][:, k, :],
                                            start=(k == 0), stop=(k == KT - 1))
                        ins.then_inc(q_mm, 1)

                def attend(g, b):
                    pe.wait_ge(qphi_done, KT * g + b + 1)
                    wait(pe, attn_done, KT * g + b)
                    if b == 0:
                        wait(pe, end, END * (g - 2) + 1)
                    pe.matmul(pcf[:, 0, :], kvb[:, b, :], qphi[:, b, :], start=True, stop=True)
                    pe.matmul(pcf[:, 1, :], ksb[:, b, :], qphi[:, b, :], start=True, stop=True
                              ).then_inc(nd_mm, 1)

                def project_out(g):
                    pe.wait_ge(attn_done, KT * (g + 1))
                    wait(pe, h_done, FT * g)
                    for j in range(TPG):
                        for k in range(KT):
                            ins = pe.matmul(pb[:, j, :], qphi[:, k, j * P:(j + 1) * P], wo[:, k, :],
                                            start=(k == 0), stop=(k == KT - 1))
                    ins.then_inc(wo_mm, 1)

                def feed(g, f, more):
                    if f < 2:
                        if more:
                            pe.wait_ge(q_act, KT * (g + 2))
                    elif f >= 4:
                        pe.wait_ge(h_done, FT * g + f - 3)
                    for k in range(KT):
                        ins = pe.matmul(ring[f % 4], w1[:, k, f * P:(f + 1) * P], x1T[:, k, :],
                                        start=(k == 0), stop=(k == KT - 1))
                    ins.then_inc(ff1_mm, 1)

                pe.wait_ge(heads_done, 1)
                queries(0)
                attend(0, 0)
                attend(0, 1)
                project_out(0)

                def group_b(g, u, i, more):
                    segment(super_b(i, u, 0))
                    if more:
                        queries(g + 1)
                    pe.wait_ge(att, ATT * g + ATT_N)
                    for k in range(KT):
                        for j in range(TPG):
                            ins = pe.transpose(pbf[:, k, j * P:(j + 1) * P], xn[:, j, k * P:(k + 1) * P],
                                               keep["ident"][:, :])
                    ins.then_inc(x1_mm, 1)
                    segment(super_b(i, u, 1))
                    pe.wait_ge(x1T_done, KT * (g + 1))
                    for f in range(4):
                        feed(g, f, more)
                    if more:
                        attend(g + 1, 0)
                    feed(g, 4, more)
                    feed(g, 5, more)
                    segment(super_b(i, u, 2))
                    if more:
                        attend(g + 1, 1)
                    feed(g, 6, more)
                    feed(g, 7, more)
                    segment(super_b(i, u, 3))
                    pe.wait_ge(h_done, FT * (g + 1))
                    if more:
                        pe.wait_ge(attn_done, KT * (g + 2))
                    wait(pe, end, END * (g - 1) + 1)
                    for j in range(TPG):
                        for k in range(FT):
                            ins = pe.matmul(pc[:, j, :], h[:, k, j * P:(j + 1) * P], w2[:, k, :],
                                            start=(k == 0), stop=(k == FT - 1))
                    ins.then_inc(ff2_mm, 1)
                    segment(super_b(i, u, 4))
                    if more:
                        project_out(g + 1)
                    segment(super_b(i, u, 5))

                each_group(pe, group_b)

            @block.scalar
            def _(act):
                feats = "(k p) n -> p k n"
                for t, src in ((wkv[:, :, :], a["w_kv"].rearrange(feats, p=P)),
                               (bkv[:, :], a["b_kv"].partition_broadcast(P)),
                               (keep["iota"][:, :], a["iota"].partition_broadcast(P)),
                               (keep["base"][:, :], a["tile_base"].partition_broadcast(P)),
                               (wq[:, :, :], a["w_q"].rearrange(feats, p=P)),
                               (wo[:, :, :], a["w_o"].rearrange(feats, p=P)),
                               (w1[:, :, :], a["w_ff1"].rearrange(feats, p=P)),
                               (w2[:, :, :], a["w_ff2"].rearrange(feats, p=P)),
                               (row6[:, 0:5, :], a["rows5"].partition_broadcast(P)),
                               (row_g1, a["ln1_g"].partition_broadcast(P)),
                               (col[:, :], a["mix_cols"])):
                    act.dma_start(t, src).then_inc(w_in, 16)
                act.wait_ge(w_in, N_W)
                act.wait_ge(set_up, 1)

                def group_a(g, u, i, more):
                    for j in range(TPG):
                        act.wait_ge(kv_bias, TPG * g + j + 1)
                        wait(act, kphi_done, TPG * g + j - 1)
                        act.activation(kex[j % 2], kb[j % 2], ACT.Exp)
                        act.activation(kre[j % 2], kb[j % 2], ACT.Relu).then_inc(kv_act, 1)

                each_group(act, group_a)

                def query_act(g):
                    wait(act, wo_mm, g)
                    for b in range(KT):
                        act.wait_ge(q_mm, KT * g + b + 1)
                        wait(act, qphi_done, KT * g + b)
                        act.activation(ex[:, :], pa[b][:, :], ACT.Exp, bias=bq[:, b:b + 1])
                        act.activation(qphi[:, b, :], pa[b][:, :], ACT.Relu, bias=bq[:, b:b + 1]
                                       ).then_inc(q_act, 1)

                def denominator(g, b):
                    k = KT * g + b
                    act.wait_ge(nd_mm, k + 1)
                    wait(act, attn_done, k)
                    act.activation(z, pcf[:, 1, :], ACT.Identity, bias=eps[:, :]).then_inc(den_done, 1)

                query_act(0)
                denominator(0, 0)
                denominator(0, 1)

                def group_b(g, u, i, more):
                    if more:
                        query_act(g + 1)
                    act.wait_ge(x1_mm, g + 1)
                    wait(act, ff1_mm, FT * g)
                    for k in range(KT):
                        act.activation(x1T[:, k, :], pbf[:, k, :], ACT.Identity, scale=g1[:, k:k + 1],
                                       bias=n1b[:, k:k + 1]).then_inc(x1T_done, 1)
                    wait(act, ff2_mm, g)
                    for f in range(FT):
                        if f == 4 and more:
                            denominator(g + 1, 0)
                        if f == 6 and more:
                            denominator(g + 1, 1)
                        act.wait_ge(ff1_mm, FT * g + f + 1)
                        act.activation(h[:, f, :], ring[f % 4], ACT.Relu, bias=b1[:, f:f + 1]
                                       ).then_inc(h_done, 1)

                each_group(act, group_b)

            @block.vector
            def _(dve):
                visit = dve.alloc_register("dve_visit")
                tile = dve.alloc_register("dve_tile")
                last = dve.alloc_register("dve_last")
                dve.reg_mov(visit, 0)
                dve.reg_mov(last, 0)
                dve.sem_inc(added, 1)
                dve.memset(zero, 0.0)
                dve.memset(ones, 1.0)
                dve.memset(eps[:, :], DEN_EPS)
                dve.memset(kvb[:, :, :], 0.0)
                dve.memset(ksb[:, :, :], 0.0)
                dve.memset(seg[:, 1, 0:RW], 0.0)
                for r in range(2):
                    ins = dve.memset(va[r][:, :, P:P + 2], 1.0)
                ins.then_inc(set_up, 1)
                dve.wait_ge(w_in, N_W)
                dve.wait_ge(set_up, 1)
                dve.tensor_tensor(row_res, row_n1b, row_b2, ALU.add).then_inc(set_up, 1)

                def add_last(v):
                    t = dve.snap(last, min_val=0, max_val=RT - 1)
                    dve.wait_ge(summed, v + 1)
                    dve.wait_ge(added, v + 1)
                    red = keep["red"][:, bass.ds(t, 1), :].rearrange("p a d -> p (a d)")
                    was = seg[:, bass.ds((v + 1) % 2, 1), 0:RW].rearrange("p a d -> p (a d)")
                    dve.tensor_tensor(red, was, red, ALU.add).then_inc(added, 1)

                def segment(c):
                    first = dve.value_load(keep["first"][0:1, bass.ds(c.s, 1)], min_val=0,
                                           max_val=RT - 1)
                    count = dve.value_load(keep["count"][0:1, bass.ds(c.s, 1)], min_val=1,
                                           max_val=RT)
                    dve.reg_mov(tile, first)
                    dve.wait_ge(edge_in[c.ring4], 16 * (c.turn4 + 1))
                    wait(dve, super_done, c.s - 1)
                    e = edge[c.ring4]
                    dve.tensor_tensor(msg[c.ring2][:, :, 2 * D:MW],
                                      e[:, 2, :].unsqueeze(2).broadcast_to([P, SC, RELS]),
                                      across(keep["iota"][:, 0:RELS], SC), ALU.is_equal)
                    with dve.Fori(0, count):
                        v = dve.snap(visit)
                        t = dve.snap(tile, min_val=0, max_val=RT - 1)
                        dve.scalar_tensor_tensor(
                            hot[:, bass.ds(v % 2, 1), :, :].rearrange("p a c n -> p (a c) n"),
                            e[:, 1, :].unsqueeze(2).broadcast_to([P, SC, P]),
                            keep["base"][:, bass.ds(t, 1)], across(keep["iota"][:, :], SC),
                            ALU.subtract, ALU.is_equal).then_inc(hot_ready, 1)
                        add_last(v)
                        dve.reg_mov(last, tile)
                        dve.reg_add(visit, visit, 1)
                        dve.reg_add(tile, tile, 1)

                def group_a(g, u, i, more):
                    def bias(j):
                        dve.wait_ge(kv_mm, TPG * g + j + 1)
                        wait(dve, kv_act, TPG * g + j - 1)
                        wait(dve, acc_mm, TPG * g + j - 1)
                        dve.tensor_tensor(kb[j % 2], pa[j % 2][:, 0:D], bkv[:, 0:D], ALU.add)
                        dve.tensor_tensor(va[j % 2][:, :, 0:P],
                                          pa[j % 2][:, D:2 * D].rearrange("p (b c) -> p b c", b=KT),
                                          bkv[:, D:2 * D].rearrange("p (b c) -> p b c", b=KT),
                                          ALU.add).then_inc(kv_bias, 1)

                    def phi(j):
                        dve.wait_ge(kv_act, TPG * g + j + 1)
                        dve.scalar_tensor_tensor(kphi[j % 2], kex[j % 2], 1.0, kre[j % 2],
                                                 ALU.min, ALU.add).then_inc(kphi_done, 1)

                    segment(super_a(i, u, 0))
                    bias(0)
                    bias(1)
                    phi(0)
                    phi(1)
                    segment(super_a(i, u, 1))
                    bias(2)
                    bias(3)
                    phi(2)
                    phi(3)

                each_group(dve, group_a)
                dve.wait_ge(acc_mm, TPG * (GROUPS - 1) + -(-VALID // P))
                for b in range(KT):
                    for r in range(0, P, HD):
                        dve.tensor_copy(kvb[r:r + HD, b, r:r + HD], acc[r:r + HD, b, r:r + HD])
                        ins = dve.tensor_scalar(ksb[r:r + HD, b, r:r + HD], ones[r:r + HD, :],
                                                acc[r:r + HD, b, P:P + 1], None, ALU.mult)
                ins.then_inc(heads_done, 1)

                def query_phi(g):
                    for b in range(KT):
                        dve.wait_ge(q_act, KT * g + b + 1)
                        dve.scalar_tensor_tensor(qphi[:, b, :], ex[:, :], 1.0, qphi[:, b, :],
                                                 ALU.min, ALU.add).then_inc(qphi_done, 1)

                def attention(g, b):
                    k = KT * g + b
                    dve.wait_ge(den_done, k + 1)
                    dve.reciprocal(z, z).then_inc(rec_done, 1)
                    dve.wait_ge(rec_done, k + 1)
                    dve.tensor_tensor(qphi[:, b, :], pcf[:, 0, :], z, ALU.mult).then_inc(attn_done, 1)

                def residual(g):
                    dve.wait_ge(xn_in, 16 * (g + 1))
                    dve.tensor_tensor(xn[:, :, :], xn[:, :, :], across(row_bo, TPG), ALU.add
                                      ).then_inc(xn_bo, 1)

                def result_in(g, u):
                    dve.wait_ge(ff2_mm, g + 1)
                    dve.wait_ge(att, ATT * (g + 1))
                    dve.tensor_tensor(out[u], pc[:, :, :], out[u], ALU.add).then_inc(end, 1)

                def result(g, u):
                    base = END * g + 1
                    dve.wait_ge(end, base)
                    norm_rows(dve, out[u], out[u], w, end, base)
                    base = base + NORM_OPS
                    dve.wait_ge(end, base)
                    dve.tensor_tensor(out[u], out[u], across(row_g2, TPG), ALU.mult).then_inc(end, 1)
                    dve.wait_ge(end, base + 1)
                    dve.tensor_tensor(out[u], out[u], across(row_n2b, TPG), ALU.add).then_inc(end, 1)
                    dve.wait_ge(end, base + 2)
                    dve.wait_ge(x_in, 16 * (g + 1))
                    dve.tensor_tensor(out[u], out[u], x, ALU.add).then_inc(end, 1)

                residual(0)
                query_phi(0)
                attention(0, 0)
                attention(0, 1)

                def group_b(g, u, i, more):
                    zeroth = isinstance(g, int) and g == 0
                    segment(super_b(i, u, 0))
                    base = ATT * g
                    dve.wait_ge(wo_mm, g + 1)
                    dve.wait_ge(xn_bo, g + 1)
                    dve.tensor_tensor(xn[:, :, :], pb[:, :, :], xn[:, :, :], ALU.add).then_inc(att, 1)
                    dve.wait_ge(att, base + 1)
                    norm_rows(dve, xn, xn, w, att, base + 1)
                    segment(super_b(i, u, 1))
                    if not zeroth:
                        result_in(g - 1, 1 - u)
                    if more:
                        query_phi(g + 1)
                    dve.wait_ge(att, base + ATT_N)
                    wait(dve, stored, 16 * (g - 1))
                    dve.tensor_tensor(out[u], xn[:, :, :], across(row_g1, TPG), ALU.mult
                                      ).then_inc(att, 1)
                    dve.wait_ge(att, base + ATT_N + 1)
                    dve.tensor_tensor(out[u], out[u], across(row_res, TPG), ALU.add).then_inc(att, 1)
                    segment(super_b(i, u, 2))
                    if more:
                        attention(g + 1, 0)
                    segment(super_b(i, u, 3))
                    if more:
                        attention(g + 1, 1)
                    if not zeroth:
                        result(g - 1, 1 - u)
                    segment(super_b(i, u, 4))
                    if more:
                        residual(g + 1)
                    segment(super_b(i, u, 5))

                each_group(dve, group_b)
                add_last(dve.snap(visit))
                result_in(GROUPS - 1, 0)
                result(GROUPS - 1, 0)
                dve.wait_ge(end, END * GROUPS)


def gru_phase(nc, a, d, keep):
    with ExitStack() as ctx:
        m = Names(nc, ctx, "gru")
        raw = m.sb("raw", [P, KT, 3 * D], F32)
        w_hi = [m.sb(f"w_hi{s}", [P, KT, 3 * D], F32R) for s in range(2)]
        w_lo = [m.sb(f"w_lo{s}", [P, KT, 3 * D], F32R) for s in range(2)]
        rel = m.sb("rel", [RELS, D], F32)
        col = m.sb("col", [P, 4 * KT], F32)
        gate_b = m.sb("gate_b", [P, 2 * KT], F32)
        xT = [m.sb(f"xT{u}", [P, KT, G], F32) for u in range(2)]
        x_hi, x_lo = m.sb("x_hi", [P, KT, G], F32R), m.sb("x_lo", [P, KT, G], F32R)
        r_hi, r_lo = m.sb("r_hi", [P, KT, G], F32R), m.sb("r_lo", [P, KT, G], F32R)
        red = m.sb("red", [P, TPG, D], F32)
        relc = m.sb("relc", [P, TPG, RELS], F32)
        relT = m.sb("relT", [RELS, G], F32)
        gr, gz, gn = m.sb("gr", [P, G], F32), m.sb("gz", [P, G], F32), m.sb("gn", [P, G], F32)
        gT = m.sb("gT", [P, KT, G], F32)
        mid = [m.sb(f"mid{u}", [P, TPG, D], F32) for u in range(2)]

        p_red = m.ps("red", [P, KT, G])
        p_gate = [m.ps(f"gate{q}", [P, G]) for q in range(4)]
        p_out = m.ps("out", [P, TPG, D])
        p_relT = p_out[0:RELS, 0:2, :].rearrange("p a d -> p (a d)")

        w_in = [m.sem(f"w_in{s}") for s in range(2)]
        c_in = m.sem("c_in")
        w_split = m.sem("w_split")
        w_high = m.sem("w_high")
        bias_sum = m.sem("bias_sum")
        xT_in = [m.sem(f"xT_in{u}") for u in range(2)]
        mid_in = [m.sem(f"mid_in{u}") for u in range(2)]
        stored = [m.sem(f"stored{u}") for u in range(2)]
        (copied, relT_mm, relT_done, red_mm, high, x_low, r_high, r_low, gates, reset, hn, pre, tan,
         diff, prod, g_done, out_mm, sum_done) = (m.sem(n) for n in (
             "copied", "relT_mm", "relT_done", "red_mm", "high", "x_low", "r_high", "r_low", "gates",
             "reset", "hn", "pre", "tan", "diff", "prod", "g_done", "out_mm", "sum_done"))
        feats = "(k p) n -> p k n"

        with nc.Block() as block:
            @block.sync
            def _(sp):
                sp.dma_start(raw[:, :, :], a["w_ihT"].rearrange(feats, p=P)).then_inc(w_in[0], 16)
                sp.dma_start(rel[:, :], a["rel"]).then_inc(c_in, 16)
                sp.dma_start(col[:, :], a["gru_cols"]).then_inc(c_in, 16)
                sp.dma_start(gate_b[:, :], a["gru_gate_cols"]).then_inc(c_in, 16)
                sp.dma_start(xT[0][:, :, :], d["xnT"][0]).then_inc(xT_in[0], 16)
                sp.dma_start(mid[0][:, :, :], rows(d["mid"], 0)).then_inc(mid_in[0], 16)
                sp.wait_ge(w_split, 1)
                sp.dma_start(raw[:, :, :], a["w_hhT"].rearrange(feats, p=P)).then_inc(w_in[1], 16)

                def group(g, u, i, more):
                    if more:
                        wait(sp, g_done, KT * g)
                        sp.dma_start(xT[1 - u][:, :, :], d["xnT"][g + 1]).then_inc(xT_in[1 - u], 16)
                        wait(sp, stored[1 - u], 16 * i if u == 0 else 16 * (i + 1))
                        sp.dma_start(mid[1 - u][:, :, :], rows(d["mid"], g + 1)
                                     ).then_inc(mid_in[1 - u], 16)
                    sp.wait_ge(sum_done, g + 1)
                    sp.dma_start(rows(d["all"], g), mid[u][:, :, :]).then_inc(stored[u], 16)

                each_group(sp, group)
                for u in range(2):
                    sp.wait_ge(stored[u], 16 * (PAIRS + 1 - u))

            @block.tensor
            def _(pe):
                pe.wait_ge(c_in, 48)
                pe.wait_ge(w_split, 2)

                def messages(g):
                    pe.wait_ge(copied, g + 1)
                    wait(pe, sum_done, g - 1)
                    for j in range(TPG):
                        ins = pe.transpose(p_relT[:, j * P:(j + 1) * P], relc[:, j, :],
                                           keep["ident"][:, :])
                    ins.then_inc(relT_mm, 1)
                    pe.wait_ge(relT_done, g + 1)
                    wait(pe, r_low, KT * g)
                    for b in range(KT):
                        pe.matmul(p_red[:, b, :], rel[:, b * P:(b + 1) * P], relT[:, :],
                                  start=True, stop=False)
                        for j in range(TPG):
                            ins = pe.matmul(p_red[:, b, j * P:(j + 1) * P],
                                            red[:, j, b * P:(b + 1) * P], keep["ident"][:, :],
                                            start=False, stop=(j == TPG - 1))
                    ins.then_inc(red_mm, 1)

                def group(g, u, i, more):
                    if isinstance(g, int) and g == 0:
                        messages(0)
                    pe.wait_ge(x_low, KT * (g + 1))
                    pe.wait_ge(r_low, KT * (g + 1))
                    for b in range(KT):
                        def products(gate, sides, col0):
                            n = 0
                            last = len(sides) * KT * 3
                            for s in sides:
                                hi, lo = ((r_hi, r_lo), (x_hi, x_lo))[s]
                                for k in range(KT):
                                    for wt, act_ in ((w_hi[s], hi), (w_hi[s], lo), (w_lo[s], hi)):
                                        ins = pe.matmul(p_gate[gate][:, :],
                                                        wt[:, k, col0 + b * P:col0 + (b + 1) * P],
                                                        act_[:, k, :], start=(n == 0), stop=(n == last - 1))
                                        n += 1
                            ins.then_inc(gates, 1)
                        item = KT * g + b
                        wait(pe, reset, 2 * item)
                        wait(pe, pre, item)
                        products(0, (1, 0), 0)
                        products(3, (1,), 2 * D)
                        products(2, (0,), 2 * D)
                        products(1, (1, 0), D)
                    if more:
                        messages(g + 1)
                    pe.wait_ge(g_done, KT * (g + 1))
                    for j in range(TPG):
                        for b in range(KT):
                            ins = pe.transpose(p_out[:, j, b * P:(b + 1) * P],
                                               gT[:, b, j * P:(j + 1) * P], keep["ident"][:, :])
                    ins.then_inc(out_mm, 1)

                each_group(pe, group)

            @block.scalar
            def _(act):
                for s in range(2):
                    act.wait_ge(w_in[s], 16)
                    act.activation(w_hi[s][:, :, :], raw[:, :, :], ACT.Copy).then_inc(w_high, 1)

                act.wait_ge(bias_sum, 1)

                def take(g, u, i):
                    wait(act, red_mm, g)
                    act.activation(red[:, :, :], keep["red"][:, bass.ds(g * TPG, TPG), 0:D], ACT.Copy,
                                   scale=1.0 / PAIR)
                    act.activation(relc[:, :, :], keep["red"][:, bass.ds(g * TPG, TPG), D:RW],
                                   ACT.Copy).then_inc(copied, 1)
                    act.wait_ge(relT_mm, g + 1)
                    act.activation(relT[:, :], p_relT, ACT.Copy).then_inc(relT_done, 1)

                def halves(g, u, i):
                    act.wait_ge(xT_in[u], 16 * (i + 1))
                    wait(act, gates, 4 * KT * g)
                    act.activation(x_hi[:, :, :], xT[u][:, :, :], ACT.Copy).then_inc(high, 1)
                    act.wait_ge(red_mm, g + 1)
                    for b in range(KT):
                        act.activation(r_hi[:, b, :], p_red[:, b, :], ACT.Copy).then_inc(r_high, 1)

                def group(g, u, i, more):
                    if isinstance(g, int) and g == 0:
                        take(0, 0, 0)
                    halves(g, u, i)
                    for b in range(KT):
                        item = KT * g + b
                        act.wait_ge(gates, 4 * item + 1)
                        wait(act, hn, item)
                        act.activation(gr[:, :], p_gate[0][:, :], ACT.Sigmoid, bias=gate_b[:, b:b + 1]
                                       ).then_inc(reset, 1)
                        act.wait_ge(gates, 4 * item + 4)
                        wait(act, g_done, item)
                        act.activation(gz[:, :], p_gate[1][:, :], ACT.Sigmoid,
                                       bias=gate_b[:, KT + b:KT + b + 1]).then_inc(reset, 1)
                        act.wait_ge(pre, item + 1)
                        act.activation(gn[:, :], gn[:, :], ACT.Tanh, bias=col[:, 2 * KT + b:2 * KT + b + 1]
                                       ).then_inc(tan, 1)
                    if more:
                        take(g + 1, 1 - u, i)

                each_group(act, group)

            @block.vector
            def _(dve):
                dve.wait_ge(c_in, 48)
                dve.tensor_tensor(gate_b[:, :], gate_b[:, :], col[:, 0:2 * KT], ALU.add
                                  ).then_inc(bias_sum, 1)
                for s in range(2):
                    dve.wait_ge(w_high, s + 1)
                    dve.tensor_tensor(w_lo[s][:, :, :], raw[:, :, :], w_hi[s][:, :, :].bitcast(F32),
                                      ALU.subtract).then_inc(w_split, 1)

                def group(g, u, i, more):
                    dve.wait_ge(high, g + 1)
                    wait(dve, gates, 4 * KT * g)
                    for b in range(KT):
                        dve.tensor_tensor(x_lo[:, b, :], xT[u][:, b, :], x_hi[:, b, :].bitcast(F32),
                                          ALU.subtract).then_inc(x_low, 1)
                    for b in range(KT):
                        dve.wait_ge(r_high, KT * g + b + 1)
                        dve.tensor_tensor(r_lo[:, b, :], p_red[:, b, :], r_hi[:, b, :].bitcast(F32),
                                          ALU.subtract).then_inc(r_low, 1)
                    for b in range(KT):
                        item = KT * g + b
                        dve.wait_ge(gates, 4 * item + 3)
                        dve.wait_ge(reset, 2 * item + 1)
                        wait(dve, g_done, item)
                        dve.scalar_tensor_tensor(gn[:, :], p_gate[3][:, :], col[:, 3 * KT + b:3 * KT + b + 1],
                                                 gr[:, :], ALU.add, ALU.mult).then_inc(hn, 1)
                        dve.wait_ge(hn, item + 1)
                        dve.tensor_tensor(gn[:, :], p_gate[2][:, :], gn[:, :], ALU.add).then_inc(pre, 1)
                        dve.wait_ge(tan, item + 1)
                        wait(dve, out_mm, g)
                        dve.tensor_tensor(gT[:, b, :], xT[u][:, b, :], gn[:, :], ALU.subtract
                                          ).then_inc(diff, 1)
                        dve.wait_ge(diff, item + 1)
                        dve.wait_ge(reset, 2 * item + 2)
                        dve.tensor_tensor(gT[:, b, :], gT[:, b, :], gz[:, :], ALU.mult).then_inc(prod, 1)
                        dve.wait_ge(prod, item + 1)
                        dve.tensor_tensor(gT[:, b, :], gT[:, b, :], gn[:, :], ALU.add).then_inc(g_done, 1)
                    dve.wait_ge(out_mm, g + 1)
                    dve.wait_ge(mid_in[u], 16 * (i + 1))
                    dve.tensor_tensor(mid[u][:, :, :], p_out[:, :, :], mid[u][:, :, :], ALU.add
                                      ).then_inc(sum_done, 1)

                each_group(dve, group)


def experts_phase(nc, a, d, keep):
    with ExitStack() as ctx:
        m = Names(nc, ctx, "moe")
        LAYERS = 3
        hi = [[m.sb(f"w_hi{l}_{e}", [P, KT, D], F32R) for e in range(NE)] for l in range(LAYERS)]
        lo = [[m.sb(f"w_lo{l}_{e}", [P, KT, D], F32R) for e in range(NE)] for l in range(LAYERS)]
        raw = [m.sb(f"raw{r}", [P, KT, D], F32) for r in range(4)]
        wr = m.sb("wr", [P, KT, NE], F32)
        wr_hi, wr_lo = m.sb("wr_hi", [P, KT, NE], F32R), m.sb("wr_lo", [P, KT, NE], F32R)
        br = m.sb("br", [P, NE], F32)
        bo = m.sb("bo", [NE, D], F32)
        bn = m.sb("bn", [P, 5, 2, NE * KT], F32)
        scale, shift = m.sb("scale", [P, 2, NE * KT], F32), m.sb("shift", [P, 2, NE * KT], F32)
        bt = m.sb("bt", [P, 2, NE * KT], F32)
        x3 = [m.sb(f"x3_{u}", [P, TPG, D], F32) for u in range(2)]
        f = m.sb("f", [P, TPG, D], F32)
        f_hi = [m.sb(f"f_hi{u}", [P, KT, G], F32R) for u in range(2)]
        f_lo = [m.sb(f"f_lo{u}", [P, KT, G], F32R) for u in range(2)]
        act_f = [m.sb(f"act{l}", [P, KT, G], F32) for l in range(2)]
        act_hi = [[m.sb(f"act_hi{l}_{r}", [P, KT, G], F32R) for r in range(2)] for l in range(2)]
        act_lo = [[m.sb(f"act_lo{l}_{r}", [P, KT, G], F32R) for r in range(2)] for l in range(2)]
        logit = m.sb("logit", [P, TPG, NE], F32)
        top, tot = m.sb("top", [P, TPG], F32), m.sb("tot", [P, TPG], F32)
        gate = [m.sb(f"gate{u}", [P, TPG, NE], F32) for u in range(2)]
        gateT = m.sb("gateT", [NE, G], F32)
        w = norm_work(m.sb)

        p_h = [[m.ps(f"h{l}_{k}", [P, G]) for k in range(KT)] for l in range(2)]
        p_y = m.ps("y", [P, TPG, D])
        p_f = m.ps("f", [P, KT, G])
        p_logit = p_f[:, 0, 0:TPG * NE].rearrange("p (j e) -> p j e", j=TPG)
        p_gateT = p_f[0:NE, 1, :]

        raw_in = [m.sem(f"raw_in{r}") for r in range(4)]
        c_in = m.sem("c_in")
        w_high, w_low, prep = m.sem("w_high"), m.sem("w_low"), m.sem("prep")
        x_in = [m.sem(f"x_in{u}") for u in range(2)]
        stored = [m.sem(f"stored{u}") for u in range(2)]
        (normed, f_mm, f_high, f_low, logit_mm, softmax, expd, gateT_mm, gateT_done, bias_mm,
         acc_done, y_mm) = (m.sem(n) for n in (
             "normed", "f_mm", "f_high", "f_low", "logit_mm", "softmax", "expd", "gateT_mm",
             "gateT_done", "bias_mm", "acc_done", "y_mm"))
        h_mm = [m.sem(f"h_mm{l}") for l in range(2)]
        h_act = [m.sem(f"h_act{l}") for l in range(2)]
        h_low = [m.sem(f"h_low{l}") for l in range(2)]
        softmax_in, normed_w = m.sem("softmax_in"), m.sem("normed_w")
        SOFTMAX = 5
        ACC = 1 + NE
        n_w = LAYERS * NE

        with nc.Block() as block:
            @block.sync
            def _(sp):
                for t, src in ((wr[:, :, :], a["w_router"].rearrange("(k p) n -> p k n", p=P)),
                               (br[:, :], a["b_router"].partition_broadcast(P)),
                               (bo[:, :], a["b_out"]),
                               (bn[:, :, :, :], a["bn_cols"])):
                    sp.dma_start(t, src).then_inc(c_in, 16)
                for n in range(n_w):
                    wait(sp, w_low, n - 3)
                    sp.dma_start(raw[n % 4][:, :, :], a["w_experts"][n % LAYERS, n // LAYERS]
                                 ).then_inc(raw_in[n % 4], 16)
                    if n == 3:
                        sp.dma_start(x3[0][:, :, :], rows(d["all"], 0)).then_inc(x_in[0], 16)

                def group(g, u, i, more):
                    if more:
                        wait(sp, stored[1 - u], 16 * i if u == 0 else 16 * (i + 1))
                        sp.dma_start(x3[1 - u][:, :, :], rows(d["all"], g + 1)
                                     ).then_inc(x_in[1 - u], 16)
                    sp.wait_ge(acc_done, ACC * (g + 1))
                    sp.dma_start(rows(a["out"], g), x3[u][:, :, :]).then_inc(stored[u], 16)

                each_group(sp, group)
                for u in range(2):
                    sp.wait_ge(stored[u], 16 * (PAIRS + 1 - u))

            @block.tensor
            def _(pe):
                def passes(out, wt, act, first, last):
                    for n, (p, q) in enumerate(((wt[0], act[0]), (wt[0], act[1]), (wt[1], act[0]))):
                        ins = pe.matmul(out, p, q, start=(first and n == 0), stop=(last and n == 2))
                    return ins

                def turn(g, u):
                    pe.wait_ge(normed, NORM_OPS * (g + 1))
                    wait(pe, gateT_done, g)
                    for k in range(KT):
                        for j in range(TPG):
                            ins = pe.transpose(p_f[:, k, j * P:(j + 1) * P], f[:, j, k * P:(k + 1) * P],
                                               keep["ident"][:, :])
                    ins.then_inc(f_mm, 1)

                def route(g, u):
                    pe.wait_ge(f_low, KT * (g + 1))
                    for j in range(TPG):
                        for k in range(KT):
                            t = slice(j * P, (j + 1) * P)
                            ins = passes(p_logit[:, j, :], (f_hi[u][:, k, t], f_lo[u][:, k, t]),
                                         (wr_hi[:, k, :], wr_lo[:, k, :]), k == 0, k == KT - 1)
                    ins.then_inc(logit_mm, 1)

                def turn_gates(g, u):
                    pe.wait_ge(softmax, SOFTMAX * (g + 1))
                    for j in range(TPG):
                        ins = pe.transpose(p_gateT[:, j * P:(j + 1) * P], gate[u][:, j, :],
                                           keep["ident"][:, :])
                    ins.then_inc(gateT_mm, 1)

                def biases(g):
                    pe.wait_ge(gateT_done, g + 1)
                    wait(pe, acc_done, ACC * g)
                    for j in range(TPG):
                        ins = pe.matmul(p_y[:, j, :], gateT[:, j * P:(j + 1) * P], bo[:, :],
                                        start=True, stop=True)
                    ins.then_inc(bias_mm, 1)

                def layer1(g, u, e):
                    n = NE * g + e
                    wait(pe, h_act[0], KT * n)
                    for b in range(KT):
                        c = slice(b * P, (b + 1) * P)
                        for k in range(KT):
                            ins = passes(p_h[0][b][:, :], (hi[0][e][:, k, c], lo[0][e][:, k, c]),
                                         (f_hi[u][:, k, :], f_lo[u][:, k, :]), k == 0, k == KT - 1)
                        ins.then_inc(h_mm[0], 1)

                def layer2(g, e):
                    n = NE * g + e
                    pe.wait_ge(h_low[0], KT * (n + 1))
                    wait(pe, h_act[1], KT * n)
                    for b in range(KT):
                        c = slice(b * P, (b + 1) * P)
                        for k in range(KT):
                            ins = passes(p_h[1][b][:, :], (hi[1][e][:, k, c], lo[1][e][:, k, c]),
                                         (act_hi[0][e % 2][:, k, :], act_lo[0][e % 2][:, k, :]),
                                         k == 0, k == KT - 1)
                        ins.then_inc(h_mm[1], 1)

                def layer3(g, e):
                    n = NE * g + e
                    pe.wait_ge(h_low[1], KT * (n + 1))
                    pe.wait_ge(acc_done, ACC * g + 1 + e)
                    for j in range(TPG):
                        t = slice(j * P, (j + 1) * P)
                        for k in range(KT):
                            ins = passes(p_y[:, j, :], (act_hi[1][e % 2][:, k, t], act_lo[1][e % 2][:, k, t]),
                                         (hi[2][e][:, k, :], lo[2][e][:, k, :]), k == 0, k == KT - 1)
                    ins.then_inc(y_mm, 1)

                pe.wait_ge(w_low, n_w)
                pe.wait_ge(prep, 2)
                turn(0, 0)
                pe.wait_ge(f_low, KT)
                layer1(0, 0, 0)
                route(0, 0)
                layer1(0, 0, 1)
                turn_gates(0, 0)
                layer2(0, 0)

                def group(g, u, i, more):
                    for e in range(NE):
                        if e < NE - 2:
                            layer1(g, u, e + 2)
                        elif more:
                            layer1(g + 1, 1 - u, e + 2 - NE)
                        if e < NE - 1:
                            layer2(g, e + 1)
                        elif more:
                            layer2(g + 1, 0)
                        if e == 0:
                            biases(g)
                        layer3(g, e)
                        if more and e == 2:
                            turn(g + 1, 1 - u)
                        if more and e == 3:
                            route(g + 1, 1 - u)
                        if more and e == 5:
                            turn_gates(g + 1, 1 - u)

                each_group(pe, group)

            @block.scalar
            def _(act):
                for n in range(n_w):
                    act.wait_ge(raw_in[n % 4], 16 * (n // 4 + 1))
                    act.activation(hi[n % LAYERS][n // LAYERS][:, :, :], raw[n % 4][:, :, :], ACT.Copy
                                   ).then_inc(w_high, 1)
                act.wait_ge(c_in, 64)
                act.activation(wr_hi[:, :, :], wr[:, :, :], ACT.Copy).then_inc(w_high, 1)

                def take_f(g, u):
                    act.wait_ge(f_mm, g + 1)
                    if isinstance(g, int) is False or g >= 1:
                        wait(act, h_mm[0], KT * NE * (g - 1))
                    for k in range(KT):
                        act.activation(f_hi[u][:, k, :], p_f[:, k, :], ACT.Copy).then_inc(f_high, 1)

                def exponent(g, u):
                    act.wait_ge(softmax, SOFTMAX * g + 2)
                    act.activation(logit[:, :, :], logit[:, :, :], ACT.Exp).then_inc(expd, 1)

                def take_gates(g):
                    act.wait_ge(gateT_mm, g + 1)
                    wait(act, bias_mm, g)
                    act.activation(gateT[:, :], p_gateT, ACT.Copy).then_inc(gateT_done, 1)

                def layer(l, g, e):
                    n = NE * g + e
                    reader = (h_mm[1], y_mm)[l]
                    wait(act, reader, KT * (n - 1) if l == 0 else n - 1)
                    for b in range(KT):
                        act.wait_ge(h_mm[l], KT * n + b + 1)
                        wait(act, h_low[l], KT * (n - 1) + b + 1)
                        c = e * KT + b
                        for t in (act_f[l], act_hi[l][e % 2]):
                            ins = act.activation(t[:, b, :], p_h[l][b][:, :], ACT.Relu,
                                                 scale=scale[:, l, c:c + 1], bias=shift[:, l, c:c + 1])
                        ins.then_inc(h_act[l], 1)

                act.wait_ge(prep, 2)
                take_f(0, 0)
                layer(0, 0, 0)
                exponent(0, 0)
                layer(0, 0, 1)
                take_gates(0)
                layer(1, 0, 0)

                def group(g, u, i, more):
                    for e in range(NE):
                        if e < NE - 2:
                            layer(0, g, e + 2)
                        elif more:
                            layer(0, g + 1, e + 2 - NE)
                        if e < NE - 1:
                            layer(1, g, e + 1)
                        elif more:
                            layer(1, g + 1, 0)
                        if more and e == 2:
                            take_f(g + 1, 1 - u)
                        if more and e == 3:
                            exponent(g + 1, 1 - u)
                        if more and e == 5:
                            take_gates(g + 1)

                each_group(act, group)

            @block.vector
            def _(dve):
                dve.wait_ge(c_in, 64)
                b_, g_, be, mean, var = (bn[:, c, :, :] for c in range(5))
                dve.tensor_scalar(var, var, BN_EPS, None, ALU.add).then_inc(normed_w, 1)
                rsqrt(dve, scale[:, :, :], var, bt[:, :, :], normed_w, 1)
                k = 1 + RSQRT_OPS
                dve.wait_ge(normed_w, k)
                dve.tensor_tensor(scale[:, :, :], scale[:, :, :], g_, ALU.mult).then_inc(normed_w, 1)
                dve.tensor_tensor(shift[:, :, :], b_, mean, ALU.subtract).then_inc(normed_w, 1)
                dve.wait_ge(normed_w, k + 2)
                dve.tensor_tensor(shift[:, :, :], shift[:, :, :], scale[:, :, :], ALU.mult
                                  ).then_inc(normed_w, 1)
                dve.wait_ge(normed_w, k + 3)
                dve.tensor_tensor(shift[:, :, :], shift[:, :, :], be, ALU.add).then_inc(prep, 1)
                for n in range(n_w):
                    dve.wait_ge(w_high, n + 1)
                    dve.tensor_tensor(lo[n % LAYERS][n // LAYERS][:, :, :], raw[n % 4][:, :, :],
                                      hi[n % LAYERS][n // LAYERS][:, :, :].bitcast(F32), ALU.subtract
                                      ).then_inc(w_low, 1)
                dve.wait_ge(w_high, n_w + 1)
                dve.tensor_tensor(wr_lo[:, :, :], wr[:, :, :], wr_hi[:, :, :].bitcast(F32), ALU.subtract
                                  ).then_inc(prep, 1)

                def norm(g, u, i):
                    dve.wait_ge(x_in[u], 16 * (i + 1))
                    wait(dve, f_mm, g)
                    norm_rows(dve, f, x3[u], w, normed, NORM_OPS * g)

                def low_f(g, u):
                    for k in range(KT):
                        dve.wait_ge(f_high, KT * g + k + 1)
                        dve.tensor_tensor(f_lo[u][:, k, :], p_f[:, k, :], f_hi[u][:, k, :].bitcast(F32),
                                          ALU.subtract).then_inc(f_low, 1)

                def softmax_a(g):
                    base = SOFTMAX * g
                    dve.wait_ge(logit_mm, g + 1)
                    wait(dve, softmax, base)
                    dve.tensor_tensor(logit[:, :, :], p_logit, across(br[:, :], TPG), ALU.add
                                      ).then_inc(softmax_in, 1)
                    dve.wait_ge(softmax_in, g + 1)
                    dve.tensor_reduce(top[:, :], logit[:, :, :], AX.X, ALU.max).then_inc(softmax, 1)
                    dve.wait_ge(softmax, base + 1)
                    dve.tensor_tensor(logit[:, :, :], logit[:, :, :],
                                      top[:, :].unsqueeze(2).broadcast_to([P, TPG, NE]), ALU.subtract
                                      ).then_inc(softmax, 1)

                def softmax_b(g, u):
                    base = SOFTMAX * g
                    dve.wait_ge(expd, g + 1)
                    dve.tensor_reduce(tot[:, :], logit[:, :, :], AX.X, ALU.add).then_inc(softmax, 1)
                    dve.wait_ge(softmax, base + 3)
                    dve.reciprocal(tot[:, :], tot[:, :]).then_inc(softmax, 1)
                    dve.wait_ge(softmax, base + 4)
                    dve.tensor_tensor(gate[u][:, :, :], logit[:, :, :],
                                      tot[:, :].unsqueeze(2).broadcast_to([P, TPG, NE]), ALU.mult
                                      ).then_inc(softmax, 1)

                def low(l, g, e):
                    n = NE * g + e
                    for b in range(KT):
                        dve.wait_ge(h_act[l], KT * n + b + 1)
                        dve.tensor_tensor(act_lo[l][e % 2][:, b, :], act_f[l][:, b, :],
                                          act_hi[l][e % 2][:, b, :].bitcast(F32), ALU.subtract
                                          ).then_inc(h_low[l], 1)

                def sum_biases(g, u):
                    dve.wait_ge(bias_mm, g + 1)
                    dve.tensor_tensor(x3[u][:, :, :], p_y[:, :, :], x3[u][:, :, :], ALU.add
                                      ).then_inc(acc_done, 1)

                def sum_expert(g, u, e):
                    dve.wait_ge(y_mm, NE * g + e + 1)
                    dve.wait_ge(acc_done, ACC * g + 1 + e)
                    for j in range(TPG):
                        ins = dve.scalar_tensor_tensor(x3[u][:, j, :], p_y[:, j, :],
                                                       gate[u][:, j, e:e + 1], x3[u][:, j, :],
                                                       ALU.mult, ALU.add)
                    ins.then_inc(acc_done, 1)

                norm(0, 0, 0)
                low_f(0, 0)
                low(0, 0, 0)
                softmax_a(0)
                softmax_b(0, 0)
                low(0, 0, 1)
                low(1, 0, 0)

                def group(g, u, i, more):
                    for e in range(NE):
                        if e < NE - 2:
                            low(0, g, e + 2)
                        elif more:
                            low(0, g + 1, e + 2 - NE)
                        if e < NE - 1:
                            low(1, g, e + 1)
                        elif more:
                            low(1, g + 1, 0)
                        if e == 0:
                            sum_biases(g, u)
                        sum_expert(g, u, e)
                        if more and e == 1:
                            norm(g + 1, 1 - u, i if u == 0 else i + 1)
                        if more and e == 2:
                            low_f(g + 1, 1 - u)
                        if more and e == 3:
                            softmax_a(g + 1)
                            softmax_b(g + 1, 1 - u)

                each_group(dve, group)


def build(nc, a):
    d = {"xn": nc.dram_tensor("xn_rows", (NP, D), F32).ap(),
         "xnT": nc.dram_tensor("xn_turned", (GROUPS + 1, P, KT, G), F32).ap(),
         "pairs": nc.dram_tensor("xn_pairs", (NP, 2 * D), F16).ap(),
         "mid": nc.dram_tensor("mid_rows", (NP, D), F32).ap(),
         "all": nc.dram_tensor("all_rows", (NP, D), F32).ap()}
    with ExitStack() as ctx:
        keep = {}
        m = Names(nc, ctx, "keep")
        keep["ident"] = m.sb("ident", [P, P], F32)
        with ExitStack() as sums:
            s = Names(nc, sums, "keep")
            keep["iota"] = s.sb("iota", [P, P], F32)
            keep["base"] = s.sb("base", [P, TILES], F32)
            keep["first"] = s.sb("first", [P, SUPER], I32)
            keep["count"] = s.sb("count", [P, SUPER], I32)
            keep["red"] = s.sb("red", [P, TILES, RW], F32)
            norm_phase(nc, a, d, keep)
            mix_phase(nc, a, d, keep)
            gru_phase(nc, a, d, keep)
        experts_phase(nc, a, d, keep)


def kernel(x, src, dst, edge_type_16, **w):
    import numpy as np

    import concourse.bacc as bacc
    from concourse.bass_utils import run_bass_kernel_spmd

    def get(name):
        return np.asarray(w[name])

    def columns(v):
        v = np.asarray(v)
        return v.reshape(-1, P).T

    xp = np.zeros((NP, D), np.float32)
    xp[:N] = np.asarray(x)
    edges = np.zeros((3, EP), np.int32)
    edges[1, :] = N
    for k, v in enumerate((src, dst, edge_type_16)):
        edges[k, :E] = np.asarray(v)
    by_super = np.ascontiguousarray(edges.reshape(3, SUPER, SC, P).transpose(1, 3, 0, 2))
    M, F, R = "L0_mix_", "L0_ffn_", "L0_gnn_"
    b_ih, b_hh = get(R + "b_ih"), get(R + "b_hh")
    arrays = {
        "x": xp,
        "edges": by_super,
        "dst_by_super": np.ascontiguousarray(by_super[:, :, 1, :].transpose(1, 0, 2)),
        "identity": np.eye(P, dtype=np.float32),
        "iota": np.arange(P, dtype=np.float32),
        "tile_base": np.arange(TILES, dtype=np.float32) * P,
        "w_kv": np.concatenate([get(M + "Wk"), get(M + "Wv")], axis=1),
        "b_kv": np.concatenate([get(M + "bk"), get(M + "bv")]),
        "w_q": get(M + "Wq"), "w_o": get(M + "Wo"), "w_ff1": get(M + "W1"), "w_ff2": get(M + "W2"),
        "rows5": np.stack([get(M + n) for n in ("bo", "ln1_b", "b2", "ln2_g", "ln2_b")]),
        "ln1_g": get(M + "ln1_g"),
        "mix_cols": np.concatenate([columns(get(M + n)) for n in ("bq", "ln1_g", "ln1_b", "b1")], axis=1),
        "w_ihT": np.ascontiguousarray(get(R + "w_ih").T),
        "w_hhT": np.ascontiguousarray(get(R + "w_hh").T),
        "rel": get(R + "relvectors"),
        "gru_cols": np.concatenate([columns(b_ih), columns(b_hh[2 * D:])], axis=1),
        "gru_gate_cols": columns(b_hh[:2 * D]),
        "w_router": get(F + "Wr"), "b_router": get(F + "br"), "b_out": get(F + "bo"),
        "w_experts": np.stack([get(F + n).reshape(NE, KT, P, D).transpose(0, 2, 1, 3)
                               for n in ("W1", "W2", "Wo")]),
        "bn_cols": np.stack([np.stack([columns(get(F + n + l)) for l in "12"], axis=1)
                             for n in ("b", "g", "be", "m", "v")], axis=1),
    }
    arrays = {k: np.ascontiguousarray(v) for k, v in arrays.items()}
    nc = bacc.Bacc("TRN2", target_bir_lowering=False, num_devices=1)
    aps = {k: nc.dram_tensor(f"in_{k}", v.shape, mybir.dt.from_np(v.dtype), kind="ExternalInput").ap()
           for k, v in arrays.items()}
    aps["out"] = nc.dram_tensor("out", (NP, D), F32, kind="ExternalOutput").ap()
    build(nc, aps)
    res = run_bass_kernel_spmd(nc, [{f"in_{k}": v for k, v in arrays.items()}], core_ids=[0])
    return res.results[0]["out"][:N]
```

```python
from contextlib import ExitStack

import concourse.bass as bass
from concourse import mybir

ALU = mybir.AluOpType
ACT = mybir.ActivationFunctionType
AX = mybir.AxisListType
F32 = mybir.dt.float32
F32R = mybir.dt.float32r
F16 = mybir.dt.float16
I32 = mybir.dt.int32

P = 128
N, D = 12500, 256
KT = D // P
TPG = 4
G = TPG * P
GROUPS = -(-N // G)
PAIRS = GROUPS // 2
NP = GROUPS * G
TILES = NP // P
E = 200000
SC = 4
RING = 4
SA, SB = 2, 14
SUPER = GROUPS * (SA + SB)
EP = SUPER * SC * P
FILLED = -(-E // (SC * P))
RELS = 16
FF = 1024
FT = FF // P
HD = 32
HPT = P // HD
NE = 8
LN_EPS = 1e-5
BN_EPS = 1e-3
DEN_EPS = 1e-6
PAIR = 2048.0
RT = N // P + 1
RW = D + RELS
MW = 2 * D + RELS
VALID = N - (GROUPS - 1) * G
NEWTON = 3
RSQRT_OPS = 1 + 3 * NEWTON
NORM_OPS = 4 + RSQRT_OPS + 1
STAT_OPS = 4 + RSQRT_OPS + 1

assert VALID <= (TPG - 1) * P and TPG == 4
assert FILLED > GROUPS * SA + (GROUPS - 1) * SB and FILLED < SUPER
assert GROUPS % 2 == 1 and EP >= E and TILES <= P
assert 2 * SA % RING == 0 and 2 * SB % RING == 0 and SB == 10 + TPG


def wait(eng, sem, value):
    if not isinstance(value, int) or value > 0:
        eng.wait_ge(sem, value)


def each_group(eng, group):
    group(0, 0, 0, True)
    group(1, 1, 0, True)
    with eng.Fori(1, PAIRS) as i:
        group(i * 2, 0, i, True)
        group(i * 2 + 1, 1, i, True)
    group(GROUPS - 1, 0, PAIRS, False)


def rsqrt(dve, y, v, t, done, base):
    dve.wait_ge(done, base)
    dve.tensor_scalar(y.bitcast(I32), v.bitcast(I32), -0.5, 1597463007.0,
                      ALU.mult, ALU.add).then_inc(done, 1)
    k = base + 1
    for _ in range(NEWTON):
        dve.wait_ge(done, k)
        dve.scalar_tensor_tensor(t, y, -0.5, y, ALU.mult, ALU.mult).then_inc(done, 1)
        dve.wait_ge(done, k + 1)
        dve.tensor_tensor(t, t, v, ALU.mult).then_inc(done, 1)
        dve.wait_ge(done, k + 2)
        dve.scalar_tensor_tensor(y, t, 1.5, y, ALU.add, ALU.mult).then_inc(done, 1)
        k = k + 3


def norm_stats(dve, x, w, done, base):
    norm_moments(dve, x, w, done, base)
    norm_factors(dve, w, done, base)


def norm_factors(dve, w, done, base):
    norm_rstd(dve, w, done, base)
    dve.wait_ge(done, base + STAT_OPS - 1)
    dve.scalar_tensor_tensor(w["nb"][:, :], w["mv"][:, :, 0], -1.0, w["rs"][:, :],
                             ALU.mult, ALU.mult).then_inc(done, 1)


def norm_rows(dve, out, x, w, done, base):
    norm_scale(dve, x, w, done, base)
    dve.wait_ge(done, base + 4 + RSQRT_OPS)
    for j in range(TPG):
        ins = dve.tensor_scalar(out[:, j, :], x[:, j, :], w["mv"][:, j, 0:1], w["rs"][:, j:j + 1],
                                ALU.subtract, ALU.mult)
    ins.then_inc(done, 1)


def norm_scale(dve, x, w, done, base):
    norm_moments(dve, x, w, done, base)
    norm_rstd(dve, w, done, base)


def norm_moments(dve, x, w, done, base):
    for j in range(TPG):
        ins = dve.bn_stats(w["st"][:, j, :], x[:, j, :])
    ins.then_inc(done, 1)
    dve.wait_ge(done, base + 1)
    dve.sem_inc(done, 1)
    for j in range(TPG):
        ins = dve.bn_aggr(w["mv"][:, j, :], w["st"][:, j, :])
    ins.then_inc(done, 1)


def norm_rstd(dve, w, done, base):
    dve.wait_ge(done, base + 3)
    dve.tensor_scalar(w["ve"][:, :], w["mv"][:, :, 1], LN_EPS, None, ALU.add).then_inc(done, 1)
    rsqrt(dve, w["rs"][:, :], w["ve"][:, :], w["tt"][:, :], done, base + 4)


def norm_work(sb, name=""):
    return {"st": sb(name + "stats", [P, TPG, 6], F32), "mv": sb(name + "mean_var", [P, TPG, 2], F32),
            "ve": sb(name + "var_eps", [P, TPG], F32), "rs": sb(name + "rstd", [P, TPG], F32),
            "tt": sb(name + "newton", [P, TPG], F32), "nb": sb(name + "mean_rstd", [P, TPG], F32)}


def rows(ap, g):
    return ap.rearrange("(g j p) d -> g p j d", j=TPG, p=P)[g]


def across(ap, n):
    return ap.unsqueeze(1).broadcast_to([ap.shape[0], n, ap.shape[1]])


class Names:

    def __init__(self, nc, ctx, phase):
        self.nc, self.ctx, self.phase = nc, ctx, phase

    def sb(self, name, shape, dt):
        return self.ctx.enter_context(self.nc.sbuf_tensor(f"{self.phase}_{name}", shape, dt))

    def ps(self, name, shape):
        return self.ctx.enter_context(self.nc.psum_tensor(f"{self.phase}_ps_{name}", shape, F32))

    def sem(self, name):
        return self.ctx.enter_context(self.nc.semaphore(f"{self.phase}_{name}"))


MIX_LOADS = 10


def mix_weights(nc, ctx, keep):
    m = Names(nc, ctx, "mix")
    keep["mix_w_in"] = m.sem("w_in")
    keep["mix_w"] = {n: m.sb(n, shape, F32) for n, shape in (
        ("wkv", [P, KT, 2 * D]), ("wq", [P, KT, D]), ("wo", [P, KT, D]), ("w1", [P, KT, FF]),
        ("w2", [P, FT, D]), ("bkv", [P, 2 * D]), ("row5", [P, 5, D]),
        ("col", [P, 3 * KT + FT]))}


def load_mix_weights(eng, a, keep):
    feats = "(k p) n -> p k n"
    t = keep["mix_w"]
    loads = ((t["wkv"][:, :, :], a["w_kv"].rearrange(feats, p=P)),
             (t["bkv"][:, :], a["b_kv"].partition_broadcast(P)),
             (keep["iota"][:, :], a["iota"].partition_broadcast(P)),
             (keep["base"][:, :], a["tile_base"].partition_broadcast(P)),
             (t["wq"][:, :, :], a["w_q"].rearrange(feats, p=P)),
             (t["wo"][:, :, :], a["w_o"].rearrange(feats, p=P)),
             (t["w1"][:, :, :], a["w_ff1"].rearrange(feats, p=P)),
             (t["w2"][:, :, :], a["w_ff2"].rearrange(feats, p=P)),
             (t["row5"][:, :, :], a["mix_rows"].partition_broadcast(P)),
             (t["col"][:, :], a["mix_cols"]))
    assert len(loads) == MIX_LOADS
    for to, src in loads:
        eng.dma_start(to, src).then_inc(keep["mix_w_in"], 16)


def norm_phase(nc, a, d, keep):
    with ExitStack() as ctx:
        m = Names(nc, ctx, "norm")
        x = [m.sb(f"x{u}", [P, TPG, D], F32) for u in range(2)]
        xn = [m.sb(f"xn{u}", [P, TPG, D], F32) for u in range(2)]
        pair = [m.sb(f"pair{u}", [P, TPG, 2, D], F16) for u in range(2)]
        xT = [m.sb(f"xT{u}", [P, KT, G], F32) for u in range(2)]
        w = [norm_work(m.sb, f"{u}_") for u in range(2)]
        dst = m.sb("dst", [P, SUPER, SC], I32)
        ends = m.sb("ends", [P, 2, SUPER], F32)
        ends_all = m.sb("ends_all", [P, 2, SUPER], F32)
        psT = [m.ps(f"T{u}", [P, KT, G]) for u in range(2)]

        x_in = [m.sem(f"x_in{u}") for u in range(2)]
        const_in = m.sem("const_in")
        ends_done = m.sem("ends_done")
        reduced = m.sem("reduced")
        stats = m.sem("stats")
        normed = m.sem("normed")
        high_done = m.sem("high_done")
        low_done = m.sem("low_done")
        turned = m.sem("turned")
        xT_done = m.sem("xT_done")
        rows_out = [m.sem(f"rows_out{u}") for u in range(2)]
        pair_out = [m.sem(f"pair_out{u}") for u in range(2)]
        xT_out = [m.sem(f"xT_out{u}") for u in range(2)]

        with nc.Block() as block:
            @block.sync
            def _(sp):
                sp.dma_start(x[0][:, :, :], rows(a["x"], 0)).then_inc(x_in[0], 16)
                sp.dma_start(keep["ident"][:, :], a["identity"]).then_inc(const_in, 16)
                sp.dma_start(dst[:, :, :], a["dst_by_super"]).then_inc(const_in, 16)

                def group(g, u, i, more):
                    if more:
                        wait(sp, normed, g)
                        sp.dma_start(x[1 - u][:, :, :], rows(a["x"], g + 1)).then_inc(x_in[1 - u], 16)
                    sp.wait_ge(normed, g + 1)
                    sp.dma_start(rows(d["xn"], g), xn[u][:, :, :]).then_inc(rows_out[u], 16)
                    if not (isinstance(g, int) and g == 0):
                        pairs(g - 1, 1 - u)
                    if not more:
                        pairs(g, u)

                def pairs(g, u):
                    sp.wait_ge(low_done, g + 1)
                    sp.dma_start(rows(d["pairs"], g), pair[u][:, :, :, :].rearrange("p j h d -> p j (h d)")
                                 ).then_inc(pair_out[u], 16)

                each_group(sp, group)
                for u in range(2):
                    for out in (rows_out[u], pair_out[u], xT_out[u]):
                        sp.wait_ge(out, 16 * (PAIRS + 1 - u))
                sp.dma_start(d["xnT"][GROUPS], xT[0][:, :, :]).then_inc(xT_out[0], 16)
                sp.wait_ge(xT_out[0], 16 * (PAIRS + 2))

            @block.vector
            def _(dve):
                dve.wait_ge(const_in, 32)
                dve.tensor_reduce(ends[:, 0, :], dst[:, :, :], AX.X, ALU.max)
                dve.tensor_reduce(ends[:, 1, :], dst[:, :, :], AX.X, ALU.min, negate=True
                                  ).then_inc(ends_done, 1)

                def group(g, u, i, more):
                    dve.wait_ge(x_in[u], 16 * (i + 1))
                    norm_stats(dve, x[u], w[u], stats, g * STAT_OPS)
                    if isinstance(g, int) and g == 0:
                        return
                    low_half(g - 1, 1 - u)
                    if not more:
                        low_half(g, u)

                def low_half(g, u):
                    dve.wait_ge(high_done, g + 1)
                    dve.scalar_tensor_tensor(pair[u][:, :, 0, :], xn[u][:, :, :], PAIR,
                                             pair[u][:, :, 1, :], ALU.mult, ALU.subtract
                                             ).then_inc(low_done, 1)

                each_group(dve, group)
                dve.wait_ge(reduced, 1)
                dve.tensor_copy(keep["reach"][:, :, 1], ends_all[:, 0, :])
                dve.tensor_scalar(keep["reach"][:, :, 0], ends_all[:, 1, :], -1.0, None, ALU.mult
                                  ).then_inc(ends_done, 1)
                dve.wait_ge(ends_done, 2)
                dve.tensor_scalar(keep["reach"][:, :, 1], keep["reach"][:, :, 1], 7, None,
                                  ALU.logical_shift_right)
                dve.tensor_scalar(keep["reach"][:, :, 0], keep["reach"][:, :, 0], 7, None,
                                  ALU.logical_shift_right).then_inc(ends_done, 1)
                dve.wait_ge(ends_done, 3)
                dve.scalar_tensor_tensor(keep["reach"][:, :, 1], keep["reach"][:, :, 1], 1.0,
                                         keep["reach"][:, :, 0], ALU.add, ALU.subtract
                                         ).then_inc(ends_done, 1)
                dve.wait_ge(ends_done, 4)

            @block.gpsimd
            def _(pool):
                pool.memset(keep["red"][:, :, :], 0.0)
                pool.wait_ge(ends_done, 1)
                pool.partition_all_reduce(ends_all[:, :, :].rearrange("p a s -> p (a s)"),
                                          ends[:, :, :].rearrange("p a s -> p (a s)"), P,
                                          bass.bass_isa.ReduceOp.max).then_inc(reduced, 1)

            @block.tensor
            def _(pe):
                pe.wait_ge(const_in, 32)

                def group(g, u, i, more):
                    pe.wait_ge(normed, g + 1)
                    wait(pe, xT_done, g - 1)
                    for k in range(KT):
                        for j in range(TPG):
                            ins = pe.transpose(psT[u][:, k, j * P:(j + 1) * P],
                                               xn[u][:, j, k * P:(k + 1) * P], keep["ident"][:, :])
                    ins.then_inc(turned, 1)

                each_group(pe, group)

            @block.scalar
            def _(act):
                load_mix_weights(act, a, keep)

                def group(g, u, i, more):
                    act.wait_ge(stats, (g + 1) * STAT_OPS)
                    wait(act, low_done, g - 1)
                    wait(act, rows_out[u], 16 * i)
                    wait(act, turned, g - 1)
                    for j in range(TPG):
                        ins = act.activation(xn[u][:, j, :], x[u][:, j, :], ACT.Identity,
                                             scale=w[u]["rs"][:, j:j + 1], bias=w[u]["nb"][:, j:j + 1])
                    ins.then_inc(normed, 1)
                    act.wait_ge(normed, g + 1)
                    wait(act, pair_out[u], 16 * i)
                    act.activation(pair[u][:, :, 1, :], xn[u][:, :, :], ACT.Copy, scale=PAIR
                                   ).then_inc(high_done, 1)
                    act.wait_ge(turned, g + 1)
                    wait(act, xT_out[u], 16 * i)
                    for k in range(KT):
                        ins = act.activation(xT[u][:, k, :], psT[u][:, k, :], ACT.Copy)
                    ins.then_inc(xT_done, 1)
                    act.wait_ge(xT_done, g + 1)
                    act.dma_start(d["xnT"][g], xT[u][:, :, :]).then_inc(xT_out[u], 16)

                each_group(act, group)


class Super:

    def __init__(self, start, steps, i, k, u, q):
        self.s = i * steps + (start + k)
        self.ring, self.turn = (start + k) % RING, i * (steps // RING) + (start + k) // RING
        self.i, self.u, self.q = i, u, q


def super_a(i, u, q):
    return Super(0, 2 * SA, i, SA * u + q, u, q)


def super_b(i, u, q):
    return Super(GROUPS * SA, 2 * SB, i, SB * u + q, u, q)


def empty(c):
    return isinstance(c.s, int) and c.s >= FILLED


ATT = 1 + STAT_OPS + 2
END = 1 + STAT_OPS + 1


def mix_phase(nc, a, d, keep):
    with ExitStack() as ctx:
        m = Names(nc, ctx, "mix")
        wkv, wq, wo, w1, w2, bkv, row5, col = (keep["mix_w"][n] for n in (
            "wkv", "wq", "wo", "w1", "w2", "bkv", "row5", "col"))
        row_bo, row_n1b, row_b2, row_g2, row_g1 = (row5[:, c, :] for c in range(5))
        row_res = row_n1b
        bq, g1, n1b, b1 = (col[:, 0:KT], col[:, KT:2 * KT], col[:, 2 * KT:3 * KT], col[:, 3 * KT:])
        kvb = m.sb("kvb", [P, KT, P], F32)
        ksb = m.sb("ksb", [P, KT, HPT], F32)
        rec = m.sb("rec", [P, TPG, KT, HPT], F32)
        edge_a = [m.sb(f"edge_a{u}", [P, SA, 3, SC], I32) for u in range(2)]
        edge_b = [m.sb(f"edge_b{u}", [P, SB, 3, SC], I32) for u in range(2)]
        msg = [m.sb(f"msg{r}", [P, SC, MW], F16) for r in range(RING)]
        hot = m.sb("hot", [P, 2, SC, P], F16)
        xT = [m.sb(f"xT{u}", [P, KT, G], F32) for u in range(2)]
        xn = m.sb("xn", [P, TPG, D], F32)
        ex = m.sb("ex", [P, G], F32)
        qphi = m.sb("qphi", [P, KT, G], F32)
        x1T = m.sb("x1T", [P, KT, G], F32)
        h = m.sb("h", [P, FT, G], F32)
        out0 = m.sb("out", [P, TPG, D], F32)
        w, w2nd = norm_work(m.sb), norm_work(m.sb, "2nd_")
        out = [out0[:, :, :], wkv[:, :, :].rearrange("p k (a d) -> p (k a) d", a=2)]
        aT = [bkv[:, :], ex[:, :]]
        attn = qphi[:, :, :].rearrange("p k (a d) -> p (k a) d", a=2)
        kb = [h[:, r, 0:D] for r in (0, 1)]
        va = [h[:, 2 + r, 0:KT * (P + 2)].rearrange("p (b c) -> p b c", b=KT) for r in (0, 1)]
        kex = [h[:, 4 + r, 0:D] for r in (0, 1)]
        kre = [h[:, 4 + r, D:2 * D] for r in (0, 1)]
        kphi = [h[:, 6 + r, 0:D] for r in (0, 1)]
        zero = qphi[:, 0, 0:P]

        pa = [m.ps(f"pa{r}", [P, G]) for r in range(2)]
        pb = m.ps("pb", [P, TPG, D])
        pc = m.ps("pc", [P, TPG, D])
        pbf = pb[:, :, :].rearrange("p (b j) d -> p b (j d)", b=2)
        pcf = pc[:, :, :].rearrange("p (b j) d -> p b (j d)", b=2)
        ring = [pbf[:, 0, :], pbf[:, 1, :], pa[0][:, :], pa[1][:, :]]
        seg = m.ps("seg", [P, 2, 2 * D])
        den = pa[1][:, 0:TPG * KT * HPT].rearrange("p (j b h) -> p j b h", j=TPG, b=KT)
        acc = pcf[:, 0, 0:KT * (P + 2)].rearrange("p (b c) -> p b c", b=KT)

        w_in = keep["mix_w_in"]
        edge_a_in = [m.sem(f"edge_a_in{u}") for u in range(2)]
        edge_b_in = [m.sem(f"edge_b_in{u}") for u in range(2)]
        gathered = [m.sem(f"gathered{r}") for r in range(RING)]
        gather_go = m.sem("gather_go")
        hot_ready = m.sem("hot_ready")
        summed = m.sem("summed")
        added = m.sem("added")
        super_done = m.sem("super_done")
        xT_in = [m.sem(f"xT_in{u}") for u in range(2)]
        xn_in = m.sem("xn_in")
        set_up = m.sem("set_up")
        kv_mm, kv_bias, kv_act, kphi_done, acc_mm = (
            m.sem(n) for n in ("kv_mm", "kv_bias", "kv_act", "kphi_done", "acc_mm"))
        heads_done = m.sem("heads_done")
        q_mm, q_act, qphi_done, nd_mm, rec_done, attn_done, turn_mm, aT_done, wo_mm = (
            m.sem(n) for n in ("q_mm", "q_act", "qphi_done", "nd_mm", "rec_done", "attn_done",
                               "turn_mm", "aT_done", "wo_mm"))
        att_norm, end_norm = m.sem("att_norm"), m.sem("end_norm")
        xn_bo, att, x1_mm, x1T_done, ff1_mm, h_done, ff2_mm, end, stored = (
            m.sem(n) for n in ("xn_bo", "att", "x1_mm", "x1T_done", "ff1_mm", "h_done", "ff2_mm",
                               "end", "stored"))
        N_W = 16 * MIX_LOADS

        with nc.Block() as block:
            @block.sync
            def _(sp):
                def edges_a(g, u):
                    sp.dma_start(edge_a[u][:, :, :, :], a["edges_a"][g]).then_inc(edge_a_in[u], 16)

                def edges_b(g, u):
                    sp.dma_start(edge_b[u][:, :, :, :], a["edges_b"][g]).then_inc(edge_b_in[u], 16)

                edges_a(0, 0)
                edges_b(0, 0)
                sp.dma_start(xT[0][:, :, :], d["xnT"][0]).then_inc(xT_in[0], 16)

                def group_a(g, u, i, more):
                    if more:
                        wait(sp, super_done, SA * g)
                        edges_a(g + 1, 1 - u)
                        wait(sp, kv_mm, TPG * g)
                        sp.dma_start(xT[1 - u][:, :, :], d["xnT"][g + 1]).then_inc(xT_in[1 - u], 16)
                    else:
                        sp.wait_ge(kv_mm, TPG * g)
                        sp.dma_start(xT[1][:, :, :], d["xnT"][0]).then_inc(xT_in[1], 16)
                        sp.dma_start(xn[:, :, :], rows(d["xn"], 0)).then_inc(xn_in, 16)

                each_group(sp, group_a)
                sp.wait_ge(q_mm, KT)
                sp.dma_start(xT[1][:, :, :], d["xnT"][1]).then_inc(xT_in[1], 16)

                def group_b(g, u, i, more):
                    if more:
                        wait(sp, super_done, 0 if isinstance(g, int) and g == 0
                             else g * SB + GROUPS * SA)
                        edges_b(g + 1, 1 - u)
                        sp.wait_ge(att, ATT * (g + 1))
                        sp.wait_ge(x1_mm, g + 1)
                        sp.dma_start(xn[:, :, :], rows(d["xn"], g + 1)).then_inc(xn_in, 16)
                    if not (isinstance(g, int) and g >= GROUPS - 2):
                        sp.wait_ge(q_mm, KT * (g + 2))
                        sp.dma_start(xT[1][:, :, :], d["xnT"][g + 2]).then_inc(xT_in[1], 16)
                    if not (isinstance(g, int) and g == 0):
                        sp.wait_ge(end, END * g)
                        sp.dma_start(rows(d["mid"], g - 1), out[1 - u]).then_inc(stored, 16)

                each_group(sp, group_b)
                sp.wait_ge(xT_in[1], 16 * (PAIRS + GROUPS + 1))
                sp.wait_ge(end, END * GROUPS)
                sp.dma_start(rows(d["mid"], GROUPS - 1), out[0]).then_inc(stored, 16)
                sp.wait_ge(stored, 16 * GROUPS)

            @block.gpsimd
            def _(pool):
                def gather(c, edge, edge_in):
                    if empty(c):
                        return
                    pool.wait_ge(edge_in[c.u], 16 * (c.i + 1))
                    wait(pool, super_done, c.s - (RING - 1))
                    pool.sem_inc(gather_go, 1)
                    for k in range(SC):
                        pool.indirect_dma_start(
                            msg[c.ring][:, k, 0:2 * D], None, d["pairs"],
                            bass.IndirectOffsetOnAxis(edge[c.u][:, c.q, 0, k:k + 1], 0)
                        ).then_inc(gathered[c.ring], 16)

                def group_a(g, u, i, more):
                    for q in range(SA):
                        gather(super_a(i, u, q), edge_a, edge_a_in)

                def group_b(g, u, i, more):
                    for q in range(SB):
                        gather(super_b(i, u, q), edge_b, edge_b_in)

                each_group(pool, group_a)
                each_group(pool, group_b)

            @block.tensor
            def _(pe):
                visit = pe.alloc_register("pe_visit")
                pe.reg_mov(visit, 0)
                pe.sem_inc(summed, 1)

                def segment(c, alone=False):
                    if empty(c):
                        return
                    count = pe.value_load(keep["reach"][0:1, bass.ds(c.s, 1), 1], min_val=1,
                                          max_val=RT)
                    with pe.Fori(0, count):
                        v = pe.snap(visit)
                        pe.wait_ge(gathered[c.ring], 16 * SC * (c.turn + 1))
                        pe.wait_ge(hot_ready, v + 1)
                        pe.wait_ge(added, v + 1)
                        to = seg[:, bass.ds(v % 2, 1), :].rearrange("p a d -> p (a d)")
                        on = hot[:, bass.ds(v % 2, 1), :, :].rearrange("p a c n -> p (a c) n")
                        for k in range(SC):
                            pe.matmul(to[:, 0:RW], on[:, k, :], msg[c.ring][:, k, D:MW],
                                      start=(k == 0), stop=False)
                            ins = pe.matmul(to[:, 0:D], on[:, k, :], msg[c.ring][:, k, 0:D],
                                            start=False, stop=(k == SC - 1))
                        ins.then_inc(summed, 1)
                        pe.reg_add(visit, visit, 1)
                    if alone:
                        pe.drain().then_inc(super_done, 1)

                def after_segment(ins, first):
                    if first:
                        ins.then_inc(super_done, 1)

                pe.wait_ge(w_in, N_W)
                pe.wait_ge(set_up, 1)
                pe.matmul(pcf[:, 0, 0:KT * (P + 2)], zero, wkv[:, 0, 0:KT * (P + 2)],
                          start=True, stop=False, skip_group_check=True)

                def group_a(g, u, i, more):
                    pe.wait_ge(xT_in[u], 16 * (i + 1))

                    def project(j):
                        wait(pe, kv_bias, TPG * g + j - 1)
                        for k in range(KT):
                            ins = pe.matmul(pa[j % 2][:, :], xT[u][:, k, j * P:(j + 1) * P],
                                            wkv[:, k, :], start=(k == 0), stop=(k == KT - 1))
                        ins.then_inc(kv_mm, 1)

                    def accumulate(j, before=0, after=False):
                        n = P if more or before else max(0, min(P, VALID - j * P))
                        if n == 0:
                            return
                        pe.wait_ge(kphi_done, TPG * (g - before) + j + 1)
                        last = not more and not before and j == (VALID - 1) // P
                        for b in range(KT):
                            ins = pe.matmul(acc[:, b, 0:P + 1], kphi[j % 2][0:n, b * P:(b + 1) * P],
                                            va[j % 2][0:n, b, 0:P + 1], start=False, stop=last,
                                            skip_group_check=True)
                            after_segment(ins, after and b == 0)
                        ins.then_inc(acc_mm, 1)

                    project(0)
                    if not (isinstance(g, int) and g == 0):
                        accumulate(TPG - 1, before=1)
                    project(1)
                    segment(super_a(i, u, 0))
                    accumulate(0, after=True)
                    project(2)
                    accumulate(1)
                    project(3)
                    segment(super_a(i, u, 1), alone=not more)
                    accumulate(2, after=True)

                each_group(pe, group_a)

                def query(g, b, after=False):
                    if b == 0:
                        pe.wait_ge(xT_in[1], 16 * (PAIRS + 1 + g))
                        wait(pe, q_act, KT * g)
                        wait(pe, h_done, FT * (g - 1))
                    for k in range(KT):
                        ins = pe.matmul(pa[b][:, :], wq[:, k, b * P:(b + 1) * P], xT[1][:, k, :],
                                        start=(k == 0), stop=(k == KT - 1))
                        after_segment(ins, after and k == 0)
                    ins.then_inc(q_mm, 1)

                def attend(g, after=False):
                    pe.wait_ge(qphi_done, KT * (g + 1))
                    wait(pe, end, END * (g - 2) + 1)
                    for j in range(TPG):
                        for b in range(KT):
                            ins = pe.matmul(pc[:, j, b * P:(b + 1) * P],
                                            qphi[:, b, j * P:(j + 1) * P], kvb[:, b, :],
                                            start=True, stop=True, skip_group_check=True)
                            after_segment(ins, after and j == 0 and b == 0)
                    if not (isinstance(g, int) and g == 0):
                        pe.wait_ge(h_done, FT * (g - 1) + 4)
                    for j in range(TPG):
                        for b in range(KT):
                            ins = pe.matmul(den[:, j, b, :], qphi[:, b, j * P:(j + 1) * P], ksb[:, b, :],
                                            start=True, stop=True, skip_group_check=True)
                    ins.then_inc(nd_mm, 1)

                def turn_attention(g, after=False):
                    pe.wait_ge(attn_done, g + 1)
                    for k in range(KT):
                        for j in range(TPG):
                            ins = pe.transpose(pcf[:, k, j * P:(j + 1) * P],
                                               attn[:, j, k * P:(k + 1) * P], keep["ident"][:, :])
                            after_segment(ins, after and k == 0 and j == 0)
                    ins.then_inc(turn_mm, 1)

                def project_out(g, after=False):
                    pe.wait_ge(aT_done, KT * (g + 1))
                    if not (isinstance(g, int) and g == 0):
                        pe.wait_ge(h_done, FT * (g - 1) + FT - 2)
                    for j in range(TPG):
                        for k in range(KT):
                            ins = pe.matmul(pb[:, j, :], aT[k][:, j * P:(j + 1) * P], wo[:, k, :],
                                            start=(k == 0), stop=(k == KT - 1))
                            after_segment(ins, after and j == 0 and k == 0)
                    ins.then_inc(wo_mm, 1)

                def turn(g, after=False):
                    pe.wait_ge(att_norm, g + 1)
                    for k in range(KT):
                        for j in range(TPG):
                            ins = pe.transpose(pbf[:, k, j * P:(j + 1) * P], xn[:, j, k * P:(k + 1) * P],
                                               keep["ident"][:, :])
                            after_segment(ins, after and k == 0 and j == 0)
                    ins.then_inc(x1_mm, 1)

                def feed(g, f, more, after=False):
                    if f == 0:
                        pe.wait_ge(x1T_done, KT * (g + 1))
                    if f == 2:
                        if more:
                            pe.wait_ge(q_act, KT * (g + 2))
                        else:
                            pe.wait_ge(h_done, FT * g)
                    if f == FT - 1 and more:
                        pe.wait_ge(rec_done, 2 * g + 3)
                    if f >= 4:
                        pe.wait_ge(h_done, FT * g + f - 3)
                    for k in range(KT):
                        ins = pe.matmul(ring[f % 4], w1[:, k, f * P:(f + 1) * P], x1T[:, k, :],
                                        start=(k == 0), stop=(k == KT - 1))
                        after_segment(ins, after and k == 0)
                    ins.then_inc(ff1_mm, 1)

                def feed_back(g, j, more):
                    if j == 0:
                        pe.wait_ge(h_done, FT * (g + 1))
                        if more:
                            pe.wait_ge(aT_done, KT * (g + 2))
                        wait(pe, end, END * (g - 1) + 1)
                    for k in range(FT):
                        ins = pe.matmul(pc[:, j, :], h[:, k, j * P:(j + 1) * P], w2[:, k, :],
                                        start=(k == 0), stop=(k == FT - 1))
                        after_segment(ins, more and k == 0)
                    if j == TPG - 1:
                        ins.then_inc(ff2_mm, 1)

                pe.wait_ge(heads_done, 1)
                query(0, 0)
                query(0, 1)
                attend(0)
                turn_attention(0)
                project_out(0)

                def group_b(g, u, i, more):
                    turn(g, after=not (isinstance(g, int) and g == 0))
                    segment(super_b(i, u, 0), alone=not more)
                    if more:
                        query(g + 1, 0, after=more)
                    segment(super_b(i, u, 1), alone=not more)
                    if more:
                        query(g + 1, 1, after=more)
                    segment(super_b(i, u, 2), alone=not more)
                    feed(g, 0, more, after=more)
                    feed(g, 1, more)
                    segment(super_b(i, u, 3), alone=not more)
                    feed(g, 2, more, after=more)
                    feed(g, 3, more)
                    segment(super_b(i, u, 4), alone=not more)
                    if more:
                        attend(g + 1, after=more)
                    segment(super_b(i, u, 5), alone=not more)
                    feed(g, 4, more, after=more)
                    feed(g, 5, more)
                    segment(super_b(i, u, 6), alone=not more)
                    if more:
                        turn_attention(g + 1, after=more)
                    feed(g, 6, more, after=False)
                    segment(super_b(i, u, 7), alone=not more)
                    feed(g, 7, more, after=more)
                    segment(super_b(i, u, 8), alone=not more)
                    if more:
                        project_out(g + 1, after=more)
                    segment(super_b(i, u, 9), alone=not more)
                    for j in range(TPG):
                        feed_back(g, j, more)
                        segment(super_b(i, u, 10 + j), alone=not more)

                each_group(pe, group_b)

            @block.scalar
            def _(act):
                act.wait_ge(w_in, N_W)
                act.wait_ge(set_up, 1)

                def group_a(g, u, i, more):
                    for j in range(TPG):
                        act.wait_ge(kv_bias, TPG * g + j + 1)
                        wait(act, kphi_done, TPG * g + j - 1)
                        act.activation(kex[j % 2], kb[j % 2], ACT.Exp)
                        act.activation(kre[j % 2], kb[j % 2], ACT.Relu).then_inc(kv_act, 1)

                each_group(act, group_a)

                def query_act(g):
                    wait(act, wo_mm, g)
                    for b in range(KT):
                        act.wait_ge(q_mm, KT * g + b + 1)
                        wait(act, qphi_done, KT * g + b)
                        act.activation(ex[:, :], pa[b][:, :], ACT.Exp, bias=bq[:, b:b + 1])
                        act.activation(qphi[:, b, :], pa[b][:, :], ACT.Relu, bias=bq[:, b:b + 1]
                                       ).then_inc(q_act, 1)

                def turn_out(g):
                    act.wait_ge(turn_mm, g + 1)
                    wait(act, wo_mm, g)
                    for k in range(KT):
                        act.activation(aT[k], pcf[:, k, :], ACT.Copy).then_inc(aT_done, 1)

                def apply_norm(rowsets, wk, chain, value, done):
                    act.wait_ge(chain, value)
                    for j in range(TPG):
                        ins = act.activation(rowsets[:, j, :], rowsets[:, j, :], ACT.Identity,
                                             scale=wk["rs"][:, j:j + 1], bias=wk["nb"][:, j:j + 1])
                    ins.then_inc(done, 1)

                query_act(0)
                turn_out(0)
                apply_norm(xn, w, att, 1 + STAT_OPS, att_norm)

                def group_b(g, u, i, more):
                    act.wait_ge(x1_mm, g + 1)
                    wait(act, ff1_mm, FT * g)
                    for k in range(KT):
                        act.activation(x1T[:, k, :], pbf[:, k, :], ACT.Identity, scale=g1[:, k:k + 1],
                                       bias=n1b[:, k:k + 1]).then_inc(x1T_done, 1)
                    if more:
                        query_act(g + 1)
                    wait(act, ff2_mm, g)
                    for f in range(FT):
                        if f == 6:
                            if more:
                                turn_out(g + 1)
                        act.wait_ge(ff1_mm, FT * g + f + 1)
                        act.activation(h[:, f, :], ring[f % 4], ACT.Relu, bias=b1[:, f:f + 1]
                                       ).then_inc(h_done, 1)
                        if f == 5 and not (isinstance(g, int) and g == 0):
                            apply_norm(out[1 - u], w2nd, end, END * (g - 1) + 1 + STAT_OPS, end_norm)
                    if more:
                        apply_norm(xn, w, att, ATT * (g + 1) + 1 + STAT_OPS, att_norm)

                each_group(act, group_b)
                apply_norm(out[0], w2nd, end, END * (GROUPS - 1) + 1 + STAT_OPS, end_norm)

            @block.vector
            def _(dve):
                visit = dve.alloc_register("dve_visit")
                tile = dve.alloc_register("dve_tile")
                count = dve.alloc_register("dve_count")
                last = dve.alloc_register("dve_last")
                dve.reg_mov(visit, 0)
                dve.reg_mov(last, 0)
                dve.sem_inc(added, 1)
                dve.memset(zero, 0.0)
                dve.memset(kvb[:, :, :], 0.0)
                dve.memset(ksb[:, :, :], 0.0)
                dve.memset(seg[:, 1, 0:RW], 0.0)
                for r in range(2):
                    ins = dve.memset(va[r][:, :, P:P + 2], 1.0)
                ins.then_inc(set_up, 1)
                dve.wait_ge(w_in, N_W)
                dve.wait_ge(set_up, 1)
                dve.tensor_tensor(row_res, row_n1b, row_b2, ALU.add).then_inc(set_up, 1)

                def add_last(v):
                    t = dve.snap(last, min_val=0, max_val=RT - 1)
                    dve.wait_ge(summed, v + 1)
                    dve.wait_ge(added, v + 1)
                    red = keep["red"][:, bass.ds(t, 1), :].rearrange("p a d -> p (a d)")
                    was = seg[:, bass.ds((v + 1) % 2, 1), 0:RW].rearrange("p a d -> p (a d)")
                    dve.tensor_tensor(red, was, red, ALU.add).then_inc(added, 1)

                def load_reach(s):
                    dve.load([tile, count], keep["reach"][0:1, bass.ds(s, 1), :]
                             .rearrange("p a d -> p (a d)"))

                def segment(c, edge, edge_in):
                    if empty(c):
                        return
                    visits = dve.snap(count, min_val=1, max_val=RT)
                    dve.wait_ge(edge_in[c.u], 16 * (c.i + 1))
                    wait(dve, super_done, c.s - (RING - 1))
                    e = edge[c.u][:, c.q, :, :]
                    dve.tensor_tensor(msg[c.ring][:, :, 2 * D:MW],
                                      e[:, 2, :].unsqueeze(2).broadcast_to([P, SC, RELS]),
                                      across(keep["iota"][:, 0:RELS], SC), ALU.is_equal)
                    with dve.Fori(0, visits):
                        v = dve.snap(visit)
                        t = dve.snap(tile, min_val=0, max_val=RT - 1)
                        dve.scalar_tensor_tensor(
                            hot[:, bass.ds(v % 2, 1), :, :].rearrange("p a c n -> p (a c) n"),
                            e[:, 1, :].unsqueeze(2).broadcast_to([P, SC, P]),
                            keep["base"][:, bass.ds(t, 1)], across(keep["iota"][:, :], SC),
                            ALU.subtract, ALU.is_equal).then_inc(hot_ready, 1)
                        add_last(v)
                        dve.reg_mov(last, tile)
                        dve.reg_add(visit, visit, 1)
                        dve.reg_add(tile, tile, 1)
                    load_reach(c.s + 1)

                def group_a(g, u, i, more):
                    def bias(j):
                        dve.wait_ge(kv_mm, TPG * g + j + 1)
                        wait(dve, kv_act, TPG * g + j - 1)
                        wait(dve, acc_mm, TPG * g + j - 1)
                        dve.tensor_tensor(kb[j % 2], pa[j % 2][:, 0:D], bkv[:, 0:D], ALU.add)
                        dve.tensor_tensor(va[j % 2][:, :, 0:P],
                                          pa[j % 2][:, D:2 * D].rearrange("p (b c) -> p b c", b=KT),
                                          bkv[:, D:2 * D].rearrange("p (b c) -> p b c", b=KT),
                                          ALU.add).then_inc(kv_bias, 1)

                    def phi(j):
                        dve.wait_ge(kv_act, TPG * g + j + 1)
                        dve.scalar_tensor_tensor(kphi[j % 2], kex[j % 2], 1.0, kre[j % 2],
                                                 ALU.min, ALU.add).then_inc(kphi_done, 1)

                    if isinstance(g, int) and g == 0:
                        load_reach(0)
                    bias(0)
                    segment(super_a(i, u, 0), edge_a, edge_a_in)
                    bias(1)
                    phi(0)
                    phi(1)
                    bias(2)
                    segment(super_a(i, u, 1), edge_a, edge_a_in)
                    bias(3)
                    phi(2)
                    phi(3)

                each_group(dve, group_a)
                dve.wait_ge(acc_mm, TPG * (GROUPS - 1) + -(-VALID // P))
                for b in range(KT):
                    for r in range(0, P, HD):
                        dve.tensor_copy(kvb[r:r + HD, b, r:r + HD], acc[r:r + HD, b, r:r + HD])
                        ins = dve.tensor_copy(ksb[r:r + HD, b, r // HD:r // HD + 1],
                                              acc[r:r + HD, b, P:P + 1])
                ins.then_inc(heads_done, 1)

                def query_phi(g, b):
                    dve.wait_ge(q_act, KT * g + b + 1)
                    dve.scalar_tensor_tensor(qphi[:, b, :], ex[:, :], 1.0, qphi[:, b, :],
                                             ALU.min, ALU.add).then_inc(qphi_done, 1)

                def attention(g):
                    dve.wait_ge(nd_mm, g + 1)
                    dve.tensor_scalar(rec[:, :, :, :], den, DEN_EPS, None, ALU.add).then_inc(rec_done, 1)
                    dve.wait_ge(rec_done, 2 * g + 1)
                    dve.reciprocal(rec[:, :, :, :], rec[:, :, :, :]).then_inc(rec_done, 1)
                    dve.wait_ge(rec_done, 2 * g + 2)
                    dve.tensor_tensor(attn.rearrange("p j (h c) -> p (j h) c", c=HD),
                                      pc[:, :, :].rearrange("p j (h c) -> p (j h) c", c=HD),
                                      rec[:, :, :, :].rearrange("p j b h -> p (j b h)").unsqueeze(2)
                                      .broadcast_to([P, TPG * KT * HPT, HD]), ALU.mult
                                      ).then_inc(attn_done, 1)

                def residual(g):
                    dve.wait_ge(xn_in, 16 * (g + 1))
                    dve.tensor_tensor(xn[:, :, :], xn[:, :, :], across(row_bo, TPG), ALU.add
                                      ).then_inc(xn_bo, 1)

                def result_in(g, u):
                    dve.wait_ge(ff2_mm, g + 1)
                    dve.wait_ge(att, ATT * (g + 1))
                    dve.tensor_tensor(out[u], pc[:, :, :], out[u], ALU.add).then_inc(end, 1)

                def result_norm(g, u):
                    dve.wait_ge(end, END * g + 1)
                    norm_stats(dve, out[u], w2nd, end, END * g + 1)

                def result_gain(g, u):
                    dve.wait_ge(end_norm, g + 1)
                    dve.wait_ge(end, END * g + 1 + STAT_OPS)
                    dve.tensor_tensor(out[u], out[u], across(row_g2, TPG), ALU.mult).then_inc(end, 1)

                def attended(g):
                    dve.wait_ge(wo_mm, g + 1)
                    dve.wait_ge(xn_bo, g + 1)
                    dve.tensor_tensor(xn[:, :, :], pb[:, :, :], xn[:, :, :], ALU.add).then_inc(att, 1)
                    dve.wait_ge(att, ATT * g + 1)
                    norm_moments(dve, xn, w, att, ATT * g + 1)

                residual(0)
                for b in range(KT):
                    query_phi(0, b)
                attention(0)
                attended(0)
                norm_factors(dve, w, att, 1)

                def group_b(g, u, i, more):
                    zeroth = isinstance(g, int) and g == 0

                    def edges(q):
                        segment(super_b(i, u, q), edge_b, edge_b_in)

                    edges(0)
                    if not zeroth:
                        result_in(g - 1, 1 - u)
                    dve.wait_ge(att_norm, g + 1)
                    dve.wait_ge(att, ATT * g + 1 + STAT_OPS)
                    wait(dve, stored, 16 * (g - 1))
                    dve.tensor_tensor(out[u], xn[:, :, :], across(row_g1, TPG), ALU.mult
                                      ).then_inc(att, 1)
                    edges(1)
                    dve.wait_ge(att, ATT * g + 2 + STAT_OPS)
                    dve.tensor_tensor(out[u], out[u], across(row_res, TPG), ALU.add).then_inc(att, 1)
                    edges(2)
                    if more:
                        query_phi(g + 1, 0)
                        query_phi(g + 1, 1)
                    edges(3)
                    if more:
                        residual(g + 1)
                    edges(4)
                    if not zeroth:
                        result_norm(g - 1, 1 - u)
                    edges(5)
                    if more:
                        attention(g + 1)
                    for q in (6, 7, 8):
                        edges(q)
                    if not zeroth:
                        result_gain(g - 1, 1 - u)
                    edges(9)
                    if more:
                        attended(g + 1)
                    edges(10)
                    if more:
                        norm_factors(dve, w, att, ATT * (g + 1) + 1)
                    for q in range(11, SB):
                        edges(q)

                each_group(dve, group_b)
                add_last(dve.snap(visit))
                result_in(GROUPS - 1, 0)
                result_norm(GROUPS - 1, 0)
                result_gain(GROUPS - 1, 0)
                dve.wait_ge(end, END * GROUPS)


def gru_phase(nc, a, d, keep):
    with ExitStack() as ctx:
        m = Names(nc, ctx, "gru")
        room = [m.sb(f"raw{s}", [P, KT * 3 * D], F32) for s in range(2)]
        raw = [room[s][:, :].rearrange("p (k n) -> p k n", k=KT) for s in range(2)]
        w_hi = [m.sb(f"w_hi{s}", [P, KT, 3 * D], F32R) for s in range(2)]
        w_lo = [m.sb(f"w_lo{s}", [P, KT, 3 * D], F32R) for s in range(2)]
        rel = m.sb("rel", [RELS, D], F32)
        col = m.sb("col", [P, 4 * KT], F32)
        gate_b = m.sb("gate_b", [P, 2 * KT], F32)
        xT = [m.sb(f"xT{u}", [P, KT, G], F32) for u in range(2)]
        x_hi, x_lo, r_hi, r_lo = ([m.sb(f"{n}{u}", [P, KT, G], F32R) for u in range(2)]
                                  for n in ("x_hi", "x_lo", "r_hi", "r_lo"))
        red = m.sb("red", [P, TPG, D], F32)
        relc = m.sb("relc", [P, TPG, RELS], F32)
        relT = m.sb("relT", [RELS, G], F32)
        gr = m.sb("gr", [P, G], F32)
        gz, gn = (room[s][:, TPG * D:TPG * D + G] for s in range(2))
        gT = m.sb("gT", [P, KT, G], F32)
        mid0 = m.sb("mid0", [P, TPG, D], F32)
        x, mid1 = (room[s][:, 0:TPG * D].rearrange("p (j d) -> p j d", j=TPG) for s in range(2))
        mid = [mid0, mid1]
        shift = m.sb("shift", [P, D], F32)

        p_red = m.ps("red", [P, KT, G])
        p_gate = [m.ps(f"gate{q}", [P, G]) for q in range(4)]
        p_out = m.ps("out", [P, TPG, D])
        p_relT = p_out[0:RELS, 0:2, :].rearrange("p a d -> p (a d)")

        w_in = [m.sem(f"w_in{s}") for s in range(2)]
        c_in = m.sem("c_in")
        w_split = m.sem("w_split")
        w_high = m.sem("w_high")
        bias_sum = m.sem("bias_sum")
        xT_in = [m.sem(f"xT_in{u}") for u in range(2)]
        mid_in = [m.sem(f"mid_in{u}") for u in range(2)]
        x_in, x_sum = m.sem("x_in"), m.sem("x_sum")
        stored = [m.sem(f"stored{u}") for u in range(2)]
        (copied, relT_mm, relT_done, red_mm, high, x_low, r_high, r_low, gates, reset, hn, pre, tan,
         diff, prod, g_done, out_mm, sum_done) = (m.sem(n) for n in (
             "copied", "relT_mm", "relT_done", "red_mm", "high", "x_low", "r_high", "r_low", "gates",
             "reset", "hn", "pre", "tan", "diff", "prod", "g_done", "out_mm", "sum_done"))
        feats = "(k p) n -> p k n"

        with nc.Block() as block:
            @block.sync
            def _(sp):
                def load_x(g):
                    sp.dma_start(x, rows(a["x"], g)).then_inc(x_in, 16)

                for s, weights in ((0, a["w_ihT"]), (1, a["w_hhT"])):
                    sp.dma_start(raw[s], weights.rearrange(feats, p=P)).then_inc(w_in[s], 16)
                sp.dma_start(rel[:, :], a["rel"]).then_inc(c_in, 16)
                sp.dma_start(col[:, :], a["gru_cols"]).then_inc(c_in, 16)
                sp.dma_start(gate_b[:, :], a["gru_gate_cols"]).then_inc(c_in, 16)
                sp.dma_start(shift[:, :], a["ln2_b"].partition_broadcast(P)).then_inc(c_in, 16)
                sp.dma_start(xT[0][:, :, :], d["xnT"][0]).then_inc(xT_in[0], 16)
                sp.dma_start(mid[0][:, :, :], rows(d["mid"], 0)).then_inc(mid_in[0], 16)
                sp.dma_start(xT[1][:, :, :], d["xnT"][1]).then_inc(xT_in[1], 16)
                sp.wait_ge(w_split, 2)
                sp.dma_start(mid[1][:, :, :], rows(d["mid"], 1)).then_inc(mid_in[1], 16)
                load_x(0)

                def group(g, u, i, more):
                    if isinstance(g, int) and g == 0:
                        return
                    if more:
                        sp.wait_ge(g_done, KT * g)
                        sp.dma_start(xT[1 - u][:, :, :], d["xnT"][g + 1]).then_inc(xT_in[1 - u], 16)
                    sp.wait_ge(x_sum, 2 * g - 1)
                    load_x(g)
                    sp.wait_ge(sum_done, g)
                    sp.dma_start(rows(d["all"], g - 1), mid[1 - u][:, :, :]).then_inc(stored[1 - u], 16)
                    if more:
                        sp.wait_ge(stored[1 - u], 16 * i if u == 0 else 16 * (i + 1))
                        sp.dma_start(mid[1 - u][:, :, :], rows(d["mid"], g + 1)
                                     ).then_inc(mid_in[1 - u], 16)

                each_group(sp, group)
                sp.wait_ge(sum_done, GROUPS)
                sp.dma_start(rows(d["all"], GROUPS - 1), mid[0][:, :, :]).then_inc(stored[0], 16)
                for u in range(2):
                    sp.wait_ge(stored[u], 16 * (PAIRS + 1 - u))

            @block.tensor
            def _(pe):
                pe.wait_ge(c_in, 64)
                pe.wait_ge(w_split, 2)

                def messages(g):
                    pe.wait_ge(copied, g + 1)
                    wait(pe, sum_done, g - 2)
                    for j in range(TPG):
                        ins = pe.transpose(p_relT[:, j * P:(j + 1) * P], relc[:, j, :],
                                           keep["ident"][:, :])
                    ins.then_inc(relT_mm, 1)
                    wait(pe, r_low, KT * g)
                    for b in range(KT):
                        for j in range(TPG):
                            pe.matmul(p_red[:, b, j * P:(j + 1) * P], red[:, j, b * P:(b + 1) * P],
                                      keep["ident"][:, :], start=(j == 0), stop=False,
                                      skip_group_check=True)
                    pe.wait_ge(relT_done, g + 1)
                    for b in range(KT):
                        ins = pe.matmul(p_red[:, b, :], rel[:, b * P:(b + 1) * P], relT[:, :],
                                        start=False, stop=True, skip_group_check=True)
                    ins.then_inc(red_mm, 1)

                def products(g, u, b, gate, sides, col0):
                    n = 0
                    last = len(sides) * KT * 3
                    for s in sides:
                        hi, lo = ((r_hi[u], r_lo[u]), (x_hi[u], x_lo[u]))[s]
                        for k in range(KT):
                            for wt, act_ in ((w_hi[s], hi), (w_hi[s], lo), (w_lo[s], hi)):
                                ins = pe.matmul(p_gate[gate][:, :],
                                                wt[:, k, col0 + b * P:col0 + (b + 1) * P],
                                                act_[:, k, :], start=(n == 0), stop=(n == last - 1))
                                n += 1
                    ins.then_inc(gates, 1)

                def gate_sums(g, u, b):
                    item = KT * g + b
                    wait(pe, reset, 2 * item - 1)
                    products(g, u, b, 0, (1, 0), 0)
                    wait(pe, hn, item)
                    products(g, u, b, 3, (1,), 2 * D)
                    wait(pe, pre, item)
                    products(g, u, b, 2, (0,), 2 * D)
                    wait(pe, reset, 2 * item)
                    products(g, u, b, 1, (1, 0), D)

                def turn_back(g):
                    pe.wait_ge(g_done, KT * (g + 1))
                    wait(pe, sum_done, g)
                    for j in range(TPG):
                        for b in range(KT):
                            ins = pe.transpose(p_out[:, j, b * P:(b + 1) * P],
                                               gT[:, b, j * P:(j + 1) * P], keep["ident"][:, :])
                    ins.then_inc(out_mm, 1)

                messages(0)

                def group(g, u, i, more):
                    pe.wait_ge(x_low, KT * (g + 1))
                    pe.wait_ge(r_low, KT * (g + 1))
                    gate_sums(g, u, 0)
                    if more:
                        messages(g + 1)
                    if not (isinstance(g, int) and g == 0):
                        turn_back(g - 1)
                    gate_sums(g, u, 1)

                each_group(pe, group)
                pe.wait_ge(g_done, KT * GROUPS)
                turn_back(GROUPS - 1)

            @block.scalar
            def _(act):
                for s in range(2):
                    act.wait_ge(w_in[s], 16)
                    act.activation(w_hi[s][:, :, :], raw[s], ACT.Copy).then_inc(w_high, 1)

                act.wait_ge(bias_sum, 1)

                def take(g):
                    wait(act, red_mm, g)
                    act.activation(red[:, :, :], keep["red"][:, bass.ds(g * TPG, TPG), 0:D], ACT.Copy,
                                   scale=1.0 / PAIR)
                    act.activation(relc[:, :, :], keep["red"][:, bass.ds(g * TPG, TPG), D:RW],
                                   ACT.Copy).then_inc(copied, 1)

                def turned_counts(g):
                    act.wait_ge(relT_mm, g + 1)
                    act.activation(relT[:, :], p_relT, ACT.Copy).then_inc(relT_done, 1)

                def high_x(g, u, i):
                    act.wait_ge(xT_in[u], 16 * (i + 1))
                    wait(act, gates, 4 * KT * (g - 1))
                    act.activation(x_hi[u][:, :, :], xT[u][:, :, :], ACT.Copy).then_inc(high, 1)

                def high_r(g, u):
                    act.wait_ge(red_mm, g + 1)
                    for b in range(KT):
                        act.activation(r_hi[u][:, b, :], p_red[:, b, :], ACT.Copy).then_inc(r_high, 1)

                take(0)
                turned_counts(0)
                high_x(0, 0, 0)
                high_r(0, 0)

                def gate_values(g, b):
                    item = KT * g + b
                    act.wait_ge(gates, 4 * item + 1)
                    wait(act, hn, item)
                    act.activation(gr[:, :], p_gate[0][:, :], ACT.Sigmoid, bias=gate_b[:, b:b + 1]
                                   ).then_inc(reset, 1)
                    act.wait_ge(gates, 4 * item + 4)
                    wait(act, g_done, item)
                    act.activation(gz[:, :], p_gate[1][:, :], ACT.Sigmoid,
                                   bias=gate_b[:, KT + b:KT + b + 1]).then_inc(reset, 1)
                    act.wait_ge(pre, item + 1)
                    act.activation(gn[:, :], gn[:, :], ACT.Tanh, bias=col[:, 2 * KT + b:2 * KT + b + 1]
                                   ).then_inc(tan, 1)

                def group(g, u, i, more):
                    if more:
                        take(g + 1)
                    gate_values(g, 0)
                    if more:
                        turned_counts(g + 1)
                        high_x(g + 1, 1 - u, i if u == 0 else i + 1)
                        high_r(g + 1, 1 - u)
                    gate_values(g, 1)

                each_group(act, group)

            @block.vector
            def _(dve):
                dve.wait_ge(c_in, 64)
                dve.tensor_tensor(gate_b[:, :], gate_b[:, :], col[:, 0:2 * KT], ALU.add
                                  ).then_inc(bias_sum, 1)
                for s in range(2):
                    dve.wait_ge(w_high, s + 1)
                    dve.tensor_tensor(w_lo[s][:, :, :], raw[s], w_hi[s][:, :, :].bitcast(F32),
                                      ALU.subtract).then_inc(w_split, 1)

                def low_x(g, u):
                    dve.wait_ge(high, g + 1)
                    wait(dve, gates, 4 * KT * (g - 1))
                    for b in range(KT):
                        dve.tensor_tensor(x_lo[u][:, b, :], xT[u][:, b, :],
                                          x_hi[u][:, b, :].bitcast(F32), ALU.subtract
                                          ).then_inc(x_low, 1)

                def low_r(g, u):
                    for b in range(KT):
                        dve.wait_ge(r_high, KT * g + b + 1)
                        dve.tensor_tensor(r_lo[u][:, b, :], p_red[:, b, :],
                                          r_hi[u][:, b, :].bitcast(F32), ALU.subtract
                                          ).then_inc(r_low, 1)

                def candidate(g, u, b):
                    item = KT * g + b
                    dve.wait_ge(gates, 4 * item + 2)
                    dve.wait_ge(reset, 2 * item + 1)
                    wait(dve, g_done, item)
                    dve.scalar_tensor_tensor(gn[:, :], p_gate[3][:, :], col[:, 3 * KT + b:3 * KT + b + 1],
                                             gr[:, :], ALU.add, ALU.mult).then_inc(hn, 1)
                    dve.wait_ge(hn, item + 1)
                    dve.wait_ge(gates, 4 * item + 3)
                    dve.tensor_tensor(gn[:, :], p_gate[2][:, :], gn[:, :], ALU.add).then_inc(pre, 1)

                def blend(g, u, b):
                    item = KT * g + b
                    dve.wait_ge(tan, item + 1)
                    if b == 0:
                        wait(dve, out_mm, g)
                    dve.tensor_tensor(gT[:, b, :], xT[u][:, b, :], gn[:, :], ALU.subtract
                                      ).then_inc(diff, 1)
                    dve.wait_ge(diff, item + 1)
                    dve.wait_ge(reset, 2 * item + 2)
                    dve.tensor_tensor(gT[:, b, :], gT[:, b, :], gz[:, :], ALU.mult).then_inc(prod, 1)
                    dve.wait_ge(prod, item + 1)
                    dve.tensor_tensor(gT[:, b, :], gT[:, b, :], gn[:, :], ALU.add).then_inc(g_done, 1)

                def add_mix(g, u, i):
                    dve.wait_ge(mid_in[u], 16 * (i + 1))
                    dve.wait_ge(x_in, 16 * (g + 1))
                    dve.tensor_tensor(mid[u][:, :, :], mid[u][:, :, :], x, ALU.add).then_inc(x_sum, 1)
                    dve.wait_ge(x_sum, 2 * g + 1)
                    dve.tensor_tensor(mid[u][:, :, :], mid[u][:, :, :], across(shift[:, :], TPG),
                                      ALU.add).then_inc(x_sum, 1)

                def add_gru(g, u):
                    dve.wait_ge(x_sum, 2 * g + 2)
                    dve.wait_ge(out_mm, g + 1)
                    dve.tensor_tensor(mid[u][:, :, :], p_out[:, :, :], mid[u][:, :, :], ALU.add
                                      ).then_inc(sum_done, 1)

                low_x(0, 0)
                low_r(0, 0)

                def group(g, u, i, more):
                    zeroth = isinstance(g, int) and g == 0
                    if not zeroth:
                        add_mix(g - 1, 1 - u, i - 1 if u == 0 else i)
                    candidate(g, u, 0)
                    blend(g, u, 0)
                    if more:
                        low_x(g + 1, 1 - u)
                        low_r(g + 1, 1 - u)
                    if not zeroth:
                        add_gru(g - 1, 1 - u)
                    candidate(g, u, 1)
                    blend(g, u, 1)

                each_group(dve, group)
                add_mix(GROUPS - 1, 0, PAIRS)
                add_gru(GROUPS - 1, 0)


def experts_phase(nc, a, d, keep):
    with ExitStack() as ctx:
        m = Names(nc, ctx, "moe")
        LAYERS = 3
        hi = [[m.sb(f"w_hi{l}_{e}", [P, KT, D], F32R) for e in range(NE)] for l in range(LAYERS)]
        lo = [[m.sb(f"w_lo{l}_{e}", [P, KT, D], F32R) for e in range(NE)] for l in range(LAYERS)]
        raw = [m.sb(f"raw{r}", [P, KT, D], F32) for r in range(4)]
        wr = m.sb("wr", [P, KT, NE], F32)
        wr_hi, wr_lo = m.sb("wr_hi", [P, KT, NE], F32R), m.sb("wr_lo", [P, KT, NE], F32R)
        br = m.sb("br", [P, NE], F32)
        bo = m.sb("bo", [NE, D], F32)
        bn = m.sb("bn", [P, 5, 2, NE * KT], F32)
        scale, shift = m.sb("scale", [P, 2, NE * KT], F32), m.sb("shift", [P, 2, NE * KT], F32)
        bt = m.sb("bt", [P, 2, NE * KT], F32)
        x3 = [m.sb(f"x3_{u}", [P, TPG, D], F32) for u in range(2)]
        f = m.sb("f", [P, TPG, D], F32)
        f_hi = [m.sb(f"f_hi{u}", [P, KT, G], F32R) for u in range(2)]
        f_lo = [m.sb(f"f_lo{u}", [P, KT, G], F32R) for u in range(2)]
        act_f = [m.sb(f"act{l}", [P, KT, G], F32) for l in range(2)]
        act_hi = [[m.sb(f"act_hi{l}_{r}", [P, KT, G], F32R) for r in range(2)] for l in range(2)]
        act_lo = [[m.sb(f"act_lo{l}_{r}", [P, KT, G], F32R) for r in range(2)] for l in range(2)]
        logit = m.sb("logit", [P, TPG, NE], F32)
        top, tot = m.sb("top", [P, TPG], F32), m.sb("tot", [P, TPG], F32)
        gate = [m.sb(f"gate{u}", [P, TPG, NE], F32) for u in range(2)]
        gateT = m.sb("gateT", [NE, G], F32)
        w = norm_work(m.sb)

        p_h = [[m.ps(f"h{l}_{k}", [P, G]) for k in range(KT)] for l in range(2)]
        p_y = m.ps("y", [P, TPG, D])
        p_f = m.ps("f", [P, KT, G])
        p_logit = p_f[:, 0, 0:TPG * NE].rearrange("p (j e) -> p j e", j=TPG)
        p_gateT = p_f[0:NE, 1, :]

        raw_in = [m.sem(f"raw_in{r}") for r in range(4)]
        c_in = m.sem("c_in")
        w_high, w_low, wr_high, prep = (m.sem(n) for n in ("w_high", "w_low", "wr_high", "prep"))
        x_in = [m.sem(f"x_in{u}") for u in range(2)]
        stored = [m.sem(f"stored{u}") for u in range(2)]
        (normed, f_mm, f_high, f_low, logit_mm, softmax, expd, gateT_mm, gateT_done, bias_mm,
         acc_done, y_mm) = (m.sem(n) for n in (
             "normed", "f_mm", "f_high", "f_low", "logit_mm", "softmax", "expd", "gateT_mm",
             "gateT_done", "bias_mm", "acc_done", "y_mm"))
        h_mm = [m.sem(f"h_mm{l}") for l in range(2)]
        h_act = [m.sem(f"h_act{l}") for l in range(2)]
        h_low = [m.sem(f"h_low{l}") for l in range(2)]
        softmax_in, normed_w = m.sem("softmax_in"), m.sem("normed_w")
        SOFTMAX = 5
        ACC = 1 + NE
        n_w = LAYERS * NE
        EARLY = 2

        with nc.Block() as block:
            @block.sync
            def _(sp):
                sp.dma_start(x3[0][:, :, :], rows(d["all"], 0)).then_inc(x_in[0], 16)
                for t, src in ((wr[:, :, :], a["w_router"].rearrange("(k p) n -> p k n", p=P)),
                               (br[:, :], a["b_router"].partition_broadcast(P)),
                               (bo[:, :], a["b_out"]),
                               (bn[:, :, :, :], a["bn_cols"])):
                    sp.dma_start(t, src).then_inc(c_in, 16)
                for n in range(n_w):
                    wait(sp, w_low, n - 3)
                    sp.dma_start(raw[n % 4][:, :, :], a["w_experts"][n % LAYERS, n // LAYERS]
                                 ).then_inc(raw_in[n % 4], 16)
                    if n == LAYERS:
                        sp.dma_start(x3[1][:, :, :], rows(d["all"], 1)).then_inc(x_in[1], 16)

                def group(g, u, i, more):
                    if more and not (isinstance(g, int) and g == 0):
                        sp.wait_ge(stored[1 - u], 16 * i if u == 0 else 16 * (i + 1))
                        sp.dma_start(x3[1 - u][:, :, :], rows(d["all"], g + 1)
                                     ).then_inc(x_in[1 - u], 16)
                    sp.wait_ge(acc_done, ACC * (g + 1))
                    sp.dma_start(rows(a["out"], g), x3[u][:, :, :]).then_inc(stored[u], 16)

                each_group(sp, group)
                for u in range(2):
                    sp.wait_ge(stored[u], 16 * (PAIRS + 1 - u))

            @block.tensor
            def _(pe):
                def passes(out, wt, act, first, last):
                    for n, (p, q) in enumerate(((wt[0], act[0]), (wt[0], act[1]), (wt[1], act[0]))):
                        ins = pe.matmul(out, p, q, start=(first and n == 0), stop=(last and n == 2))
                    return ins

                def turn(g, u):
                    pe.wait_ge(normed, NORM_OPS * (g + 1))
                    wait(pe, gateT_done, g)
                    for k in range(KT):
                        for j in range(TPG):
                            ins = pe.transpose(p_f[:, k, j * P:(j + 1) * P], f[:, j, k * P:(k + 1) * P],
                                               keep["ident"][:, :])
                    ins.then_inc(f_mm, 1)

                def route(g, u):
                    pe.wait_ge(f_low, KT * (g + 1))
                    for j in range(TPG):
                        for k in range(KT):
                            t = slice(j * P, (j + 1) * P)
                            ins = passes(p_logit[:, j, :], (f_hi[u][:, k, t], f_lo[u][:, k, t]),
                                         (wr_hi[:, k, :], wr_lo[:, k, :]), k == 0, k == KT - 1)
                    ins.then_inc(logit_mm, 1)

                def turn_gates(g, u):
                    pe.wait_ge(softmax, SOFTMAX * (g + 1))
                    for j in range(TPG):
                        ins = pe.transpose(p_gateT[:, j * P:(j + 1) * P], gate[u][:, j, :],
                                           keep["ident"][:, :])
                    ins.then_inc(gateT_mm, 1)

                def biases(g):
                    pe.wait_ge(gateT_done, g + 1)
                    wait(pe, acc_done, ACC * g)
                    for j in range(TPG):
                        ins = pe.matmul(p_y[:, j, :], gateT[:, j * P:(j + 1) * P], bo[:, :],
                                        start=True, stop=True)
                    ins.then_inc(bias_mm, 1)

                def weights(g, l, e):
                    if isinstance(g, int) and g == 0:
                        pe.wait_ge(w_low, LAYERS * e + l + 1)

                def layer1(g, u, e):
                    n = NE * g + e
                    weights(g, 0, e)
                    wait(pe, h_act[0], KT * n)
                    for b in range(KT):
                        c = slice(b * P, (b + 1) * P)
                        for k in range(KT):
                            ins = passes(p_h[0][b][:, :], (hi[0][e][:, k, c], lo[0][e][:, k, c]),
                                         (f_hi[u][:, k, :], f_lo[u][:, k, :]), k == 0, k == KT - 1)
                        ins.then_inc(h_mm[0], 1)

                def layer2(g, e):
                    n = NE * g + e
                    weights(g, 1, e)
                    pe.wait_ge(h_low[0], KT * (n + 1))
                    wait(pe, h_act[1], KT * n)
                    for b in range(KT):
                        c = slice(b * P, (b + 1) * P)
                        for k in range(KT):
                            ins = passes(p_h[1][b][:, :], (hi[1][e][:, k, c], lo[1][e][:, k, c]),
                                         (act_hi[0][e % 2][:, k, :], act_lo[0][e % 2][:, k, :]),
                                         k == 0, k == KT - 1)
                        ins.then_inc(h_mm[1], 1)

                def layer3(g, e):
                    n = NE * g + e
                    weights(g, 2, e)
                    pe.wait_ge(h_low[1], KT * (n + 1))
                    pe.wait_ge(acc_done, ACC * g + 1 + e)
                    for j in range(TPG):
                        t = slice(j * P, (j + 1) * P)
                        for k in range(KT):
                            ins = passes(p_y[:, j, :], (act_hi[1][e % 2][:, k, t], act_lo[1][e % 2][:, k, t]),
                                         (hi[2][e][:, k, :], lo[2][e][:, k, :]), k == 0, k == KT - 1)
                    ins.then_inc(y_mm, 1)

                pe.wait_ge(prep, 2)
                turn(0, 0)
                pe.wait_ge(f_low, KT)
                layer1(0, 0, 0)
                route(0, 0)
                layer1(0, 0, 1)
                turn_gates(0, 0)
                layer2(0, 0)

                def group(g, u, i, more):
                    for e in range(NE):
                        if e < NE - 2:
                            layer1(g, u, e + 2)
                        elif more:
                            layer1(g + 1, 1 - u, e + 2 - NE)
                        if e == 0:
                            biases(g)
                        if e < NE - 1:
                            layer2(g, e + 1)
                        elif more:
                            layer2(g + 1, 0)
                        layer3(g, e)
                        if more and e == 2:
                            turn(g + 1, 1 - u)
                        if more and e == 3:
                            route(g + 1, 1 - u)
                        if more and e == 5:
                            turn_gates(g + 1, 1 - u)

                each_group(pe, group)

            @block.scalar
            def _(act):
                def high_weights(e):
                    for l in range(LAYERS):
                        n = LAYERS * e + l
                        act.wait_ge(raw_in[n % 4], 16 * (n // 4 + 1))
                        act.activation(hi[l][e][:, :, :], raw[n % 4][:, :, :], ACT.Copy
                                       ).then_inc(w_high, 1)

                act.wait_ge(c_in, 64)
                act.activation(wr_hi[:, :, :], wr[:, :, :], ACT.Copy).then_inc(wr_high, 1)
                for e in range(EARLY):
                    high_weights(e)

                def take_f(g, u):
                    act.wait_ge(f_mm, g + 1)
                    wait(act, h_mm[0], KT * NE * (g - 1))
                    for k in range(KT):
                        act.activation(f_hi[u][:, k, :], p_f[:, k, :], ACT.Copy).then_inc(f_high, 1)

                def exponent(g, u):
                    act.wait_ge(softmax, SOFTMAX * g + 2)
                    act.activation(logit[:, :, :], logit[:, :, :], ACT.Exp).then_inc(expd, 1)

                def take_gates(g):
                    act.wait_ge(gateT_mm, g + 1)
                    wait(act, bias_mm, g)
                    act.activation(gateT[:, :], p_gateT, ACT.Copy).then_inc(gateT_done, 1)

                def layer(l, g, e):
                    n = NE * g + e
                    reader = (h_mm[1], y_mm)[l]
                    wait(act, reader, KT * (n - 1) if l == 0 else n - 1)
                    for b in range(KT):
                        act.wait_ge(h_mm[l], KT * n + b + 1)
                        wait(act, h_low[l], KT * (n - 1) + b + 1)
                        c = e * KT + b
                        for t in (act_f[l], act_hi[l][e % 2]):
                            ins = act.activation(t[:, b, :], p_h[l][b][:, :], ACT.Relu,
                                                 scale=scale[:, l, c:c + 1], bias=shift[:, l, c:c + 1])
                        ins.then_inc(h_act[l], 1)

                act.wait_ge(prep, 2)
                take_f(0, 0)
                layer(0, 0, 0)
                exponent(0, 0)
                layer(0, 0, 1)
                take_gates(0)
                layer(1, 0, 0)

                def group(g, u, i, more):
                    for e in range(NE):
                        if isinstance(g, int) and g == 0 and e + EARLY < NE:
                            high_weights(e + EARLY)
                        if e < NE - 2:
                            layer(0, g, e + 2)
                        elif more:
                            layer(0, g + 1, e + 2 - NE)
                        if e < NE - 1:
                            layer(1, g, e + 1)
                        elif more:
                            layer(1, g + 1, 0)
                        if more and e == 2:
                            take_f(g + 1, 1 - u)
                        if more and e == 3:
                            exponent(g + 1, 1 - u)
                        if more and e == 5:
                            take_gates(g + 1)

                each_group(act, group)

            @block.vector
            def _(dve):
                def norm(g, u, i):
                    dve.wait_ge(x_in[u], 16 * (i + 1))
                    wait(dve, f_mm, g)
                    norm_rows(dve, f, x3[u], w, normed, NORM_OPS * g)

                norm(0, 0, 0)

                dve.wait_ge(c_in, 64)
                b_, g_, be, mean, var = (bn[:, c, :, :] for c in range(5))
                dve.tensor_scalar(var, var, BN_EPS, None, ALU.add).then_inc(normed_w, 1)
                rsqrt(dve, scale[:, :, :], var, bt[:, :, :], normed_w, 1)
                k = 1 + RSQRT_OPS
                dve.wait_ge(normed_w, k)
                dve.tensor_tensor(scale[:, :, :], scale[:, :, :], g_, ALU.mult).then_inc(normed_w, 1)
                dve.tensor_tensor(shift[:, :, :], b_, mean, ALU.subtract).then_inc(normed_w, 1)
                dve.wait_ge(normed_w, k + 2)
                dve.tensor_tensor(shift[:, :, :], shift[:, :, :], scale[:, :, :], ALU.mult
                                  ).then_inc(normed_w, 1)
                dve.wait_ge(normed_w, k + 3)
                dve.tensor_tensor(shift[:, :, :], shift[:, :, :], be, ALU.add).then_inc(prep, 1)
                def low_weights(e):
                    for l in range(LAYERS):
                        n = LAYERS * e + l
                        dve.wait_ge(w_high, n + 1)
                        dve.tensor_tensor(lo[l][e][:, :, :], raw[n % 4][:, :, :],
                                          hi[l][e][:, :, :].bitcast(F32), ALU.subtract
                                          ).then_inc(w_low, 1)

                for e in range(EARLY):
                    low_weights(e)
                dve.wait_ge(wr_high, 1)
                dve.tensor_tensor(wr_lo[:, :, :], wr[:, :, :], wr_hi[:, :, :].bitcast(F32), ALU.subtract
                                  ).then_inc(prep, 1)

                def low_f(g, u):
                    for k in range(KT):
                        dve.wait_ge(f_high, KT * g + k + 1)
                        dve.tensor_tensor(f_lo[u][:, k, :], p_f[:, k, :], f_hi[u][:, k, :].bitcast(F32),
                                          ALU.subtract).then_inc(f_low, 1)

                def softmax_a(g):
                    base = SOFTMAX * g
                    dve.wait_ge(logit_mm, g + 1)
                    wait(dve, softmax, base)
                    dve.tensor_tensor(logit[:, :, :], p_logit, across(br[:, :], TPG), ALU.add
                                      ).then_inc(softmax_in, 1)
                    dve.wait_ge(softmax_in, g + 1)
                    dve.tensor_reduce(top[:, :], logit[:, :, :], AX.X, ALU.max).then_inc(softmax, 1)
                    dve.wait_ge(softmax, base + 1)
                    dve.tensor_tensor(logit[:, :, :], logit[:, :, :],
                                      top[:, :].unsqueeze(2).broadcast_to([P, TPG, NE]), ALU.subtract
                                      ).then_inc(softmax, 1)

                def softmax_b(g, u):
                    base = SOFTMAX * g
                    dve.wait_ge(expd, g + 1)
                    dve.tensor_reduce(tot[:, :], logit[:, :, :], AX.X, ALU.add).then_inc(softmax, 1)
                    dve.wait_ge(softmax, base + 3)
                    dve.reciprocal(tot[:, :], tot[:, :]).then_inc(softmax, 1)
                    dve.wait_ge(softmax, base + 4)
                    dve.tensor_tensor(gate[u][:, :, :], logit[:, :, :],
                                      tot[:, :].unsqueeze(2).broadcast_to([P, TPG, NE]), ALU.mult
                                      ).then_inc(softmax, 1)

                def low(l, g, e):
                    n = NE * g + e
                    for b in range(KT):
                        dve.wait_ge(h_act[l], KT * n + b + 1)
                        dve.tensor_tensor(act_lo[l][e % 2][:, b, :], act_f[l][:, b, :],
                                          act_hi[l][e % 2][:, b, :].bitcast(F32), ALU.subtract
                                          ).then_inc(h_low[l], 1)

                def sum_biases(g, u):
                    dve.wait_ge(bias_mm, g + 1)
                    dve.tensor_tensor(x3[u][:, :, :], p_y[:, :, :], x3[u][:, :, :], ALU.add
                                      ).then_inc(acc_done, 1)

                def sum_expert(g, u, e):
                    dve.wait_ge(y_mm, NE * g + e + 1)
                    dve.wait_ge(acc_done, ACC * g + 1 + e)
                    for j in range(TPG):
                        ins = dve.scalar_tensor_tensor(x3[u][:, j, :], p_y[:, j, :],
                                                       gate[u][:, j, e:e + 1], x3[u][:, j, :],
                                                       ALU.mult, ALU.add)
                    ins.then_inc(acc_done, 1)

                low_f(0, 0)
                low(0, 0, 0)
                softmax_a(0)
                softmax_b(0, 0)
                low(0, 0, 1)
                low(1, 0, 0)

                def group(g, u, i, more):
                    for e in range(NE):
                        if isinstance(g, int) and g == 0 and e + EARLY < NE:
                            low_weights(e + EARLY)
                        if e < NE - 2:
                            low(0, g, e + 2)
                        elif more:
                            low(0, g + 1, e + 2 - NE)
                        if e == 0:
                            sum_biases(g, u)
                        if e < NE - 1:
                            low(1, g, e + 1)
                        elif more:
                            low(1, g + 1, 0)
                        sum_expert(g, u, e)
                        if more and e == 1:
                            norm(g + 1, 1 - u, i if u == 0 else i + 1)
                        if more and e == 2:
                            low_f(g + 1, 1 - u)
                        if more and e == 3:
                            softmax_a(g + 1)
                            softmax_b(g + 1, 1 - u)

                each_group(dve, group)


def build(nc, a):
    d = {"xn": nc.dram_tensor("xn_rows", (NP, D), F32).ap(),
         "xnT": nc.dram_tensor("xn_turned", (GROUPS + 1, P, KT, G), F32).ap(),
         "pairs": nc.dram_tensor("xn_pairs", (NP, 2 * D), F16).ap(),
         "mid": nc.dram_tensor("mid_rows", (NP, D), F32).ap(),
         "all": nc.dram_tensor("all_rows", (NP, D), F32).ap()}
    with ExitStack() as ctx:
        keep = {}
        m = Names(nc, ctx, "keep")
        keep["ident"] = m.sb("ident", [P, P], F32)
        with ExitStack() as sums:
            s = Names(nc, sums, "keep")
            keep["iota"] = s.sb("iota", [P, P], F32)
            keep["base"] = s.sb("base", [P, TILES], F32)
            keep["reach"] = s.sb("reach", [P, SUPER, 2], I32)
            keep["red"] = s.sb("red", [P, TILES, RW], F32)
            with ExitStack() as mix:
                mix_weights(nc, mix, keep)
                norm_phase(nc, a, d, keep)
                mix_phase(nc, a, d, keep)
            gru_phase(nc, a, d, keep)
        experts_phase(nc, a, d, keep)


def kernel(x, src, dst, edge_type_16, **w):
    import numpy as np

    import concourse.bacc as bacc
    from concourse.bass_utils import run_bass_kernel_spmd

    def get(name):
        return np.asarray(w[name])

    def columns(v):
        v = np.asarray(v)
        return v.reshape(-1, P).T

    xp = np.zeros((NP, D), np.float32)
    xp[:N] = np.asarray(x)
    edges = np.zeros((3, EP), np.int32)
    edges[1, :] = N
    for k, v in enumerate((src, dst, edge_type_16)):
        edges[k, :E] = np.asarray(v)
    by_super = np.ascontiguousarray(edges.reshape(3, SUPER, SC, P).transpose(1, 3, 0, 2))
    M, F, R = "L0_mix_", "L0_ffn_", "L0_gnn_"
    b_ih, b_hh = get(R + "b_ih"), get(R + "b_hh")
    arrays = {
        "x": xp,
        "edges_a": by_super[:GROUPS * SA].reshape(GROUPS, SA, P, 3, SC).transpose(0, 2, 1, 3, 4),
        "edges_b": by_super[GROUPS * SA:].reshape(GROUPS, SB, P, 3, SC).transpose(0, 2, 1, 3, 4),
        "dst_by_super": np.ascontiguousarray(by_super[:, :, 1, :].transpose(1, 0, 2)),
        "identity": np.eye(P, dtype=np.float32),
        "iota": np.arange(P, dtype=np.float32),
        "tile_base": np.arange(TILES, dtype=np.float32) * P,
        "w_kv": np.concatenate([get(M + "Wk"), get(M + "Wv")], axis=1),
        "b_kv": np.concatenate([get(M + "bk"), get(M + "bv")]),
        "w_q": get(M + "Wq"), "w_o": get(M + "Wo"), "w_ff1": get(M + "W1"), "w_ff2": get(M + "W2"),
        "mix_rows": np.stack([get(M + n) for n in ("bo", "ln1_b", "b2", "ln2_g", "ln1_g")]),
        "ln2_b": get(M + "ln2_b"),
        "mix_cols": np.concatenate([columns(get(M + n)) for n in ("bq", "ln1_g", "ln1_b", "b1")], axis=1),
        "w_ihT": np.ascontiguousarray(get(R + "w_ih").T),
        "w_hhT": np.ascontiguousarray(get(R + "w_hh").T),
        "rel": get(R + "relvectors"),
        "gru_cols": np.concatenate([columns(b_ih), columns(b_hh[2 * D:])], axis=1),
        "gru_gate_cols": columns(b_hh[:2 * D]),
        "w_router": get(F + "Wr"), "b_router": get(F + "br"), "b_out": get(F + "bo"),
        "w_experts": np.stack([get(F + n).reshape(NE, KT, P, D).transpose(0, 2, 1, 3)
                               for n in ("W1", "W2", "Wo")]),
        "bn_cols": np.stack([np.stack([columns(get(F + n + l)) for l in "12"], axis=1)
                             for n in ("b", "g", "be", "m", "v")], axis=1),
    }
    arrays = {k: np.ascontiguousarray(v) for k, v in arrays.items()}
    nc = bacc.Bacc("TRN2", target_bir_lowering=False, num_devices=1)
    aps = {k: nc.dram_tensor(f"in_{k}", v.shape, mybir.dt.from_np(v.dtype), kind="ExternalInput").ap()
           for k, v in arrays.items()}
    aps["out"] = nc.dram_tensor("out", (NP, D), F32, kind="ExternalOutput").ap()
    build(nc, aps)
    res = run_bass_kernel_spmd(nc, [{f"in_{k}": v for k, v in arrays.items()}], core_ids=[0])
    return res.results[0]["out"][:N]
```
